# Optimizing a Trainium2 kernel written in Bass

```python
import numpy as np
import jax
import jax.numpy as jnp

def _softmax(x, axis=-1):
    return jax.nn.softmax(x, axis=axis)

def _gelu(x):
    return jax.nn.gelu(x, approximate=True)

def _silu(x):
    return jax.nn.silu(x)

def _sigmoid(x):
    return jax.nn.sigmoid(x)

def _layernorm(x, axis=-1, eps=1e-05):
    m = jnp.mean(x, axis=axis, keepdims=True)
    v = jnp.var(x, axis=axis, keepdims=True)
    return (x - m) / jnp.sqrt(v + eps)

def _scatter_add(tgt, idx, src, axis=0):
    return tgt.at[idx].add(src)

def _segment_sum(src, seg, n):
    return jax.ops.segment_sum(src, seg, n)
kernel_name = 'mk_xattn_ffn_d2_seqx_r8_ee56ca'

def setup_inputs(seed: int=0):
    np.random.seed(seed)
    _w = jnp.asarray

    def _rec_inputs():
        import jax
        import jax.numpy as jnp
        _rk = jax.random.key(seed)
        x = 7.22e-05 + 1 * jax.random.normal(jax.random.fold_in(_rk, 1), (16, 128, 128), jnp.float32)
        _lenS = 128 - jax.random.randint(jax.random.fold_in(_rk, 7), (16,), 0, max(1, 128 // 4) + 1, jnp.int32)
        _lenS2 = 128 - jax.random.randint(jax.random.fold_in(_rk, 8), (16,), 0, max(1, 128 // 4) + 1, jnp.int32)
        _ctx_1024P = jax.random.normal(jax.random.fold_in(_rk, 11), (16, 16, 128), jnp.float32)
        _ctx_1024c = jax.random.dirichlet(jax.random.fold_in(_rk, 511), 0.3 * jnp.ones((16,), jnp.float32), (16, 128))
        _ctx_1024t = jnp.einsum('bsk,bkd->bsd', _ctx_1024c, _ctx_1024P)
        _ctx_1024t = _ctx_1024t * jax.lax.rsqrt(jnp.mean(jnp.square(_ctx_1024t)) + 1e-12) * 0.953939
        ctx_1024 = 4.13588e-05 + 0.999923 * (_ctx_1024t + 0.3 * jax.random.normal(jax.random.fold_in(_rk, 611), (16, 128, 128), jnp.float32))
        return (x, ctx_1024, _lenS2)
    x, ctx_1024, _lenS2 = _rec_inputs()

    def _L0_xattn_setup():
        import jax, jax.numpy as jnp
        import numpy as np
        from jax import lax
        NUM_HEADS = 16
        DIM = 128
        BATCH = 4
        SEQ = 256
        key = jax.random.key(seed)
        ks = jax.random.split(key, 12)
        f32 = jnp.float32
        q = jax.random.normal(ks[0], (BATCH, SEQ, DIM), dtype=f32)
        k = jax.random.normal(ks[1], (BATCH, SEQ, DIM), dtype=f32)
        v = jax.random.normal(ks[2], (BATCH, SEQ, DIM), dtype=f32)
        lim = 1.0 / np.sqrt(DIM)
        Wi = jax.random.uniform(ks[3], (DIM, DIM), minval=-lim, maxval=lim, dtype=f32)
        bi = jax.random.uniform(ks[4], (DIM,), minval=-lim, maxval=lim, dtype=f32)
        Wg = jax.random.uniform(ks[5], (DIM, DIM), minval=-lim, maxval=lim, dtype=f32)
        bg = jax.random.uniform(ks[6], (DIM,), minval=-lim, maxval=lim, dtype=f32)
        Wo = jax.random.uniform(ks[7], (DIM, DIM), minval=-lim, maxval=lim, dtype=f32)
        bo = jax.random.uniform(ks[8], (DIM,), minval=-lim, maxval=lim, dtype=f32)
        A = jax.random.normal(ks[9], (DIM, DIM), dtype=f32) * 0.1
        Bm = jax.random.normal(ks[10], (DIM, DIM), dtype=f32) * 0.1
        decay = jnp.full((1, NUM_HEADS, 1), 0.9, dtype=f32)
        return dict(q=q, k=k, v=v, Wi=Wi, bi=bi, Wg=Wg, bg=bg, A=A, Bm=Bm, Wo=Wo, bo=bo, decay=decay)
    _L0_xattn_all = _L0_xattn_setup()
    _L0_xattn_in = {k: v for k, v in _L0_xattn_all.items() if k in ('Wi', 'bi', 'Wg', 'bg', 'A', 'Bm', 'Wo', 'bo', 'decay')}
    del _L0_xattn_all

    def _L0_ffn_setup():
        import jax, jax.numpy as jnp
        import numpy as np
        from jax import lax
        D_MODEL = 128
        D_FF = 512
        NUM_EXPERTS = 24
        TOP_K = 2
        key = jax.random.key(seed)
        ks = jax.random.split(key, 7)
        s1 = 1.0 / np.sqrt(D_MODEL)
        s2 = 1.0 / np.sqrt(D_FF)
        x = jax.random.normal(ks[0], (2, 128, D_MODEL), dtype=jnp.float32)
        gate_w = jax.random.uniform(ks[1], (D_MODEL, NUM_EXPERTS), jnp.float32, -s1, s1)
        gate_b = jax.random.uniform(ks[2], (NUM_EXPERTS,), jnp.float32, -s1, s1)
        w1 = jax.random.uniform(ks[3], (NUM_EXPERTS, D_MODEL, D_FF), jnp.float32, -s1, s1)
        b1 = jax.random.uniform(ks[4], (NUM_EXPERTS, D_FF), jnp.float32, -s1, s1)
        w2 = jax.random.uniform(ks[5], (NUM_EXPERTS, D_FF, D_MODEL), jnp.float32, -s2, s2)
        b2 = jax.random.uniform(ks[6], (NUM_EXPERTS, D_MODEL), jnp.float32, -s2, s2)
        return {'x': x, 'gate_w': gate_w, 'gate_b': gate_b, 'w1': w1, 'b1': b1, 'w2': w2, 'b2': b2}
    _L0_ffn_all = _L0_ffn_setup()
    _L0_ffn_in = {k: v for k, v in _L0_ffn_all.items() if k in ('gate_w', 'gate_b', 'w1', 'b1', 'w2', 'b2')}
    del _L0_ffn_all

    def _L1_xattn_setup():
        import jax, jax.numpy as jnp
        import numpy as np
        B, T, S, H = (32, 64, 128, 128)
        key = jax.random.key(seed)
        k1, k2, k3, k4, k5, k6 = jax.random.split(key, 6)
        query = jax.random.normal(k1, (B, T, H), dtype=jnp.float32)
        encoder_outputs = jax.random.normal(k2, (B, S, H), dtype=jnp.float32)
        src_lengths = jax.random.randint(k3, (B,), S // 2, S + 1, dtype=jnp.int32)
        src_lengths = src_lengths.at[0].set(S).astype(jnp.int64)
        scale = 1.0 / np.sqrt(H)
        W_in = jax.random.normal(k4, (H, H), dtype=jnp.float32) * scale
        W_out = jax.random.normal(k5, (H, 2 * H), dtype=jnp.float32) * scale
        b_out = jax.random.normal(k6, (H,), dtype=jnp.float32) * scale
        return {'query': query, 'encoder_outputs': encoder_outputs, 'src_lengths': src_lengths, 'W_in': W_in, 'W_out': W_out, 'b_out': b_out}
    _L1_xattn_all = _L1_xattn_setup()
    _L1_xattn_in = {k: v for k, v in _L1_xattn_all.items() if k in ('W_in', 'W_out', 'b_out')}
    del _L1_xattn_all

    def _L1_ffn_setup():
        import jax, jax.numpy as jnp
        import numpy as np
        D = 128
        H = 16
        HD = D // H
        L = 64
        E = 8
        B, T = (4, 256)
        EPS = 1e-06

        def _glorot(k, shape):
            fan_in, fan_out = (shape[-2], shape[-1])
            lim = np.sqrt(6.0 / (fan_in + fan_out)).astype(np.float32)
            return jax.random.uniform(k, shape, jnp.float32, -lim, lim)

        def _rmsnorm(x, gamma):
            return gamma * x * jax.lax.rsqrt(jnp.mean(x * x, axis=-1, keepdims=True) + EPS)
        key = jax.random.key(seed)
        ks = jax.random.split(key, 8)
        return {'x': jax.random.normal(ks[0], (B, T, D), jnp.float32), 'gamma1': jnp.ones((D,), jnp.float32), 'Wq': _glorot(ks[1], (D, D)), 'bq': jnp.zeros((D,), jnp.float32), 'Wdown': _glorot(ks[2], (D, L)), 'bdown': jnp.zeros((L,), jnp.float32), 'Wup': _glorot(ks[3], (L, 2 * D)), 'bup': jnp.zeros((2 * D,), jnp.float32), 'Wo': _glorot(ks[4], (D, D)), 'bo': jnp.zeros((D,), jnp.float32), 'gamma2': jnp.ones((D,), jnp.float32), 'Wg': _glorot(ks[5], (D, E)), 'bg': jnp.zeros((E,), jnp.float32), 'We': _glorot(ks[6], (E, D, D))}
    _L1_ffn_all = _L1_ffn_setup()
    _L1_ffn_in = {k: v for k, v in _L1_ffn_all.items() if k in ('gamma1', 'Wq', 'bq', 'Wdown', 'bdown', 'Wup', 'bup', 'Wo', 'bo', 'gamma2', 'Wg', 'bg', 'We')}
    del _L1_ffn_all
    return {'x': x, 'ctx_1024': ctx_1024, '_lenS2': _lenS2, 'L0_xattn_Wi': _L0_xattn_in['Wi'], 'L0_xattn_bi': _L0_xattn_in['bi'], 'L0_xattn_Wg': _L0_xattn_in['Wg'], 'L0_xattn_bg': _L0_xattn_in['bg'], 'L0_xattn_A': _L0_xattn_in['A'], 'L0_xattn_Bm': _L0_xattn_in['Bm'], 'L0_xattn_Wo': _L0_xattn_in['Wo'], 'L0_xattn_bo': _L0_xattn_in['bo'], 'L0_xattn_decay': _L0_xattn_in['decay'], 'L0_ffn_gate_w': _L0_ffn_in['gate_w'], 'L0_ffn_gate_b': _L0_ffn_in['gate_b'], 'L0_ffn_w1': _L0_ffn_in['w1'], 'L0_ffn_b1': _L0_ffn_in['b1'], 'L0_ffn_w2': _L0_ffn_in['w2'], 'L0_ffn_b2': _L0_ffn_in['b2'], 'L1_xattn_W_in': _L1_xattn_in['W_in'], 'L1_xattn_W_out': _L1_xattn_in['W_out'], 'L1_xattn_b_out': _L1_xattn_in['b_out'], 'L1_ffn_gamma1': _L1_ffn_in['gamma1'], 'L1_ffn_Wq': _L1_ffn_in['Wq'], 'L1_ffn_bq': _L1_ffn_in['bq'], 'L1_ffn_Wdown': _L1_ffn_in['Wdown'], 'L1_ffn_bdown': _L1_ffn_in['bdown'], 'L1_ffn_Wup': _L1_ffn_in['Wup'], 'L1_ffn_bup': _L1_ffn_in['bup'], 'L1_ffn_Wo': _L1_ffn_in['Wo'], 'L1_ffn_bo': _L1_ffn_in['bo'], 'L1_ffn_gamma2': _L1_ffn_in['gamma2'], 'L1_ffn_Wg': _L1_ffn_in['Wg'], 'L1_ffn_bg': _L1_ffn_in['bg'], 'L1_ffn_We': _L1_ffn_in['We']}

def reference(x, ctx_1024, _lenS2, L0_xattn_Wi, L0_xattn_bi, L0_xattn_Wg, L0_xattn_bg, L0_xattn_A, L0_xattn_Bm, L0_xattn_Wo, L0_xattn_bo, L0_xattn_decay, L0_ffn_gate_w, L0_ffn_gate_b, L0_ffn_w1, L0_ffn_b1, L0_ffn_w2, L0_ffn_b2, L1_xattn_W_in, L1_xattn_W_out, L1_xattn_b_out, L1_ffn_gamma1, L1_ffn_Wq, L1_ffn_bq, L1_ffn_Wdown, L1_ffn_bdown, L1_ffn_Wup, L1_ffn_bup, L1_ffn_Wo, L1_ffn_bo, L1_ffn_gamma2, L1_ffn_Wg, L1_ffn_bg, L1_ffn_We):
    import jax
    import jax.numpy as jnp

    def _L0_xattn_ref(q, k, v, Wi, bi, Wg, bg, A, Bm, Wo, bo, decay):
        import jax, jax.numpy as jnp
        import numpy as np
        from jax import lax
        NUM_HEADS = 16
        DIM = 128
        BATCH = 4
        SEQ = 256
        B, S, D = q.shape
        H = decay.shape[1]
        hd = D // H
        qh = jnp.moveaxis(q.reshape(B, S, H, hd), 1, 0)
        kh = jnp.moveaxis(k.reshape(B, S, H, hd), 1, 0)
        vh = jnp.moveaxis(v.reshape(B, S, H, hd), 1, 0)

        def step(carry, xs):
            r, state = carry
            qt, kt, vt = xs
            r = decay * r + kt * vt
            retained = (qt * r).reshape(B, D)
            inp = retained @ Wi.T + bi
            gate = jax.nn.sigmoid(inp @ Wg.T + bg)
            blended = gate * state + (1.0 - gate) * inp
            state = jnp.tanh(blended @ A.T + inp @ Bm.T)
            out = state @ Wo.T + bo
            return ((r, state), out)
        r0 = jnp.zeros((B, H, hd), dtype=q.dtype)
        s0 = jnp.zeros((B, D), dtype=q.dtype)
        _, outs = lax.scan(step, (r0, s0), (qh, kh, vh))
        return jnp.moveaxis(outs, 0, 1)

    def _L0_ffn_ref(x, gate_w, gate_b, w1, b1, w2, b2):
        import jax, jax.numpy as jnp
        import numpy as np
        from jax import lax
        D_MODEL = 128
        D_FF = 512
        NUM_EXPERTS = 24
        TOP_K = 2
        gate_scores = jnp.einsum('bsd,de->bse', x, gate_w) + gate_b
        topk_val, topk_idx = lax.top_k(gate_scores, TOP_K)
        sparse_gates = jax.nn.softmax(topk_val, axis=-1)
        combine = jnp.sum(jax.nn.one_hot(topk_idx, NUM_EXPERTS, dtype=x.dtype) * sparse_gates[..., None], axis=-2)
        h = jax.nn.gelu(jnp.einsum('bsd,edf->besf', x, w1) + b1[None, :, None, :], approximate=False)
        y = jnp.einsum('besf,efd->besd', h, w2) + b2[None, :, None, :]
        out = jnp.einsum('bse,besd->bsd', combine, y)
        return out + x

    def _L1_xattn_ref(query, encoder_outputs, src_lengths, W_in, W_out, b_out):
        import jax, jax.numpy as jnp
        import numpy as np
        B, T, S, H = (32, 64, 128, 128)
        pad = jnp.arange(S)[None, :] >= src_lengths[:, None]
        qw = jnp.einsum('bth,oh->bto', query, W_in)
        score = jnp.einsum('bto,bso->bts', qw, encoder_outputs)
        score = jnp.where(pad[:, None, :], -jnp.inf, score)
        p = jax.nn.softmax(score, axis=2)
        c = jnp.einsum('bts,bsh->bth', p, encoder_outputs)
        concat = jnp.concatenate([query, c], axis=2)
        out = jnp.tanh(jnp.einsum('btk,ok->bto', concat, W_out) + b_out)
        return out

    def _L1_ffn_ref(x, gamma1, Wq, bq, Wdown, bdown, Wup, bup, Wo, bo, gamma2, Wg, bg, We):
        import jax, jax.numpy as jnp
        import numpy as np
        D = 128
        H = 16
        HD = D // H
        L = 64
        E = 8
        B, T = (4, 256)
        EPS = 1e-06

        def _glorot(k, shape):
            fan_in, fan_out = (shape[-2], shape[-1])
            lim = np.sqrt(6.0 / (fan_in + fan_out)).astype(np.float32)
            return jax.random.uniform(k, shape, jnp.float32, -lim, lim)

        def _rmsnorm(x, gamma):
            return gamma * x * jax.lax.rsqrt(jnp.mean(x * x, axis=-1, keepdims=True) + EPS)
        b, t = (x.shape[0], x.shape[1])
        h = _rmsnorm(x, gamma1)
        q = (h @ Wq + bq).reshape(b, t, H, HD)
        kv = ((h @ Wdown + bdown) @ Wup + bup).reshape(b, t, H, 2 * HD)
        k, v = jnp.split(kv, 2, axis=-1)
        att = jnp.einsum('bthd,btgd->bthg', q, k) / np.sqrt(HD).astype(np.float32)
        att = jax.nn.softmax(att, axis=-1)
        out = jnp.einsum('bthg,btgd->bthd', att, v).reshape(b, t, D)
        x = x + (out @ Wo + bo)
        h2 = _rmsnorm(x, gamma2)
        gate = jax.nn.softmax(h2 @ Wg + bg, axis=-1)
        combined = jnp.einsum('btd,edf,bte->btf', h2, We, gate)
        return x + combined
    x = x + _L0_xattn_ref(_layernorm(x, axis=-1), ctx_1024, ctx_1024, L0_xattn_Wi, L0_xattn_bi, L0_xattn_Wg, L0_xattn_bg, L0_xattn_A, L0_xattn_Bm, L0_xattn_Wo, L0_xattn_bo, L0_xattn_decay)
    x = x + _L0_ffn_ref(_layernorm(x, axis=-1), L0_ffn_gate_w, L0_ffn_gate_b, L0_ffn_w1, L0_ffn_b1, L0_ffn_w2, L0_ffn_b2)
    x = x + _L1_xattn_ref(_layernorm(x, axis=-1), ctx_1024, _lenS2, L1_xattn_W_in, L1_xattn_W_out, L1_xattn_b_out)
    x = x + _L1_ffn_ref(_layernorm(x, axis=-1), L1_ffn_gamma1, L1_ffn_Wq, L1_ffn_bq, L1_ffn_Wdown, L1_ffn_bdown, L1_ffn_Wup, L1_ffn_bup, L1_ffn_Wo, L1_ffn_bo, L1_ffn_gamma2, L1_ffn_Wg, L1_ffn_bg, L1_ffn_We)
    return x

_drawn_inputs = setup_inputs


def setup_inputs(seed=0):
    import zlib

    import numpy as np

    out = dict(_drawn_inputs(seed))
    spreads = {'L0_xattn_decay': (0.8999999761581421, 0.2),
     'L1_ffn_gamma1': (1.0, 0.536),
     'L1_ffn_bq': (0.0, 0.8),
     'L1_ffn_bdown': (0.0, 0.8),
     'L1_ffn_bup': (0.0, 0.554),
     'L1_ffn_bo': (0.0, 0.1),
     'L1_ffn_gamma2': (1.0, 0.2),
     'L1_ffn_bg': (0.0, 0.674)}
    factors = {'L0_xattn_bi': 8.0, 'L0_xattn_bg': 8.0, 'L0_ffn_b1': 7.756, 'L0_ffn_b2': 5.58}
    for name, (base, spread) in spreads.items():
        noise = np.random.default_rng([zlib.crc32(name.encode()), seed]).standard_normal(out[name].shape)
        drawn = base * np.exp(spread * noise) if base else spread * noise
        out[name] = jnp.asarray(drawn.astype(out[name].dtype))
    for name, factor in factors.items():
        out[name] = (out[name] * factor).astype(out[name].dtype)
    return out
```

```python
from contextlib import ExitStack

import concourse.bass as bass
from concourse import mybir

ALU = mybir.AluOpType
ACT = mybir.ActivationFunctionType
F32 = mybir.dt.float32
BF16 = mybir.dt.bfloat16
U32 = mybir.dt.uint32
I32 = mybir.dt.int32
AX = mybir.AxisListType.X

P = 128
B, T, D = 16, 128, 128
TOK = B * T
NE, F = 24, 512
NT = (2 * TOK + NE * (P - 1)) // P
H, HD = 16, 8
NX = 8
EPS, RMS_EPS = 1e-5, 1e-6
G4 = 4
NG = B // G4
STEPS = 32
NCH = T // STEPS
BIG = -1e30

W_NAMES = ("WiT", "WgT", "AT", "BmT", "Wo0T", "Win", "Wo1T", "Wo2T", "Wq", "Wo")
COLS = ("decay", "bi", "bg", "bo0", "gamma1", "gamma2")
R_B1, R_B2 = 0, NE * F
R_BOUT = R_B2 + NE * D
R_BO = R_BOUT + D
R_GB = R_BO + D
R_BG = R_GB + NE
NROW = R_BG + NX
RP = 96
RC = NROW // RP
assert RP * RC == NROW


def build(nc, a, out, debug=None):
    with ExitStack() as ctx:
        def sb(name, shape, dt=F32):
            return ctx.enter_context(nc.sbuf_tensor(name, shape, dt))

        def sem(name):
            return ctx.enter_context(nc.semaphore(name))

        bank = [ctx.enter_context(nc.psum_tensor(f"bank{i}", [P, 512], F32)) for i in range(8)]

        slots_in = nc.dram_tensor("slots_in", (NT * P, D), F32, kind="Internal").ap()
        slots_out = nc.dram_tensor("slots_out", (NT * P, D), F32, kind="Internal").ap()
        rows_dram = nc.dram_tensor("rows_dram", (3, NROW), BF16, kind="Internal").ap()

        bq_dram = nc.dram_tensor("bq_dram", (3, 3 * D), BF16, kind="Internal").ap()

        w1 = sb("w1", [P, NE * F])
        w2 = sb("w2", [P, NE * 4 * D])
        rows_all = sb("rows_all", [P, NROW // 2])
        rows = rows_all[0:3, :].bitcast(BF16)
        wkv = rows_all[64:128, 0:3 * D]
        bd = rows_all[64:128, 3 * D:3 * D + 1]
        ctxT = sb("ctxT", [P, TOK])
        x = sb("x", [P, B, D])
        xn = sb("xn", [P, B, D])
        xr = sb("xr", [P, B, D])
        pool_a = sb("pool_a", [P, 2 * TOK])
        sT = pool_a[:, 0:TOK].rearrange("p (b t) -> p b t", t=T)
        gate = pool_a[:, TOK:2 * TOK]
        yg = pool_a[:].rearrange("p (b k d) -> p b k d", k=2, d=D)

        def router(at, n=NE * B):
            return pool_a[:, at:at + n]

        wpk = sb("wpk", [P, len(W_NAMES) * P])
        cols = sb("cols", [P, len(COLS)])
        gatew = sb("gatew", [P, NE])
        ident = sb("ident", [P, P])
        inp = sb("inp", [P, 2, 512])
        ginp = sb("ginp", [P, 2, 512])
        dec = sb("dec", [P, 512])
        rbuf = sb("rbuf", [P, 2, 512])
        hbg = sb("hbg", [P, 1])
        gs = sb("gs", [P, 2, B])
        mhalf = sb("mhalf", [P, B])
        st = sb("st", [P, B, 6])
        mv = sb("mv", [P, B, 2])
        veps = sb("veps", [P, B])
        rstd = sb("rstd", [P, B])
        rowf = pool_a[0:RP, 0:3 * RC].rearrange("p (k c) -> p k c", k=3)
        rowb = pool_a[0:RP, 512:512 + 3 * RC].bitcast(BF16)[:, 0:3 * RC].rearrange("p (k c) -> p k c", k=3)
        ones3 = sb("ones3", [3, P], BF16)
        onesb = sb("onesb", [P, P], BF16)
        lower = sb("lower", [P, P], BF16)
        zeros = sb("zeros", [P, 512])
        oT, xnT = inp, ginp
        xr2 = xr[:].rearrange("p b d -> p (b d)")
        sc = xr2[:, 0:384].rearrange("p (b e) -> p b e", e=NE)
        m8 = xr2[:, 384:512].rearrange("p (b e) -> p b e", e=8)
        i8 = xr2[:, 512:640].bitcast(U32).rearrange("p (b e) -> p b e", e=8)
        i8f = sb("i8f", [P, 2, B])
        iota_e = sb("iota_e", [P, NE])
        iota_s = sb("iota_s", [P, P])
        slot128 = sb("slot128", [1, NT])
        ei = lambda at: router(at).rearrange("p (e i) -> p e i", i=B)
        pick = [ei(TOK + k * NE * B) for k in range(2)]
        picks = sb("picks", [P, NE, B], BF16)
        cnt, incl, pos = (ei(TOK + k * NE * B) for k in (2, 3, 4))
        scanm = xr2[:, 640:1024].rearrange("p (e i) -> p e i", i=B)
        ppos = router(0).rearrange("p (i e) -> p i e", e=NE)
        slotf = sb("slotf", [P, 2, B])
        sloti = sb("sloti", [P, 2, B], I32)
        npad_i = sb("npad_i", [P, NE], I32)
        npad = sb("npad", [P, NE])
        end_e = sb("end_e", [P, NE])
        base_e = sb("base_e", [P, NE])
        ones24 = sb("ones24", [P, NE])
        over = pool_a[0:1, NE * B:NE * B + NT * NE].rearrange("p (j e) -> p j e", e=NE)
        tab_f = sb("tab_f", [1, NT])
        tab = sb("tab", [1, NT], I32)
        mix = sb("mix", [P, 2, B])
        mixe = sb("mixe", [P, B])
        mixs = sb("mixs", [P, B])
        hS, hT = inp, ginp
        rb = rbuf[:].rearrange("p a b -> p (a b)")
        xin = rb[:, 0:512].rearrange("p (u d) -> p u d", u=4)
        xsT = rb[:, 512:768].rearrange("p (u d) -> p u d", u=2)
        yS = rb[:, 768:1024].rearrange("p (u d) -> p u d", u=2)

        bqkv = xr2[0:1, 1024:1024 + 6 * D]
        bqkv3 = rb[0:1, 0:5 * D].bitcast(BF16)[:, 0:9 * D].rearrange("p (k c) -> p k c", k=3)
        rowsq = sb("rowsq", [3, 3 * D], BF16)
        wqkv = sb("wqkv", [P, 3 * D])
        we = sb("we", [P, NX * D + NX])
        lens_i = sb("lens_i", [P, B], I32)
        settled = sb("settled", [P, 1])
        rmse = sb("rmse", [P, 1])
        lens = sb("lens", [P, B])
        prod = w1[:, 0:4 * 2048].rearrange("p (k u n) -> p k u n", k=2, u=2)
        spare = [0]

        def room(n, u=2):
            at = spare[0]
            spare[0] += n * u
            return w2[:, at:at + n * u].rearrange("p (u n) -> p u n", u=u)

        xn3, xn3T, msk, scs, pr, pT, t3, hrow, hTd = (room(D) for _ in range(9))
        qkv, ST, pe_, pn = room(3 * D), room(2 * D), room(2 * D), room(2 * D)
        OT, h2, h2T, acc, junk = (room(D) for _ in range(5))
        mx16, sum16, rec16 = room(H), room(H), room(H)
        ST2 = room(2 * D)
        g8x = room(1)
        g8, ge8, gn8 = room(NX), room(NX), room(NX)
        st3, st4 = room(6), room(6)
        mv3, mv4 = room(2), room(2)
        (ve3, r3, mx1, sm1, rc1, ve4, r4, q4, ve5, r5, r45, ssq, ve6, r6, gmx, gsm, grc) = (room(1) for _ in range(17))

        def W(name):
            k = W_NAMES.index(name)
            return wpk[:, k * P:(k + 1) * P]

        def col(name):
            k = COLS.index(name)
            return cols[:, k:k + 1]

        ld_x = [sem(f"ld_x{g}") for g in range(NG)]
        ld_ctx, ld_w, ld_moe, ld_rowf, ld_rows = map(sem, ("ld_ctx", "ld_w", "ld_moe", "ld_rowf", "ld_rows"))
        st_rows, st_zero = map(sem, ("st_rows", "st_zero"))
        k_id0, k_id, k_iota, k_low0, k_low, k_half = map(sem, ("k_id0", "k_id", "k_iota", "k_low0", "k_low", "k_half"))
        k_dve = sem("k_dve")
        ln1_var, ln1_rstd, ln1_x, ln1_t = map(sem, ("ln1_var", "ln1_rstd", "ln1_x", "ln1_t"))
        ctx2, rscan, retd = map(sem, ("ctx2", "rscan", "retd"))
        p_inp, s_inp, p_gate, s_gate, s_ginp, p_u = map(sem, ("p_inp", "s_inp", "p_gate", "s_gate", "s_ginp", "p_u"))
        gs_ok, u_ok, state_ok = map(sem, ("gs_ok", "u_ok", "state_ok"))
        dchain = sem("dchain")
        p_o, s_o, p_oT, x1_ok = map(sem, ("p_o", "s_o", "p_oT", "x1_ok"))
        ln2_var, ln2_rstd, ln2_x, p_xT, s_xT, p_sc, sc_ok = map(
            sem, ("ln2_var", "ln2_rstd", "ln2_x", "p_xT", "s_xT", "p_sc", "sc_ok"))
        picks_ok, p_cnt, slot_ok, tab_ok, mix_d, mix_e = map(
            sem, ("picks_ok", "p_cnt", "slot_ok", "tab_ok", "mix_d", "mix_e"))
        res_ok = sem("res_ok")
        scattered = sem("scattered")
        ld_in = [sem(f"ld_in{u}") for u in range(4)]
        p_in, s_in, p_h, s_h, p_hT, s_hT, p_y, s_y = map(
            sem, ("p_in", "s_in", "p_h", "s_h", "p_hT", "s_hT", "p_y", "s_y"))
        st_y = [sem(f"st_y{u}") for u in range(2)]
        gathered = [sem(f"gathered{g}") for g in range(NG)]
        x2_ok, st_out = sem("x2_ok"), sem("st_out")
        ld_bqf = sem("ld_bqf")
        ld_d, bq_sum, bq3, st_bq, ld_bq = map(sem, ("ld_d", "bq_sum", "bq3", "st_bq", "ld_bq"))
        p_v, s_v, p_kw, s_kw, p_wkv, s_wkv, lens_ok = map(sem, ("p_v", "s_v", "p_kw", "s_kw", "p_wkv", "s_wkv", "lens_ok"))
        (d_var3, d_r3, d_xn3, d_xn3T, d_cxn3, d_score, d_masked, d_exp, d_p, d_pT, d_cpT, d_o, d_tanh, d_x3, d_var4,
         d_r45, d_xf, d_h, d_hT, d_chT, d_qkv, d_cqkv, d_qk, d_S, d_cS, d_S2, d_sub, d_exp2, d_pn, d_pv, d_O, d_cO,
         d_w, d_xf2, d_ssq, d_r6, d_acc, d_h2, d_h2T, d_ch2T, d_lg, d_gmax, d_gexp, d_gn, d_we, d_out) = (
            sem("d_" + n) for n in (
                "var3 r3 xn3 xn3T cxn3 score masked exp p pT cpT o tanh x3 var4 r45 xf h hT chT qkv cqkv qk S cS S2 "
                "sub exp2 pn pv O cO w xf2 ssq r6 acc h2 h2T ch2T lg gmax gexp gn we out").split())
        st_d = [sem(f"st_d{u}") for u in range(2)]
        l_dve, l_pool, d_sq = map(sem, ("l_dve", "l_pool", "d_sq"))

        block = ctx.enter_context(nc.Block())

        def ge(eng, semaphore, count):
            if not isinstance(count, int) or count > 0:
                eng.wait_ge(semaphore, count)

        def lag_next(i, t, lag, other):
            return min(t + (lag - other + 1), B) if isinstance(t, int) else t + (lag - other + 1)

        LAST = 4

        class Links:

            def __init__(self, eng, semaphore):
                self.eng, self.semaphore, self.n, self.each, self.trip = eng, semaphore, 0, 0, None

            def __call__(self, ins):
                self.n += 1
                ins.then_inc(self.semaphore, 1)
                self.eng.wait_ge(self.semaphore, self.n if self.trip is None else self.trip + self.n)

        def run_tiles(eng, step, links=None):
            for i in range(6):
                before = links.n if links else 0
                step(i, i % 2)
            each = links.n - before if links else 0
            with eng.Fori(3, B // 2) as n:
                if links:
                    links.trip = n * (2 * each)
                    links.n -= 6 * each
                for u in range(2):
                    step(n * 2 + u, u)
                if links:
                    links.trip = None
                    links.n += (B - 2) * each
            for i in range(B, B + LAST):
                step(i, i % 2)

        def lagged(i, u, lag):
            if isinstance(i, int):
                return (i - lag, (i - lag) % 2) if 0 <= i - lag < B else None
            return i - lag, (u - lag) % 2

        def at(tile3, tile):
            return tile3[:, bass.ds(tile, 1), :].rearrange("p a d -> p (a d)")

        def g512(g):
            return slice(g * 512, (g + 1) * 512)

        def seqs(tile3, g):
            return tile3[:, g * G4:(g + 1) * G4, :]

        @block.sync
        def _(sp):
            xv = a["x"].rearrange("b t d -> t b d")
            for g in range(NG):
                sp.dma_start(seqs(x, g), xv[:, g * G4:(g + 1) * G4, :]).then_inc(ld_x[g], 16)
            sp.dma_start(w1[:].rearrange("p (e f) -> p e f", e=NE), a["w1"].rearrange("e p f -> p e f")).then_inc(ld_moe, 16)
            sp.dma_start(w2[:].rearrange("p (e c d) -> p e c d", e=NE, c=4),
                         a["w2"].rearrange("e (c p) d -> p e c d", c=4)).then_inc(ld_moe, 16)
            for t_, n in ((wkv, "wkv"), (bd, "bd"), (we[:], "we")):
                sp.dma_start(t_, a[n]).then_inc(ld_d, 16)
            sp.dma_start(lens_i[:], a["lens"].to_broadcast([P, B])).then_inc(ld_d, 16)
            sp.wait_ge(k_dve, 3)
            zv = slots_in.rearrange("(n p) d -> p n d", p=P)
            for n in range(0, NT, 4):
                m = min(4, NT - n)
                sp.dma_start(zv[:, n:n + m, :], zeros[:, 0:m * D].rearrange("p (n d) -> p n d", n=m)).then_inc(st_zero, 16)
            sp.wait_ge(k_dve, 8)
            sp.dma_start(rows_dram.rearrange("k (p c) -> p k c", p=RP), rowb).then_inc(st_rows, 16)
            sp.wait_ge(st_rows, 16)
            sp.dma_start(rows[:], rows_dram).then_inc(ld_rows, 16)
            sp.wait_ge(p_u, NCH)
            sp.dma_start(bqkv[:, 0:3 * D], a["bqkv"]).then_inc(ld_bqf, 16)
            sp.wait_ge(bq3, 1)
            sp.dma_start(bq_dram.rearrange("k c -> (k c)").unsqueeze(0), bqkv3.rearrange("p k c -> p (k c)")).then_inc(st_bq, 16)
            sp.wait_ge(st_bq, 16)
            sp.dma_start(rowsq[:], bq_dram).then_inc(ld_bq, 16)
            sp.wait_ge(scattered, 16 * 2 * B)
            sl = slots_in.rearrange("(n p) d -> n p d", p=P)
            so = slots_out.rearrange("(n p) d -> n p d", p=P)

            def load(j, u):
                sp.dma_start(xin[:, u, :], sl[bass.ds(j, 1), :, :].rearrange("a p d -> p (a d)")).then_inc(ld_in[u], 16)

            def store(j, u):
                sp.wait_ge(s_y, j + 1)
                sp.dma_start(so[bass.ds(j, 1), :, :].rearrange("a p d -> p (a d)"), yS[:, u, :]).then_inc(st_y[u], 16)

            for j in range(4):
                load(j, j)
            full = (NT - 4) // 4
            with sp.Fori(0, full) as i:
                for u in range(4):
                    sp.wait_ge(p_in, i * 4 + u + 1)
                    load(i * 4 + u + 4, u)
                    store(i * 4 + u, u % 2)
            for j in range(4 * full, NT):
                if j + 4 < NT:
                    sp.wait_ge(p_in, j + 1)
                    load(j + 4, j % 4)
                store(j, j % 2)
            def step(i, u):
                if z := lagged(i, u, 4):
                    t, p = z
                    sp.wait_ge(d_out, t + 1)
                    sp.dma_start(out[bass.ds(t, 1), :, :].rearrange("a t d -> t (a d)"), acc[:, p, :]).then_inc(st_d[p], 16)

            run_tiles(sp, step)
            for u in range(2):
                sp.wait_ge(st_d[u], 16 * B // 2)

        @block.gpsimd
        def _(pool):
            g = nc.gpsimd
            g.memset(ident[:], 0.0).then_inc(k_id0, 1)
            g.memset(lower[:], 1.0).then_inc(k_low0, 1)
            g.memset(mhalf[:], -0.5).then_inc(k_half, 1)
            pool.wait_ge(k_id0, 1)
            g.affine_select(out=ident[:], in_=ident[:], compare_op=ALU.not_equal, fill=1.0, base=0,
                            pattern=[[-1, P]], channel_multiplier=1).then_inc(k_id, 1)
            pool.wait_ge(k_low0, 1)
            g.affine_select(out=lower[:], in_=lower[:], compare_op=ALU.is_gt, fill=0.0, base=0,
                            pattern=[[1, P]], channel_multiplier=-1).then_inc(k_low, 1)
            g.iota(iota_e[:], pattern=[[1, NE]], base=0, channel_multiplier=0,
                   allow_small_or_imprecise_dtypes=True).then_inc(k_iota, 1)
            g.iota(iota_s[:], pattern=[[1, P]], base=0, channel_multiplier=0,
                   allow_small_or_imprecise_dtypes=True).then_inc(k_iota, 1)
            g.iota(slot128[:], pattern=[[P, NT]], base=0, channel_multiplier=0,
                   allow_small_or_imprecise_dtypes=True).then_inc(k_iota, 1)
            pool.wait_ge(k_half, 1)
            for ready, done in ((ln1_var, ln1_rstd), (ln2_var, ln2_rstd)):
                for k in range(NG):
                    c = slice(k * G4, (k + 1) * G4)
                    pool.wait_ge(ready, k + 1)
                    g.tensor_tensor(rstd[:, c], veps[:, c], mhalf[:, c], ALU.pow).then_inc(done, 1)
            pool.wait_ge(st_zero, 16 * ((NT + 3) // 4))
            pool.wait_ge(slot_ok, 1)
            for i in range(B):
                for k in range(2):
                    pool.indirect_dma_start(slots_in[:, :], bass.IndirectOffsetOnAxis(ap=sloti[:, k, i:i + 1], axis=0),
                                            xn[:, i, :], None).then_inc(scattered, 16)
            pool.wait_ge(st_y[0], 16 * ((NT + 1) // 2))
            pool.wait_ge(st_y[1], 16 * (NT // 2))
            for i in range(B):
                for k in range(2):
                    pool.indirect_dma_start(yg[:, i, k, :], None, slots_out[:, :],
                                            bass.IndirectOffsetOnAxis(ap=sloti[:, k, i:i + 1], axis=0)).then_inc(gathered[i // G4], 16)

            half = mhalf[:, 0:1]
            link = Links(pool, l_pool)

            def step(i, u):
                if z := lagged(i, u, 0):
                    t, p = z
                    pool.wait_ge(d_var3, t + 1)
                    g.tensor_tensor(r3[:, p, :], ve3[:, p, :], half, ALU.pow).then_inc(d_r3, 1)
                if z := lagged(i, u, 1):
                    t, p = z
                    pool.wait_ge(d_var4, t + 1)
                    ge(pool, d_h, t - 1)
                    link(g.tensor_tensor(r4[:, p, :], ve4[:, p, :], half, ALU.pow))
                    link(g.tensor_tensor(q4[:, p, :], mv4[:, p, 1:2], r4[:, p, :], ALU.mult))
                    link(g.tensor_tensor(ve5[:, p, :], q4[:, p, :], r4[:, p, :], ALU.mult))
                    link(g.tensor_tensor(ve5[:, p, :], ve5[:, p, :], rmse[:], ALU.add))
                    link(g.tensor_tensor(r5[:, p, :], ve5[:, p, :], half, ALU.pow))
                    g.tensor_tensor(r45[:, p, :], r4[:, p, :], r5[:, p, :], ALU.mult).then_inc(d_r45, 1)
                if z := lagged(i, u, 3):
                    t, p = z
                    pool.wait_ge(d_xf2, t + 1)
                    ge(pool, st_d[p], (t + -p) * 8)
                    g.tensor_tensor(acc[:, p, :], at(x, t), at(xn, t), ALU.add).then_inc(d_acc, 1)
                    pool.wait_ge(d_ssq, t + 1)
                    g.tensor_tensor(r6[:, p, :], ve6[:, p, :], half, ALU.pow).then_inc(d_r6, 1)

            run_tiles(pool, step, link)

        @block.scalar
        def _(act):
            s = nc.scalar
            act.dma_start(ctxT[:], a["ctxT"]).then_inc(ld_ctx, 16)
            for t, n in ((wpk, "wpk"), (cols, "cols"), (gatew, "gate_w")):
                act.dma_start(t[:], a[n]).then_inc(ld_w, 16)
            act.dma_start(rowf[:, 0, :], a["rowb"]).then_inc(ld_rowf, 16)
            act.wait_ge(ld_ctx, 16)
            for k in range(NG):
                if k >= 2:
                    act.wait_ge(retd, k - 1)
                s.activation(rbuf[:, k % 2, :], ctxT[:, g512(k)], ACT.Square).then_inc(ctx2, 1)
            act.wait_ge(ld_w, 48)
            for c in range(NCH):
                act.wait_ge(p_inp, c + 1)
                if c >= 2:
                    act.wait_ge(p_u, c - 1)
                s.activation(inp[:, c % 2, :], bank[0][:], ACT.Identity, bias=col("bi")).then_inc(s_inp, 1)
                act.wait_ge(p_gate, c + 1)
                s.activation(gate[:, g512(c)], bank[1][:], ACT.Tanh, bias=hbg[:], scale=0.5).then_inc(s_gate, 1)
            act.wait_ge(st_rows, 16)
            for c in range(NCH):
                with act.Fori(0, STEPS // 4) as i:
                    for u in range(4):
                        act.wait_ge(u_ok, i * 4 + (c * STEPS + u + 1))
                        s.activation(sT[:, :, bass.ds(i * 4 + (c * STEPS + u), 1)].rearrange("p b t -> p (b t)"),
                                     bank[4 + c][:, bass.ds(i * (4 * B) + u * B, B)], ACT.Tanh).then_inc(state_ok, 1)
            for k in range(NG):
                act.wait_ge(p_o, k + 1)
                if k >= 2:
                    act.wait_ge(p_oT, k - 1)
                s.activation(oT[:, k % 2, :], bank[k % 2][:], ACT.Identity, bias=col("bo0")).then_inc(s_o, 1)
            for k in range(NG):
                act.wait_ge(p_xT, k + 1)
                if k >= 2:
                    act.wait_ge(p_sc, k - 1)
                s.activation(xnT[:, k % 2, :], bank[4 + k % 2][:], ACT.Copy).then_inc(s_xT, 1)
            act.wait_ge(mix_d, 1)
            s.activation(mixe[:], mixs[:], ACT.Exp).then_inc(mix_e, 1)
            act.wait_ge(slot_ok, 1)
            act.wait_ge(bq3, 1)
            act.wait_ge(ld_d, 64)
            for k in range(NG):
                act.wait_ge(p_v, k + 1)
                s.activation(seqs(xr, k).rearrange("p b d -> p (b d)"), bank[2 + k % 2][:], ACT.Copy).then_inc(s_v, 1)
            for k in range(NG):
                act.wait_ge(p_kw, k + 1)
                s.activation(ctxT[:, g512(k)], bank[4 + k % 2][:], ACT.Copy, scale=-1.0).then_inc(s_kw, 1)
            act.wait_ge(p_wkv, 2)
            s.activation(wqkv[:, D:3 * D], bank[6][:, 0:2 * D], ACT.Copy, scale=col("gamma1")).then_inc(s_wkv, 1)
            s.activation(wqkv[:, 0:D], W("Wq"), ACT.Copy, scale=col("gamma1")).then_inc(s_wkv, 1)
            s.activation(we[:], we[:], ACT.Copy, scale=col("gamma2")).then_inc(s_wkv, 1)
            def gelu(j, u):
                act.wait_ge(p_h, j + 1)
                s.activation(hS[:, u, :], bank[1 + u][:], ACT.Gelu).then_inc(s_h, 1)

            def ycopy(j, u, stored):
                act.wait_ge(p_y, j + 1)
                if stored is not None:
                    act.wait_ge(st_y[u], stored)
                s.activation(yS[:, u, :], bank[5 + u][:, 0:D], ACT.Copy).then_inc(s_y, 1)

            gelu(0, 0)
            gelu(1, 1)
            gelu(2, 0)
            ycopy(0, 0, None)
            gelu(3, 1)
            ycopy(1, 1, None)
            n = (NT - 4) // 2
            with act.Fori(0, n) as i:
                for u in range(2):
                    gelu(i * 2 + (4 + u), u)
                    ycopy(i * 2 + (2 + u), u, i * 16 + 16)
            for j in range(4 + 2 * n, NT):
                gelu(j, j % 2)
                ycopy(j - 2, j % 2, 16 * ((j - 2) // 2))
            for j in (NT - 2, NT - 1):
                ycopy(j, j % 2, 16 * (j // 2))

            def step(i, u):
                a0, a1, a2, a3 = (lagged(i, u, k) for k in range(4))
                if a3:
                    t, p = a3
                    act.wait_ge(d_O, t + 1)
                    ge(act, d_w, t - 1)
                    s.activation(OT[:, p, :], bank[4][:, 256:384], ACT.Copy).then_inc(d_cO, 1)
                if a0:
                    t, p = a0
                    act.wait_ge(d_xn3T, t + 1)
                    ge(act, d_o, t - 1)
                    s.activation(xn3T[:, p, :], bank[0][:, 0:P], ACT.Copy).then_inc(d_cxn3, 1)
                if a1:
                    t, p = a1
                    act.wait_ge(d_hT, t + 1)
                    ge(act, d_qkv, t - 1)
                    s.activation(hTd[:, p, :], bank[2][:, 0:P], ACT.Copy).then_inc(d_chT, 1)
                    act.wait_ge(d_qkv, t + 1)
                    ge(act, d_pv, t - 1)
                    s.activation(qkv[:, p, :], bank[3][:, 0:3 * D], ACT.Copy).then_inc(d_cqkv, 1)
                if a0:
                    t, p = a0
                    act.wait_ge(d_masked, t + 1)
                    s.activation(pr[:, p, :], scs[:, p, :], ACT.Exp, bias=mx1[:, p, :], scale=-1.0,
                                 accum_out=sm1[:, p, :]).then_inc(d_exp, 1)
                if a2:
                    t, p = a2
                    act.wait_ge(d_S, t + 1)
                    ge(act, d_S2, t - 1)
                    s.activation(ST[:, p, :], bank[4][:, 0:256], ACT.Copy).then_inc(d_cS, 1)
                if a3:
                    t, p = a3
                    act.wait_ge(d_xf2, t + 1)
                    s.activation(junk[:, p, :], at(xn, t), ACT.Square, accum_out=ssq[:, p, :]).then_inc(d_sq, 1)
                    act.wait_ge(d_sq, t + 1)
                    s.activation(ve6[:, p, :], ssq[:, p, :], ACT.Identity, bias=rmse[:], scale=1.0 / D).then_inc(d_ssq, 1)
                if a0:
                    t, p = a0
                    act.wait_ge(d_pT, t + 1)
                    ge(act, d_o, t - 1)
                    s.activation(pT[:, p, :], bank[0][:, P:2 * P], ACT.Copy).then_inc(d_cpT, 1)
                if a2:
                    t, p = a2
                    act.wait_ge(d_sub, t + 1)
                    s.activation(pe_[:, p, :], ST2[:, p, :], ACT.Exp, scale=float(HD) ** -0.5).then_inc(d_exp2, 1)
                if a0:
                    t, p = a0
                    act.wait_ge(d_o, t + 1)
                    ge(act, d_x3, t - 1)
                    s.activation(t3[:, p, :], bank[1][:, P:2 * P], ACT.Tanh).then_inc(d_tanh, 1)
                if a3:
                    t, p = a3
                    act.wait_ge(d_h2T, t + 1)
                    ge(act, d_we, t - 1)
                    s.activation(h2T[:, p, :], bank[2][:, P:2 * P], ACT.Copy).then_inc(d_ch2T, 1)
                    act.wait_ge(d_gmax, t + 1)
                    s.activation(ge8[:, p, :], g8[:, p, :], ACT.Exp, bias=gmx[:, p, :],
                                 accum_out=gsm[:, p, :]).then_inc(d_gexp, 1)

            run_tiles(act, step)

        @block.tensor
        def _(pe):
            t = nc.tensor

            def mm(o, l, r, start=True, stop=True):
                return t.matmul(o, l, r, start=start, stop=stop, skip_group_check=True)

            pe.wait_ge(k_id, 1)
            for k in range(NG):
                pe.wait_ge(ln1_x, k + 1)
                if k >= 2:
                    pe.wait_ge(retd, k - 1)
                for b in range(G4):
                    ins = t.transpose(bank[2 + k % 2][:, b * P:(b + 1) * P], xn[:, k * G4 + b, :], ident[:])
                ins.then_inc(ln1_t, 1)
            pe.wait_ge(retd, NG)
            pe.wait_ge(ld_w, 48)
            ret = xr[:].rearrange("p b d -> p (b d)")
            for c in range(NCH):
                if c:
                    pe.wait_ge(s_inp, c)
                mm(bank[0][:], W("WiT"), ret[:, g512(c)]).then_inc(p_inp, 1)
                pe.wait_ge(s_inp, c + 1)
                if c:
                    pe.wait_ge(s_gate, c)
                mm(bank[1][:], W("WgT"), inp[:, c % 2, :]).then_inc(p_gate, 1)
                pe.wait_ge(s_ginp, c + 1)
                mm(bank[4 + c][:], W("AT"), ginp[:, c % 2, :], stop=False)
                mm(bank[4 + c][:], W("BmT"), inp[:, c % 2, :], start=False, stop=False).then_inc(p_u, 1)
            for c in range(NCH):
                with pe.Fori(0, STEPS // 4) as i:
                    for u in range(4):
                        pe.wait_ge(gs_ok, i * 4 + (c * STEPS + u + 1))
                        mm(bank[4 + c][:, bass.ds(i * (4 * B) + u * B, B)], W("AT"), gs[:, u % 2, :],
                           start=False, stop=False).then_inc(u_ok, 1)
            pe.wait_ge(state_ok, T)
            for k in range(NG):
                if k >= 2:
                    pe.wait_ge(s_o, k - 1)
                mm(bank[k % 2][:], W("Wo0T"), seqs(sT, k).rearrange("p b t -> p (b t)")).then_inc(p_o, 1)
                pe.wait_ge(s_o, k + 1)
                if k >= 2:
                    pe.wait_ge(x1_ok, k - 1)
                for b in range(G4):
                    ins = t.transpose(bank[2 + k % 2][:, b * P:(b + 1) * P], oT[:, k % 2, b * P:(b + 1) * P], ident[:])
                ins.then_inc(p_oT, 1)
            pe.wait_ge(ld_rows, 16)
            for k in range(NG):
                pe.wait_ge(ln2_x, k + 1)
                if k >= 2:
                    pe.wait_ge(s_xT, k - 1)
                for b in range(G4):
                    ins = t.transpose(bank[4 + k % 2][:, b * P:(b + 1) * P], xn[:, k * G4 + b, :], ident[:])
                ins.then_inc(p_xT, 1)
                pe.wait_ge(s_xT, k + 1)
                if k >= 2:
                    pe.wait_ge(sc_ok, k - 1)
                for b in range(G4):
                    o = bank[6 + k % 2][:, b * NE:(b + 1) * NE]
                    mm(o, xnT[:, k % 2, b * P:(b + 1) * P], gatew[:], stop=False)
                    ins = mm(o, ones3[:], rows[:, R_GB:R_GB + NE], start=False)
                ins.then_inc(p_sc, 1)
            pe.wait_ge(picks_ok, 1)
            pe.wait_ge(k_low, 1)
            pk = picks[:].rearrange("p e i -> p (e i)")
            mm(bank[0][:, 0:NE * B], onesb[:], pk)
            mm(bank[1][:, 0:NE * B], lower[:], pk).then_inc(p_cnt, 1)
            pe.wait_ge(ld_d, 64)
            pe.wait_ge(sc_ok, NG)
            mm(bank[7][0:1, 0:2 * D], bd, wkv[:, D:3 * D]).then_inc(p_wkv, 1)
            mm(bank[6][:, 0:2 * D], wkv[:, 0:D], wkv[:, D:3 * D]).then_inc(p_wkv, 1)
            for k in range(NG):
                if k >= 2:
                    pe.wait_ge(s_v, k - 1)
                for b in range(G4):
                    ins = mm(bank[2 + k % 2][:, b * P:(b + 1) * P], ctxT[:, (k * G4 + b) * P:(k * G4 + b + 1) * P], W("Wo2T"))
                ins.then_inc(p_v, 1)
            for k in range(NG):
                if k >= 2:
                    pe.wait_ge(s_kw, k - 1)
                mm(bank[4 + k % 2][:], W("Win"), ctxT[:, g512(k)]).then_inc(p_kw, 1)
            pe.wait_ge(s_wkv, 1)
            pe.wait_ge(s_v, NG)
            pe.wait_ge(s_kw, NG)
            pe.wait_ge(tab_ok, 1)
            pe.wait_ge(ld_moe, 32)
            pe.wait_ge(slot_ok, 1)

            def t_in(j, u4, u):
                pe.wait_ge(ld_in[u4], (j + (4 - u4)) * 4)
                if not isinstance(j, int) or j >= 1:
                    pe.wait_ge(s_in, j)
                t.transpose(bank[0][:, 0:P], xin[:, u4, :], ident[:]).then_inc(p_in, 1)

            def hidden(j, u):
                e = pe.value_load(tab[0:1, bass.ds(j, 1)], min_val=0, max_val=NE - 1)
                pe.wait_ge(s_in, j + 1)
                if not isinstance(j, int) or j >= 2:
                    pe.wait_ge(s_h, j - 1)
                mm(bank[1 + u][:], ones3[:], rows[:, bass.ds(e * F + R_B1, F)], stop=False)
                mm(bank[1 + u][:], xsT[:, u, :], w1[:, bass.ds(e * F, F)], start=False).then_inc(p_h, 1)

            def t_hidden(j, u):
                pe.wait_ge(s_h, j + 1)
                if not isinstance(j, int) or j >= 2:
                    pe.wait_ge(s_hT, j - 1)
                for c in range(4):
                    ins = t.transpose(bank[3 + u][:, c * P:(c + 1) * P], hS[:, u, c * P:(c + 1) * P], ident[:])
                ins.then_inc(p_hT, 1)

            def yout(j, u):
                e = pe.value_load(tab[0:1, bass.ds(j, 1)], min_val=0, max_val=NE - 1)
                pe.wait_ge(s_hT, j + 1)
                if not isinstance(j, int) or j >= 2:
                    pe.wait_ge(s_y, j - 1)
                o = bank[5 + u][:, 0:D]
                mm(o, ones3[:], rows[:, bass.ds(e * D + R_B2, D)], stop=False)
                for c in range(4):
                    ins = mm(o, hT[:, u, c * P:(c + 1) * P], w2[:, bass.ds(e * (4 * D) + c * D, D)],
                             start=False, stop=c == 3)
                ins.then_inc(p_y, 1)

            def step(k, u4):
                fixed = isinstance(k, int)
                if not fixed or k + 3 < NT:
                    t_in(k + 3, (u4 + 3) % 4, (u4 + 3) % 2)
                if not fixed or 0 <= k + 2 < NT:
                    hidden(k + 2, u4 % 2)
                if not fixed or 0 <= k + 1 < NT:
                    t_hidden(k + 1, (u4 + 1) % 2)
                if not fixed or k >= 0:
                    yout(k, u4 % 2)

            n = (NT - 3) // 4
            for k in range(-3, 4):
                step(k, k % 4)
            with pe.Fori(1, n) as i:
                for u in range(4):
                    step(i * 4 + u, u)
            for k in range(4 * n, NT):
                step(k, k % 4)

            pe.wait_ge(ld_bq, 16)
            pe.wait_ge(s_wkv, 3)

            def flip(o, i, start=True):
                return t.matmul(o, i, ident[:], start=start, stop=True, is_transpose=True, skip_group_check=True)

            def step(i, u):
                a0, a1, a2, a3 = (lagged(i, u, k) for k in range(4))
                if a3:
                    t_, p = a3
                    pe.wait_ge(d_pv, t_ + 1)
                    ge(pe, d_cS, t_ + 1)
                    for k in range(H):
                        ins = flip(bank[4][:, 256:384], prod[:, 1, p, k * P:(k + 1) * P], start=k == 0)
                    ins.then_inc(d_O, 1)
                    pe.wait_ge(d_cO, t_ + 1)
                    ge(pe, d_sub, t_ + 1)
                    mm(bank[5][:, 256:384], ones3[:], rows[:, R_BO:R_BO + D], stop=False)
                    mm(bank[5][:, 256:384], OT[:, p, :], W("Wo"), start=False).then_inc(d_w, 1)
                if a0:
                    t_, p = a0
                    pe.wait_ge(d_xn3, t_ + 1)
                    ge(pe, d_cpT, t_)
                    flip(bank[0][:, 0:P], xn3[:, p, :]).then_inc(d_xn3T, 1)
                if a1:
                    t_, p = a1
                    pe.wait_ge(d_h, t_ + 1)
                    ge(pe, d_ch2T, t_ - 2)
                    flip(bank[2][:, 0:P], hrow[:, p, :]).then_inc(d_hT, 1)
                if a0:
                    t_, p = a0
                    pe.wait_ge(d_cxn3, t_ + 1)
                    ge(pe, d_tanh, t_)
                    mm(bank[1][:, 0:P], xn3T[:, p, :], ctxT[:, bass.ds(t_ * P, P)]).then_inc(d_score, 1)
                if a1:
                    t_, p = a1
                    pe.wait_ge(d_chT, t_ + 1)
                    ge(pe, d_gmax, t_ - 2)
                    mm(bank[3][:, 0:3 * D], ones3[:], rowsq[:], stop=False)
                    mm(bank[3][:, 0:3 * D], hTd[:, p, :], wqkv[:], start=False).then_inc(d_qkv, 1)
                if a2:
                    t_, p = a2
                    pe.wait_ge(d_qk, t_ + 1)
                    ge(pe, d_cO, t_)
                    for hh in range(2):
                        for d in range(HD):
                            ins = flip(bank[4][:, hh * P:(hh + 1) * P],
                                       prod[:, 0, p, d * 256 + hh * P:d * 256 + (hh + 1) * P], start=d == 0)
                    ins.then_inc(d_S, 1)
                if a0:
                    t_, p = a0
                    pe.wait_ge(d_p, t_ + 1)
                    flip(bank[0][:, P:2 * P], pr[:, p, :]).then_inc(d_pT, 1)
                if a2:
                    t_, p = a2
                    pe.wait_ge(d_cS, t_ + 1)
                    ge(pe, d_xf2, t_)
                    for hh in range(2):
                        ins = flip(bank[5][:, hh * P:(hh + 1) * P], ST[:, p, hh * P:(hh + 1) * P])
                    ins.then_inc(d_S2, 1)
                if a0:
                    t_, p = a0
                    pe.wait_ge(d_cpT, t_ + 1)
                    mm(bank[1][:, P:2 * P], ones3[:], rows[:, R_BOUT:R_BOUT + D], stop=False)
                    mm(bank[1][:, P:2 * P], xn3T[:, p, :], W("Wo1T"), start=False, stop=False)
                    mm(bank[1][:, P:2 * P], pT[:, p, :], at(xr, t_), start=False).then_inc(d_o, 1)
                if a3:
                    t_, p = a3
                    pe.wait_ge(d_h2, t_ + 1)
                    ge(pe, d_chT, lag_next(i, t_, 3, 1))
                    flip(bank[2][:, P:2 * P], h2[:, p, :]).then_inc(d_h2T, 1)
                    pe.wait_ge(d_ch2T, t_ + 1)
                    ge(pe, d_cqkv, lag_next(i, t_, 3, 1))
                    mm(bank[3][:, 384:384 + NX], ones3[:], rows[:, R_BG:R_BG + NX], stop=False)
                    mm(bank[3][:, 384:384 + NX], h2T[:, p, :], we[:, NX * D:NX * D + NX], start=False).then_inc(d_lg, 1)
                    ge(pe, d_out, t_)
                    for hh in range(2):
                        ins = mm(bank[6 + hh][:], h2T[:, p, :], we[:, g512(hh)])
                    ins.then_inc(d_we, 1)

            run_tiles(pe, step)

        @block.vector
        def _(dve):
            v = nc.vector
            chained = [0]

            def chain(ins):
                chained[0] += 1
                ins.then_inc(dchain, 1)
                dve.wait_ge(dchain, chained[0])

            v.memset(ones3[:], 1.0).then_inc(k_dve, 1)
            v.memset(onesb[:], 1.0).then_inc(k_dve, 1)
            v.memset(zeros[:], 0.0).then_inc(k_dve, 1)
            v.memset(ones24[:], 1.0)
            v.memset(gs[:, 0, :], 0.0).then_inc(gs_ok, 1)
            def stats(k, ready):
                for b in range(k * G4, (k + 1) * G4):
                    ins = v.bn_stats(st[:, b, :], x[:, b, :])
                chain(ins)
                for b in range(k * G4, (k + 1) * G4):
                    ins = v.bn_aggr(mv[:, b, :], st[:, b, :])
                chain(ins)
                c = slice(k * G4, (k + 1) * G4)
                v.tensor_scalar(veps[:, c], mv[:, c, 1:2].rearrange("p b a -> p (b a)"), EPS, None, ALU.add).then_inc(ready, 1)

            def normalise(k, rstd_ok, done):
                dve.wait_ge(rstd_ok, k + 1)
                for b in range(k * G4, (k + 1) * G4):
                    ins = v.tensor_scalar(xn[:, b, :], x[:, b, :], mv[:, b, 0:1], rstd[:, b:b + 1], ALU.subtract, ALU.mult)
                ins.then_inc(done, 1)

            for k in range(NG):
                dve.wait_ge(ld_x[k], 16)
                stats(k, ln1_var)
            for k in range(NG):
                normalise(k, ln1_rstd, ln1_x)
            dve.wait_ge(ld_w, 48)
            chain(v.memset(dec[:], 1.0))
            chain(v.memset(dec[:].rearrange("p (b t) -> p b t", t=T)[:, :, 0:1], 0.0))
            chain(v.tensor_scalar(dec[:], dec[:], col("decay"), None, ALU.mult))
            chain(v.tensor_scalar(hbg[:], col("bg"), 0.5, None, ALU.mult))
            for k in range(NG):
                dve.wait_ge(ctx2, k + 1)
                chain(v.tensor_tensor_scan(rbuf[:, k % 2, :], dec[:], rbuf[:, k % 2, :], 0.0, ALU.mult, ALU.add))
                dve.wait_ge(ln1_t, k + 1)
                o = xr[:].rearrange("p b d -> p (b d)").rearrange("p (t b) -> p b t", b=B)[:, k * G4:(k + 1) * G4, :]
                v.tensor_tensor(o, bank[2 + k % 2][:].rearrange("p (b t) -> p b t", t=T),
                                rbuf[:, k % 2, :].rearrange("p (b t) -> p b t", t=T), ALU.mult).then_inc(retd, 1)
            dve.wait_ge(ld_rowf, 16)
            chain(v.tensor_copy(rowb[:, 0, :], rowf[:, 0, :]))
            chain(v.tensor_tensor(rowf[:, 1, :], rowf[:, 0, :], rowb[:, 0, :], ALU.subtract))
            chain(v.tensor_copy(rowb[:, 1, :], rowf[:, 1, :]))
            chain(v.tensor_tensor(rowf[:, 2, :], rowf[:, 1, :], rowb[:, 1, :], ALU.subtract))
            v.tensor_copy(rowb[:, 2, :], rowf[:, 2, :]).then_inc(k_dve, 5)
            for c in range(NCH):
                dve.wait_ge(s_gate, c + 1)
                dve.wait_ge(s_inp, c + 1)
                gc, ic, oc = gate[:, g512(c)], inp[:, c % 2, :], ginp[:, c % 2, :]
                chain(v.tensor_scalar(gc, gc, 0.5, 0.5, ALU.mult, ALU.add))
                if c >= 2:
                    dve.wait_ge(p_u, c - 1)
                chain(v.tensor_tensor(oc, gc, ic, ALU.mult))
                v.tensor_tensor(oc, ic, oc, ALU.subtract).then_inc(s_ginp, 1)
            def next_gs(tt, u, gcol):
                dve.wait_ge(state_ok, tt + 1)
                v.tensor_tensor(gs[:, (u + 1) % 2, :], gate[:, gcol],
                                sT[:, :, bass.ds(tt, 1)].rearrange("p b t -> p (b t)"), ALU.mult).then_inc(gs_ok, 1)

            with dve.Fori(0, (T - 4) // 4) as i:
                for u in range(4):
                    next_gs(i * 4 + u, u, bass.ds(i * (4 * B) + (u + 1) * B, B))
            for tt in range(T - 4, T - 1):
                next_gs(tt, tt, slice((tt + 1) * B, (tt + 2) * B))
            v.memset(rmse[:], RMS_EPS).then_inc(k_dve, 1)
            chain(v.memset(scanm, 1.0))
            chain(v.memset(scanm[:, :, 0:1], 0.0))
            for k in range(NG):
                dve.wait_ge(p_oT, k + 1)
                xg = seqs(x, k).rearrange("p b d -> p (b d)")
                v.tensor_tensor(xg, bank[2 + k % 2][:], xg, ALU.add).then_inc(x1_ok, 1)
                dve.wait_ge(x1_ok, k + 1)
                stats(k, ln2_var)
                if k:
                    normalise(k - 1, ln2_rstd, ln2_x)
            normalise(NG - 1, ln2_rstd, ln2_x)
            for k in range(NG):
                dve.wait_ge(p_sc, k + 1)
                scg = seqs(sc, k)
                v.tensor_copy(scg.rearrange("p b e -> p (b e)"), bank[6 + k % 2][:, 0:G4 * NE]).then_inc(sc_ok, 1)
                dve.wait_ge(sc_ok, k + 1)
                for b in range(k * G4, (k + 1) * G4):
                    ins = v.max(m8[:, b, :], sc[:, b, :])
                chain(ins)
                for b in range(k * G4, (k + 1) * G4):
                    ins = v.max_index(i8[:, b, :], m8[:, b, :], sc[:, b, :])
                chain(ins)
            for k in range(2):
                chain(v.tensor_copy(i8f[:, k, :], i8[:, :, k:k + 1].rearrange("p b a -> p (b a)")))
            dve.wait_ge(k_iota, 3)
            for k in range(2):
                chain(v.tensor_tensor(pick[k], iota_e[:].unsqueeze(2).to_broadcast([P, NE, B]),
                                      i8f[:, k, :].unsqueeze(1).to_broadcast([P, NE, B]), ALU.is_equal))
            v.tensor_tensor(picks[:], pick[0], pick[1], ALU.add).then_inc(picks_ok, 1)
            v.tensor_tensor(mixs[:], m8[:, :, 1:2].rearrange("p b a -> p (b a)"),
                            m8[:, :, 0:1].rearrange("p b a -> p (b a)"), ALU.subtract).then_inc(mix_d, 1)
            dve.wait_ge(p_cnt, 1)
            fl = lambda z: z[:, :, :].rearrange("p e i -> p (e i)")
            chain(v.tensor_copy(fl(cnt), bank[0][:, 0:NE * B]))
            chain(v.tensor_tensor_scan(fl(incl), fl(scanm), fl(cnt), 0.0, ALU.mult, ALU.add))
            chain(v.tensor_scalar(npad[:], incl[:, :, B - 1:B].rearrange("p e a -> p (e a)"), float(P - 1), None, ALU.add))
            chain(v.tensor_copy(npad_i[:], npad[:]))
            chain(v.tensor_scalar(npad_i[:], npad_i[:], 7, 7, ALU.arith_shift_right, ALU.arith_shift_left))
            chain(v.tensor_copy(npad[:], npad_i[:]))
            chain(v.tensor_tensor_scan(end_e[:], ones24[:], npad[:], 0.0, ALU.mult, ALU.add))
            chain(v.tensor_tensor(base_e[:], end_e[:], npad[:], ALU.subtract))
            chain(v.tensor_tensor(fl(pos), bank[1][:, 0:NE * B], fl(incl), ALU.add))
            chain(v.tensor_tensor(fl(pos), fl(pos), fl(cnt), ALU.subtract))
            chain(v.tensor_tensor(pos, pos, base_e[:].unsqueeze(2).to_broadcast([P, NE, B]), ALU.add))
            for k in range(2):
                chain(v.tensor_tensor(ppos, pick[k].rearrange("p e i -> p i e"),
                                      pos.rearrange("p e i -> p i e"), ALU.mult))
                chain(v.tensor_reduce(slotf[:, k, :], ppos, AX, ALU.add))
            v.tensor_copy(sloti[:], slotf[:]).then_inc(slot_ok, 1)
            chain(v.tensor_tensor(over, end_e[0:1, :].unsqueeze(1).to_broadcast([1, NT, NE]),
                                  slot128[:].unsqueeze(2).to_broadcast([1, NT, NE]), ALU.is_le))
            chain(v.tensor_reduce(tab_f[:], over, AX, ALU.add))
            chain(v.tensor_scalar(tab_f[:], tab_f[:], float(NE - 1), None, ALU.min))
            v.tensor_copy(tab[:], tab_f[:]).then_inc(tab_ok, 1)
            dve.wait_ge(ld_d, 64)
            v.tensor_copy(lens[:], lens_i[:]).then_inc(lens_ok, 1)
            dve.wait_ge(ld_bqf, 16)
            bsum = bqkv[:, 3 * D:6 * D]
            v.tensor_copy(bsum[:, 0:D], bqkv[:, 0:D])
            dve.wait_ge(p_wkv, 2)
            chain(v.tensor_tensor(bsum[:, D:3 * D], bank[7][0:1, 0:2 * D], bqkv[:, D:3 * D], ALU.add))
            chain(v.tensor_copy(bqkv3[:, 0, :], bsum))
            chain(v.tensor_tensor(bsum, bsum, bqkv3[:, 0, :], ALU.subtract))
            chain(v.tensor_copy(bqkv3[:, 1, :], bsum))
            chain(v.tensor_tensor(bsum, bsum, bqkv3[:, 1, :], ALU.subtract))
            v.tensor_copy(bqkv3[:, 2, :], bsum).then_inc(bq3, 1)
            dve.wait_ge(mix_e, 1)
            chain(v.tensor_scalar(mixs[:], mixe[:], 1.0, None, ALU.add))
            chain(v.reciprocal(mix[:, 0, :], mixs[:]))
            chain(v.tensor_tensor(mix[:, 1, :], mixe[:], mix[:, 0, :], ALU.mult))
            chain(v.tensor_tensor(x[:], x[:], xn[:], ALU.add))

            def copy_in(j, u):
                dve.wait_ge(p_in, j + 1)
                if not isinstance(j, int) or j >= 2:
                    dve.wait_ge(p_h, j - 1)
                v.tensor_copy(xsT[:, u, :], bank[0][:, 0:P]).then_inc(s_in, 1)

            def copy_hT(j, u):
                dve.wait_ge(p_hT, j + 1)
                if not isinstance(j, int) or j >= 2:
                    dve.wait_ge(p_y, j - 1)
                v.tensor_copy(hT[:, u, :], bank[3 + u][:]).then_inc(s_hT, 1)

            copy_in(0, 0)
            copy_in(1, 1)
            copy_in(2, 0)
            copy_hT(0, 0)
            copy_in(3, 1)
            copy_hT(1, 1)
            n = (NT - 4) // 2
            with dve.Fori(0, n) as i:
                for u in range(2):
                    copy_in(i * 2 + (4 + u), u)
                    copy_hT(i * 2 + (2 + u), u)
            for j in range(4 + 2 * n, NT + 2):
                if j < NT:
                    copy_in(j, j % 2)
                copy_hT(j - 2, j % 2)
            for i in range(B):
                dve.wait_ge(gathered[i // G4], 32 * G4)
                chain(v.scalar_tensor_tensor(x[:, i, :], yg[:, i, 0, :], mix[:, 0, i:i + 1], x[:, i, :], ALU.mult, ALU.add))
                v.scalar_tensor_tensor(x[:, i, :], yg[:, i, 1, :], mix[:, 1, i:i + 1], x[:, i, :],
                                       ALU.mult, ALU.add).then_inc(x2_ok, 1)

            link = Links(dve, l_dve)

            def settle():
                v.memset(settled[:], 0.0)

            def hd(ap, a, b):
                return ap.rearrange("p (a b) -> p a b", a=a, b=b)

            def step(i, u):
                a0, a1, a2, a3, a4 = (lagged(i, u, k) for k in range(5))

                def pv(part):
                    t, p = a3
                    k = slice(part * 8, part * 8 + 8)
                    o = prod[:, 1, p, :].rearrange("p (g h d) -> p g h d", g=H, h=H)[:, k, :, :]
                    w = hd(pn[:, p, :], H, H).rearrange("p h g -> p g h")[:, k, :].unsqueeze(3).to_broadcast([P, 8, H, HD])
                    vv = hd(qkv[:, p, 2 * D:3 * D], H, HD)[:, k, :].unsqueeze(2).to_broadcast([P, 8, H, HD])
                    return v.tensor_tensor(o, w, vv, ALU.mult)

                def qk(part):
                    t, p = a2
                    k = slice(part * 4, part * 4 + 4)
                    o = prod[:, 0, p, :].rearrange("p (d h g) -> p d h g", d=HD, h=H)[:, k, :, :]
                    q = hd(qkv[:, p, 0:D], HD, H)[:, k, :].unsqueeze(3).to_broadcast([P, 4, H, H])
                    kk = hd(qkv[:, p, D:2 * D], HD, H)[:, k, :].unsqueeze(2).to_broadcast([P, 4, H, H])
                    return v.tensor_tensor(o, q, kk, ALU.mult)

                if a3:
                    t, p = a3
                    dve.wait_ge(d_pn, t + 1)
                    ge(dve, d_O, t - 1)
                    pv(0)
                if a0:
                    t, p = a0
                    settle()
                    link(v.bn_stats(st3[:, p, :], at(x, t)))
                    settle()
                    link(v.bn_aggr(mv3[:, p, :], st3[:, p, :]))
                    v.tensor_scalar(ve3[:, p, :], mv3[:, p, 1:2], EPS, None, ALU.add).then_inc(d_var3, 1)
                if a1:
                    t, p = a1
                    dve.wait_ge(d_tanh, t + 1)
                    v.tensor_tensor(at(x, t), at(x, t), t3[:, p, :], ALU.add).then_inc(d_x3, 1)
                    dve.wait_ge(d_x3, t + 1)
                    settle()
                    link(v.bn_stats(st4[:, p, :], at(x, t)))
                    ge(dve, d_r45, t - 1)
                    settle()
                    link(v.bn_aggr(mv4[:, p, :], st4[:, p, :]))
                    v.tensor_scalar(ve4[:, p, :], mv4[:, p, 1:2], EPS, None, ALU.add).then_inc(d_var4, 1)
                if a3:
                    pv(1).then_inc(d_pv, 1)
                if a0:
                    t, p = a0
                    dve.wait_ge(d_r3, t + 1)
                    ge(dve, d_xn3T, t - 1)
                    v.tensor_scalar(xn3[:, p, :], at(x, t), mv3[:, p, 0:1], r3[:, p, :], ALU.subtract, ALU.mult).then_inc(d_xn3, 1)
                if a1:
                    t, p = a1
                    dve.wait_ge(d_r45, t + 1)
                    ge(dve, d_hT, t - 1)
                    v.tensor_scalar(hrow[:, p, :], at(x, t), mv4[:, p, 0:1], r45[:, p, :], ALU.subtract, ALU.mult).then_inc(d_h, 1)
                    v.tensor_scalar(at(xn, t), at(x, t), mv4[:, p, 0:1], r4[:, p, :], ALU.subtract, ALU.mult).then_inc(d_xf, 1)
                if a2:
                    t, p = a2
                    dve.wait_ge(d_cqkv, t + 1)
                    ge(dve, d_S, t - 1)
                    qk(0)
                if a0:
                    t, p = a0
                    link(v.tensor_scalar(msk[:, p, :], iota_s[:], lens[:, bass.ds(t, 1)], -BIG, ALU.is_ge, ALU.mult))
                    dve.wait_ge(d_score, t + 1)
                    settle()
                    v.tensor_tensor_reduce(out=scs[:, p, :], in0=bank[1][:, 0:P], in1=msk[:, p, :], scale=1.0,
                                           scalar=-BIG, op0=ALU.add, op1=ALU.min, accum_out=mx1[:, p, :]).then_inc(d_masked, 1)
                if a2:
                    qk(1).then_inc(d_qk, 1)
                if a3:
                    t, p = a3
                    dve.wait_ge(d_w, t + 1)
                    dve.wait_ge(d_xf, t + 1)
                    v.tensor_tensor(at(xn, t), bank[5][:, 256:384], at(xn, t), ALU.add).then_inc(d_xf2, 1)
                if a0:
                    t, p = a0
                    dve.wait_ge(d_exp, t + 1)
                    link(v.reciprocal(rc1[:, p, :], sm1[:, p, :]))
                    v.tensor_scalar(pr[:, p, :], pr[:, p, :], rc1[:, p, :], None, ALU.mult).then_inc(d_p, 1)
                if a4:
                    t, p = a4
                    dve.wait_ge(d_we, t + 1)
                    dve.wait_ge(d_gn, t + 1)
                    dve.wait_ge(d_acc, t + 1)
                    for e in range(NX):
                        ins = v.scalar_tensor_tensor(acc[:, p, :], bank[6 + e // 4][:, e % 4 * D:(e % 4 + 1) * D],
                                                     gn8[:, p, e:e + 1], acc[:, p, :], ALU.mult, ALU.add)
                        if e < NX - 1:
                            link(ins)
                    ins.then_inc(d_out, 1)
                if a2:
                    t, p = a2
                    dve.wait_ge(d_S2, t + 1)
                    S2 = hd(bank[5][:, 0:256], H, H)
                    link(v.tensor_reduce(mx16[:, p, :], S2, AX, ALU.max))
                    v.tensor_tensor(hd(ST2[:, p, :], H, H), S2, mx16[:, p, :].unsqueeze(2).to_broadcast([P, H, H]),
                                    ALU.subtract).then_inc(d_sub, 1)
                if a3:
                    t, p = a3
                    dve.wait_ge(d_r6, t + 1)
                    ge(dve, d_h2T, t - 1)
                    v.tensor_scalar(h2[:, p, :], at(xn, t), r6[:, p, :], None, ALU.mult).then_inc(d_h2, 1)
                if a2:
                    t, p = a2
                    dve.wait_ge(d_exp2, t + 1)
                    link(v.tensor_reduce(sum16[:, p, :], hd(pe_[:, p, :], H, H), AX, ALU.add))
                    link(v.reciprocal(rec16[:, p, :], sum16[:, p, :]))
                    v.tensor_tensor(hd(pn[:, p, :], H, H), hd(pe_[:, p, :], H, H),
                                    rec16[:, p, :].unsqueeze(2).to_broadcast([P, H, H]), ALU.mult).then_inc(d_pn, 1)
                if a3:
                    t, p = a3
                    dve.wait_ge(d_lg, t + 1)
                    link(v.tensor_copy(g8[:, p, :], bank[3][:, 384:384 + NX]))
                    link(v.tensor_reduce(g8x[:, p, :], g8[:, p, :], AX, ALU.max))
                    v.tensor_scalar(gmx[:, p, :], g8x[:, p, :], -1.0, None, ALU.mult).then_inc(d_gmax, 1)
                    dve.wait_ge(d_gexp, t + 1)
                    link(v.reciprocal(grc[:, p, :], gsm[:, p, :]))
                    v.tensor_scalar(gn8[:, p, :], ge8[:, p, :], grc[:, p, :], None, ALU.mult).then_inc(d_gn, 1)

            dve.wait_ge(lens_ok, 1)
            dve.wait_ge(x2_ok, B)
            run_tiles(dve, step, link)


def kernel(**inputs):
    import numpy as np
    import concourse.bacc as bacc
    from concourse.bass_utils import run_bass_kernel_spmd as run

    i = {k: np.asarray(v) for k, v in inputs.items()}
    c = np.ascontiguousarray
    Wout = i["L1_xattn_W_out"]
    dh = lambda w: c(w.reshape(w.shape[:-1] + (H, HD)).swapaxes(-1, -2)).reshape(w.shape)

    def kv(w):
        w = w.reshape(w.shape[:-1] + (H, 2, HD))
        k, v_ = w[..., 0, :], w[..., 1, :]
        flat = w.shape[:-3] + (D,)
        return np.concatenate([c(k.swapaxes(-1, -2)).reshape(flat), c(v_).reshape(flat)], axis=-1)

    wp = {
        "WiT": i["L0_xattn_Wi"].T, "WgT": i["L0_xattn_Wg"].T, "AT": i["L0_xattn_A"].T, "BmT": i["L0_xattn_Bm"].T,
        "Wo0T": i["L0_xattn_Wo"].T, "Win": i["L1_xattn_W_in"], "Wo1T": Wout[:, :D].T, "Wo2T": Wout[:, D:].T,
        "Wq": dh(i["L1_ffn_Wq"]), "Wo": i["L1_ffn_Wo"],
    }
    arrays = {
        "x": c(i["x"]),
        "ctxT": c(i["ctx_1024"].transpose(2, 0, 1)).reshape(D, TOK),
        "wpk": c(np.concatenate([wp[n] for n in W_NAMES], axis=1)),
        "cols": c(np.stack([np.repeat(i["L0_xattn_decay"].reshape(H), HD), i["L0_xattn_bi"], i["L0_xattn_bg"],
                            i["L0_xattn_bo"], i["L1_ffn_gamma1"], i["L1_ffn_gamma2"]], axis=1)),
        "gate_w": c(i["L0_ffn_gate_w"]),
        "rowb": c(np.concatenate([i["L0_ffn_b1"].reshape(-1), i["L0_ffn_b2"].reshape(-1), i["L1_xattn_b_out"],
                                  i["L1_ffn_bo"], i["L0_ffn_gate_b"], i["L1_ffn_bg"]])).reshape(RP, RC),
        "wkv": c(np.concatenate([i["L1_ffn_Wdown"].T, kv(i["L1_ffn_Wup"])], axis=1)),
        "bd": c(i["L1_ffn_bdown"]).reshape(-1, 1),
        "bqkv": c(np.concatenate([dh(i["L1_ffn_bq"]), kv(i["L1_ffn_bup"])])).reshape(1, 3 * D),
        "we": c(np.concatenate([i["L1_ffn_We"].transpose(1, 0, 2).reshape(D, NX * D), i["L1_ffn_Wg"]], axis=1)),
        "lens": c(i["_lenS2"]).reshape(1, B),
        "w1": c(i["L0_ffn_w1"]), "w2": c(i["L0_ffn_w2"]),
    }
    nc = bacc.Bacc("TRN2", target_bir_lowering=False, num_devices=1)
    a = {n: nc.dram_tensor(f"in_{n}", v.shape, mybir.dt.from_np(v.dtype), kind="ExternalInput").ap() for n, v in arrays.items()}
    out = nc.dram_tensor("out_0", (B, T, D), F32, kind="ExternalOutput").ap()
    build(nc, a, out)
    r = run(nc, [{f"in_{n}": v for n, v in arrays.items()}], core_ids=[0])
    return r.results[0]["out_0"]
```

```python
from contextlib import ExitStack

import concourse.bass as bass
from concourse import mybir

ALU = mybir.AluOpType
ACT = mybir.ActivationFunctionType
F32 = mybir.dt.float32
BF16 = mybir.dt.bfloat16
U32 = mybir.dt.uint32
I32 = mybir.dt.int32
AX = mybir.AxisListType.X

P = 128
B, T, D = 16, 128, 128
TOK = B * T
TILES = TOK // P
STEPS = P // B
NE, F = 24, 512
CAP = TOK + P
NT = (2 * TOK + NE * (P - 1)) // P
H, HD = 16, 8
NX = 8
EPS, RMS_EPS = 1e-5, 1e-6
G4 = 4
NG = B // G4
BIG = -1e30
ZERO_AT = (0, 4, 8, 12, 18, 24)
ZG = len(ZERO_AT) - 1
AHEAD, BEHIND = 3, 4

W_NAMES = ("WiT", "WgT", "AT", "BmT", "Wo0T", "Win", "Wo1T", "Wo2T", "Wq", "Wo")
COLS = ("decay", "bi", "bg", "gamma1", "gamma2")
R_B1, R_B2 = 0, NE * F
R_BOUT = R_B2 + NE * D
R_BO = R_BOUT + D
R_BO0 = R_BO + D
R_GB = R_BO0 + D
R_BG = R_GB + NE
NROW = R_BG + NX
RP = 116
RC = NROW // RP
assert RP * RC == NROW


def build(nc, a, out):
    with ExitStack() as ctx:
        def sb(name, shape, dt=F32):
            return ctx.enter_context(nc.sbuf_tensor(name, shape, dt))

        def sem(name):
            return ctx.enter_context(nc.semaphore(name))

        bank = [ctx.enter_context(nc.psum_tensor(f"bank{i}", [P, 512], F32)) for i in range(8)]

        lists = nc.dram_tensor("lists", (NE * CAP, D), F32, kind="Internal").ap()
        said = nc.dram_tensor("said", (NT * P, D), F32, kind="Internal").ap()
        res_dram = nc.dram_tensor("res_dram", (TOK, D), F32, kind="Internal").ap()
        route_dram = nc.dram_tensor("route_dram", (4, TOK), F32, kind="Internal").ap()
        rows_dram = nc.dram_tensor("rows_dram", (3, NROW), BF16, kind="Internal").ap()
        bq_dram = nc.dram_tensor("bq_dram", (3, 3 * D), BF16, kind="Internal").ap()

        w1 = sb("w1", [P, NE * F])
        w2 = sb("w2", [P, NE * 4 * D])
        rows_all = sb("rows_all", [P, NROW // 2])
        rows = rows_all[0:3, :].bitcast(BF16)
        wkv = rows_all[64:128, 0:3 * D]
        bd = rows_all[64:128, 3 * D:3 * D + 1]
        ctxT = sb("ctxT", [P, TOK])
        x = sb("x", [P, B, D])
        xn = sb("xn", [P, B, D])
        cw2 = sb("cw2", [P, B, D])
        rT = sb("rT", [P, B, T])
        sT = sb("sT", [P, TOK])
        wpk = sb("wpk", [P, len(W_NAMES) * P])
        cols = sb("cols", [P, len(COLS)])
        gatew = sb("gatew", [P, NE])
        ident = sb("ident", [P, P])
        rowf = sT[0:RP, 1024:1024 + 3 * RC].rearrange("p (k c) -> p k c", k=3)
        rowb = sT[0:RP, 1536:1536 + 3 * RC].bitcast(BF16)[:, 0:3 * RC].rearrange("p (k c) -> p k c", k=3)
        tiles_a = sb("tiles_a", [P, 8, P])
        xa, ret, inp, ginp = (tiles_a[:, 2 * k:2 * k + 2, :] for k in range(4))
        gate = sb("gate", [P, 3, P])
        hbg = sb("hbg", [P, 1])
        gs = sb("gs", [P, 2, B])
        mhalf = sb("mhalf", [P, 2])
        rmse = sb("rmse", [P, 1])
        settled = sb("settled", [P, 1])
        st1, st2 = (sb(f"st{k}", [P, TILES, 6]) for k in (1, 2))
        mv1, mv2 = (sb(f"mv{k}", [P, TILES, 2]) for k in (1, 2))
        ve1, ve2, rs1, rs2 = (sb(n, [P, TILES]) for n in ("ve1", "ve2", "rs1", "rs2"))
        ones3, minus3 = (sb(n, [3, P], BF16) for n in ("ones3", "minus3"))
        onesb = sb("onesb", [P, P], BF16)
        lower = sb("lower", [P, P], BF16)
        zeros = sb("zeros", [P, P])
        xnT = sb("xnT", [P, 2, P])
        sc = sb("sc", [P, 2, NE])
        m8 = sb("m8", [P, TILES, 8])
        i8 = sb("i8", [P, TILES, 8], U32)
        i8f = sb("i8f", [P, TILES, 2])
        iota_e = sb("iota_e", [P, NE])
        iota_s = sb("iota_s", [P, P])
        iota_p = sb("iota_p", [P, 1])
        ecap = sb("ecap", [P, NE])
        pick = [sb(f"pick{k}", [P, TILES, NE]) for k in range(2)]
        picks = sb("picks", [P, 2, NE], BF16)
        total = sb("total", [P, NE])
        rank = sb("rank", [P, NE])
        junkr = sb("junkr", [P, 2, NE])
        slotf = sb("slotf", [P, 2, TILES])
        sloti = sb("sloti", [P, 2, TILES], I32)
        endrow = sb("endrow", [P, NE])
        endrow_i = sb("endrow_i", [1, NE], I32)
        npad_i = sb("npad_i", [P, NE], I32)
        npad = sb("npad", [P, NE])
        end_e = sb("end_e", [P, NE])
        base_e = sb("base_e", [P, NE])
        ones24 = sb("ones24", [P, NE])
        over = sb("over", [P, NE])
        tabc = sb("tabc", [P, 2])
        tab = sb("tab", [2, P], I32)
        route = sb("route", [P, 4, TILES])
        routeT = sb("routeT", [4 * TILES, P])
        mixe = sb("mixe", [P, TILES])
        mixs = sb("mixs", [P, TILES])
        hS = rT[:, 0:8, :].rearrange("p (u a) b -> p u (a b)", u=2)
        hT = rT[:, 8:16, :].rearrange("p (u a) b -> p u (a b)", u=2)
        xin, xsT, yS = tiles_a[:, 0:4, :], tiles_a[:, 4:6, :], tiles_a[:, 6:8, :]
        dec = cw2[:, 0:G4, :].rearrange("p b t -> p (b t)")
        tmp_re = sT[:, 0:TILES * NE].rearrange("p (i e) -> p i e", e=NE)
        bqkv = sT[0:1, 512:512 + 6 * D]
        bqkv3 = sb("bqkv3", [1, 3, 3 * D], BF16)
        rowsq = sb("rowsq", [3, 3 * D], BF16)
        wqkv = sb("wqkv", [P, 3 * D])
        we = sb("we", [P, NX * D + NX])
        lens_i = sb("lens_i", [P, B], I32)
        lens = sb("lens", [P, B])
        routeD = sb("routeD", [P, 4, B])
        rowD = sb("rowD", [P, 2, B], I32)
        prod = w1[:, 0:4 * 2048].rearrange("p (k u n) -> p k u n", k=2, u=2)
        spare = [0]

        def room(n, u=2):
            at = spare[0]
            spare[0] += n * u
            return w2[:, at:at + n * u].rearrange("p (u n) -> p u n", u=u)

        yg, ysc = ([room(D) for _ in range(2)] for _ in range(2))
        xn3, xn3T, pr, pT, t3, hrow, hTd, OT, h2, h2T, junk = (room(D) for _ in range(11))
        qkv = room(3 * D, 4)
        ST, ST2, pe_, pn = (room(2 * D) for _ in range(4))
        wg = room(NX * D)
        mx16, sum16, rec16 = room(H), room(H), room(H)
        ge8, gn8 = room(NX), room(NX)
        st3, st4 = room(6), room(6)
        mv3, mv4, ve4, r45 = (room(2) for _ in range(4))
        ve3, r3, mx1, sm1, rc1, ssq, ve6, r6, gmx, gsm, grc = (room(1) for _ in range(11))
        assert spare[0] <= NE * 4 * D
        padded = sT[64:65, 1024:2048].bitcast(BF16)

        def W(name):
            k = W_NAMES.index(name)
            return wpk[:, k * P:(k + 1) * P]

        def col(name):
            k = COLS.index(name)
            return cols[:, k:k + 1]

        ld_x = [sem(f"ld_x{g}") for g in range(4)]
        ld_ctx = [sem(f"ld_ctx{g}") for g in range(NG)]
        ld_w, ld_moe, ld_rowf, ld_rows, ld_bqf, ld_d = map(sem, ("ld_w", "ld_moe", "ld_rowf", "ld_rows", "ld_bqf", "ld_d"))
        st_rows, st_res, ld_res, st_route, ld_route = map(sem, ("st_rows", "st_res", "ld_res", "st_route", "ld_route"))
        st_zero = [sem(f"st_zero{g}") for g in range(ZG)]
        bq3, st_bq, ld_bq = map(sem, ("bq3", "st_bq", "ld_bq"))
        k_id0, k_id, k_iota, k_low0, k_low, k_half, k_dve, rows3 = map(
            sem, ("k_id0", "k_id", "k_iota", "k_low0", "k_low", "k_half", "k_dve", "rows3"))
        ln1_var, ln1_rstd, ln1_x, ln1_t, ctx2, rscan, retd = map(
            sem, ("ln1_var", "ln1_rstd", "ln1_x", "ln1_t", "ctx2", "rscan", "retd"))
        p_inp, s_inp, p_gate, s_gate, s_ginp, p_u = map(sem, ("p_inp", "s_inp", "p_gate", "s_gate", "s_ginp", "p_u"))
        gs_ok, u_ok, state_ok, dchain = map(sem, ("gs_ok", "u_ok", "state_ok", "dchain"))
        p_o, x1_ok, ln2_var, ln2_rstd, ln2_x, p_xT, s_xT, p_sc, sc_ok = map(
            sem, ("p_o", "x1_ok", "ln2_var", "ln2_rstd", "ln2_x", "p_xT", "s_xT", "p_sc", "sc_ok"))
        picks_ok, p_cnt, rank_ok, slot_ok, res_ok, scattered = map(
            sem, ("picks_ok", "p_cnt", "rank_ok", "slot_ok", "res_ok", "scattered"))
        p_v, s_v, p_kw, s_kw, p_wkv, s_wkv = map(sem, ("p_v", "s_v", "p_kw", "s_kw", "p_wkv", "s_wkv"))
        endrow_ok, tabc_ok, p_tab, tab_ok, mix_d, mix_e, route_ok, p_route, routeT_ok = map(
            sem, ("endrow_ok", "tabc_ok", "p_tab", "tab_ok", "mix_d", "mix_e", "route_ok", "p_route", "routeT_ok"))
        ld_in = [sem(f"ld_in{u}") for u in range(4)]
        p_in, s_in, p_h, s_h, p_hT, s_hT, p_y, s_y = map(
            sem, ("p_in", "s_in", "p_h", "s_h", "p_hT", "s_hT", "p_y", "s_y"))
        st_y = [sem(f"st_y{u}") for u in range(2)]
        (d_ys, d_x2, d_var3, d_r3, d_xn3, d_xn3T, d_cxn3, d_score, d_min, d_exp, d_rc, d_p, d_pT, d_cpT, d_o,
         d_tanh, d_var4, d_r45, d_h, d_hT, d_chT, d_qkv, d_cqkv, d_qk, d_S, d_cS, d_S2, d_sub, d_exp2, d_rec16,
         d_pn, d_pv, d_O, d_cO, d_w, d_xf2, d_acc, d_ssq, d_r6, d_h2, d_h2T, d_ch2T, d_lg, d_we, d_gmax, d_gexp,
         d_gn, d_wg, d_half, d_moe, d_out, d_row) = (
            sem("d_" + n) for n in (
                "ys x2 var3 r3 xn3 xn3T cxn3 score min exp rc p pT cpT o tanh var4 r45 h hT chT qkv cqkv qk S cS "
                "S2 sub exp2 rec16 pn pv O cO w xf2 acc ssq r6 h2 h2T ch2T lg we gmax gexp gn wg half moe out "
                "row").split())
        gathered = [sem(f"gathered{u}") for u in range(2)]
        st_d, padded_ok = sem("st_d"), sem("padded_ok")
        l_dve, l_pool, l_act = map(sem, ("l_dve", "l_pool", "l_act"))

        block = ctx.enter_context(nc.Block())

        def ge(eng, semaphore, count):
            if not isinstance(count, int) or count > 0:
                eng.wait_ge(semaphore, count)

        LAST = 8

        class Own:

            def __init__(self, eng, semaphore):
                self.eng, self.semaphore, self.n = eng, semaphore, 0

            def __call__(self, ins):
                ins.then_inc(self.semaphore, 1)
                self.n += 1
                return self.n

            def need(self, count):
                self.eng.wait_ge(self.semaphore, count)

        def hd(ap, a, b):
            return ap.rearrange("p (a b) -> p a b", a=a, b=b)

        def seq(i):
            return i if 0 <= i < B else None

        def upto(i):
            return min(max(i + 1, 0), B)

        def tile(j):
            return j if 0 <= j < TILES else None

        def tcol(i):
            return slice(i * P, (i + 1) * P)

        def g512(g):
            return slice(g * 512, (g + 1) * 512)

        def zero_fill(eng, g):
            for e in range(ZERO_AT[g], ZERO_AT[g + 1]):
                end = eng.value_load(endrow_i[0:1, e:e + 1], min_val=0, max_val=NE * CAP - P)
                eng.dma_start(lists[bass.ds(end, P), :], zeros[:]).then_inc(st_zero[g], 16)

        FIRST, STOP = -AHEAD * STEPS, (TILES + BEHIND) * STEPS

        @block.sync
        def _(sp):
            xv = a["x"].rearrange("(i p) d -> p i d", p=P)
            for g in range(4):
                sp.dma_start(x[:, 4 * g:4 * g + 4, :], xv[:, 4 * g:4 * g + 4, :]).then_inc(ld_x[g], 16)
            sp.dma_start(rowf[:, 0, :], a["rowb"]).then_inc(ld_rowf, 16)
            for t_, n in ((wkv, "wkv"), (bd, "bd"), (we[:], "we")):
                sp.dma_start(t_, a[n]).then_inc(ld_d, 16)
            sp.dma_start(lens_i[:], a["lens"].to_broadcast([P, B])).then_inc(ld_d, 16)
            sp.wait_ge(rows3, 1)
            sp.dma_start(rows_dram.rearrange("k (p c) -> p k c", p=RP), rowb).then_inc(st_rows, 16)
            sp.wait_ge(st_rows, 16)
            sp.dma_start(rows, rows_dram).then_inc(ld_rows, 16)
            sp.dma_start(w1[:].rearrange("p (e f) -> p e f", e=NE), a["w1"].rearrange("e p f -> p e f")).then_inc(ld_moe, 16)
            sp.dma_start(w2[:].rearrange("p (e c d) -> p e c d", e=NE, c=4),
                         a["w2"].rearrange("e (c p) d -> p e c d", c=4)).then_inc(ld_moe, 16)
            for i in range(TILES):
                sp.wait_ge(res_ok, i + 1)
                sp.dma_start(res_dram[i * P:(i + 1) * P, :], x[:, i, :]).then_inc(st_res, 16)
            sp.wait_ge(endrow_ok, 1)
            zero_fill(sp, 0)
            sp.wait_ge(tab_ok, 1)
            sp.wait_ge(scattered, 16 * 2 * TILES)
            so = said.rearrange("(n p) d -> n p d", p=P)

            def load(j, u):
                if isinstance(j, int):
                    for g in range(ZG):
                        if j == ZERO_AT[g] or (j == 0 and g == 0):
                            sp.wait_ge(st_zero[g], 16 * (ZERO_AT[g + 1] - ZERO_AT[g]))
                row = sp.value_load(tab[1:2, bass.ds(j, 1)], min_val=0, max_val=NE * CAP - P)
                sp.dma_start(xin[:, u, :], lists[bass.ds(row, P), :]).then_inc(ld_in[u], 16)

            def store(j, u):
                sp.wait_ge(s_y, j + 1)
                sp.dma_start(so[bass.ds(j, 1), :, :].rearrange("a p d -> p (a d)"), yS[:, u, :]).then_inc(st_y[u], 16)

            for j in range(4):
                load(j, j)

            def step(j, u):
                if not isinstance(j, int) or j + 4 < NT:
                    sp.wait_ge(p_in, j + 1)
                    load(j + 4, u)
                if not isinstance(j, int) or j >= 3:
                    store(j - 3, (u + 1) % 2)

            full = (NT - 4) // 4
            peeled = NE // 4
            for j in range(4 * peeled):
                step(j, j % 4)
            with sp.Fori(peeled, full) as i:
                for u in range(4):
                    step(i * 4 + u, u)
            for j in range(4 * full, NT + 3):
                step(j, j % 4)

            for t in range(B):
                sp.wait_ge(d_out, t + 1)
                sp.dma_start(out[t, :, :], x[:, t, :]).then_inc(st_d, 16)
            sp.wait_ge(st_d, 16 * B)

        @block.gpsimd
        def _(pool):
            g = nc.gpsimd
            g.memset(mhalf[:], -0.5).then_inc(k_half, 1)
            g.memset(ident[:], 0.0).then_inc(k_id0, 1)
            g.memset(lower[:], 1.0).then_inc(k_low0, 1)
            pool.wait_ge(k_id0, 1)
            g.affine_select(out=ident[:], in_=ident[:], compare_op=ALU.not_equal, fill=1.0, base=0,
                            pattern=[[-1, P]], channel_multiplier=1).then_inc(k_id, 1)
            pool.wait_ge(k_low0, 1)
            g.affine_select(out=lower[:], in_=lower[:], compare_op=ALU.is_gt, fill=0.0, base=0,
                            pattern=[[1, P]], channel_multiplier=-1).then_inc(k_low, 1)
            for tile_, pattern, by in ((iota_e, [[1, NE]], 0), (iota_s, [[1, P]], 0), (iota_p, [[0, 1]], P),
                                       (ecap, [[CAP, NE]], 0)):
                g.iota(tile_[:], pattern=pattern, base=0, channel_multiplier=by,
                       allow_small_or_imprecise_dtypes=True).then_inc(k_iota, 1)
            pool.wait_ge(k_half, 1)
            for j in range(-AHEAD, TILES + BEHIND):
                if (i := tile(j - 2)) is not None:
                    pool.wait_ge(ln2_var, i + 1)
                    g.tensor_tensor(rs2[:, i:i + 1], ve2[:, i:i + 1], mhalf[:, 0:1], ALU.pow).then_inc(ln2_rstd, 1)
                if (m := tile(j + 3)) is not None:
                    pool.wait_ge(ln1_var, m + 1)
                    g.tensor_tensor(rs1[:, m:m + 1], ve1[:, m:m + 1], mhalf[:, 0:1], ALU.pow).then_inc(ln1_rstd, 1)
                if (i := tile(j - 2)) is not None:
                    pool.wait_ge(ln2_x, i + 1)
                    g.tensor_tensor(x[:, i, :], x[:, i, :], xn[:, i, :], ALU.add).then_inc(res_ok, 1)
                if (i := tile(j - 4)) is not None:
                    pool.wait_ge(slot_ok, i + 1)
                    for k in range(2):
                        pool.indirect_dma_start(lists[:, :], bass.IndirectOffsetOnAxis(ap=sloti[:, k, i:i + 1], axis=0),
                                                xn[:, i, :], None).then_inc(scattered, 16)
            pool.wait_ge(p_o, TILES)
            pool.dma_start(bqkv[:, 0:3 * D], a["bqkv"]).then_inc(ld_bqf, 16)
            pool.wait_ge(bq3, 1)
            pool.dma_start(bq_dram.rearrange("k c -> (k c)").unsqueeze(0), bqkv3[:].rearrange("p k c -> p (k c)")).then_inc(st_bq, 16)
            pool.wait_ge(endrow_ok, 1)
            for zg in range(1, ZG):
                zero_fill(pool, zg)
            pool.wait_ge(st_bq, 16)
            pool.dma_start(rowsq[:], bq_dram).then_inc(ld_bq, 16)
            pool.wait_ge(st_res, 16 * TILES)
            pool.dma_start(x[:], res_dram.rearrange("(t b) d -> t b d", b=B)).then_inc(ld_res, 16)
            pool.wait_ge(routeT_ok, 1)
            pool.dma_start(route_dram.rearrange("q (i p) -> (q i) p", p=P), routeT[:]).then_inc(st_route, 16)
            pool.wait_ge(st_route, 16)
            pool.dma_start(routeD[:], route_dram.rearrange("q (t b) -> t q b", b=B)).then_inc(ld_route, 16)
            pool.wait_ge(ld_route, 16)
            g.tensor_copy(rowD[:], routeD[:, 0:2, :]).then_inc(d_row, 1)
            pool.wait_ge(d_row, 1)
            pool.wait_ge(st_y[0], 16 * ((NT + 1) // 2))
            pool.wait_ge(st_y[1], 16 * (NT // 2))
            pool.wait_ge(ld_res, 16)
            own = Own(pool, l_pool)
            for i in range(B + LAST):
                if (t := seq(i)) is not None:
                    p = t % 2
                    ge(pool, d_ys, t - 1)
                    pool.indirect_dma_start(yg[0][:, p, :], None, said[:, :],
                                            bass.IndirectOffsetOnAxis(ap=rowD[:, 0, t:t + 1], axis=0)).then_inc(gathered[p], 16)
                if (t := seq(i)) is not None:
                    p = t % 2
                    pool.indirect_dma_start(yg[1][:, p, :], None, said[:, :],
                                            bass.IndirectOffsetOnAxis(ap=rowD[:, 1, t:t + 1], axis=0)).then_inc(gathered[p], 16)
                if (t := seq(i)) is not None:
                    p = t % 2
                    pool.wait_ge(d_ys, t + 1)
                    x2a = own(g.tensor_tensor(x[:, t, :], x[:, t, :], ysc[0][:, p, :], ALU.add))
                if (t := seq(i)) is not None:
                    p = t % 2
                    own.need(x2a)
                    g.tensor_tensor(x[:, t, :], x[:, t, :], ysc[1][:, p, :], ALU.add).then_inc(d_x2, 1)
                if (t := seq(i)) is not None:
                    p = t % 2
                    pool.wait_ge(d_var3, t + 1)
                    ge(pool, d_xn3, t - 1)
                    g.tensor_tensor(r3[:, p, :], ve3[:, p, :], mhalf[:, 0:1], ALU.pow).then_inc(d_r3, 1)
                if (t := seq(i - 2)) is not None:
                    p = t % 2
                    pool.wait_ge(d_var4, t + 1)
                    ge(pool, d_h, t - 1)
                    g.tensor_tensor(r45[:, p, :], ve4[:, p, :], mhalf[:], ALU.pow).then_inc(d_r45, 1)
                if (t := seq(i - 4)) is not None:
                    p = t % 2
                    pool.wait_ge(d_rec16, t + 1)
                    ge(pool, d_pv, 2 * (t - 1))
                    g.tensor_tensor(hd(pn[:, p, :], H, H), hd(pe_[:, p, :], H, H),
                                    rec16[:, p, :].unsqueeze(2).to_broadcast([P, H, H]), ALU.mult).then_inc(d_pn, 1)
                if (t := seq(i - 5)) is not None:
                    pool.wait_ge(d_xf2, t + 1)
                    g.tensor_tensor(x[:, t, :], x[:, t, :], xn[:, t, :], ALU.add).then_inc(d_acc, 1)
                if (t := seq(i - 5)) is not None:
                    p = t % 2
                    pool.wait_ge(d_ssq, t + 1)
                    ge(pool, d_h2, t - 1)
                    g.tensor_tensor(r6[:, p, :], ve6[:, p, :], mhalf[:, 0:1], ALU.pow).then_inc(d_r6, 1)
                if (t := seq(i - 7)) is not None:
                    p = t % 2
                    pool.wait_ge(d_wg, 2 * t + 2)
                    g.tensor_tensor(wg[:, p, g512(0)], wg[:, p, g512(0)], wg[:, p, g512(1)], ALU.add).then_inc(d_half, 1)

        @block.scalar
        def _(act):
            s = nc.scalar
            for k in range(NG):
                act.dma_start(ctxT[:, g512(k)], a["ctxT"][:, g512(k)]).then_inc(ld_ctx[k], 16)
            for t, n in ((wpk, "wpk"), (cols, "cols"), (gatew, "gate_w")):
                act.dma_start(t[:], a[n]).then_inc(ld_w, 16)
            for k in range(NG):
                act.wait_ge(ld_ctx[k], 16)
                s.activation(rT[:, k * G4:(k + 1) * G4, :].rearrange("p b t -> p (b t)"), ctxT[:, g512(k)],
                             ACT.Square).then_inc(ctx2, 1)
            act.wait_ge(ld_w, 48)
            for t in range(FIRST, STOP):
                if 0 <= t < T:
                    if t == 1024 // B:
                        act.wait_ge(st_rows, 16)
                    act.wait_ge(u_ok, t + 1)
                    s.activation(sT[:, t * B:(t + 1) * B], bank[t // STEPS % 2][:, t % STEPS * B:(t % STEPS + 1) * B],
                                 ACT.Tanh).then_inc(state_ok, 1)
                j, k = divmod(t, STEPS)
                if k == 2 and (m := tile(j + 2)) is not None:
                    act.wait_ge(p_inp, m + 1)
                    ge(act, p_u, m - 1)
                    s.activation(inp[:, m % 2, :], bank[3][:, 0:P], ACT.Identity, bias=col("bi")).then_inc(s_inp, 1)
                if k == 4 and (m := tile(j + 2)) is not None:
                    act.wait_ge(p_gate, m + 1)
                    s.activation(gate[:, m % 3, :], bank[3][:, P:2 * P], ACT.Tanh, bias=hbg[:], scale=0.5).then_inc(s_gate, 1)
                if k == 6 and (i := tile(j - 2)) is not None:
                    act.wait_ge(p_xT, i + 1)
                    ge(act, p_sc, i - 1)
                    s.activation(xnT[:, i % 2, :], bank[5][:, 0:P], ACT.Copy).then_inc(s_xT, 1)
                if k == 7 and (b := tile(j)) is not None:
                    act.wait_ge(p_v, b + 1)
                    s.activation(cw2[:, b, :], bank[7][:, 0:P], ACT.Copy).then_inc(s_v, 1)
            for k in range(NG):
                act.wait_ge(p_kw, k + 1)
                s.activation(ctxT[:, g512(k)], bank[k % 2][:], ACT.Copy, scale=-1.0).then_inc(s_kw, 1)
            act.wait_ge(ld_d, 64)
            act.wait_ge(p_wkv, 2)
            s.activation(wqkv[:, D:3 * D], bank[2][:, 0:2 * D], ACT.Copy, scale=col("gamma1")).then_inc(s_wkv, 1)
            s.activation(wqkv[:, 0:D], W("Wq"), ACT.Copy, scale=col("gamma1")).then_inc(s_wkv, 1)
            s.activation(we[:], we[:], ACT.Copy, scale=col("gamma2")).then_inc(s_wkv, 1)
            act.wait_ge(s_wkv, 3)
            s.activation(we[:, NX * D:], we[:, NX * D:], ACT.Copy, scale=-1.0).then_inc(s_wkv, 1)
            act.wait_ge(mix_d, 1)
            s.activation(mixe[:], mixs[:], ACT.Exp).then_inc(mix_e, 1)
            def gelu(j, u):
                act.wait_ge(p_h, j + 1)
                s.activation(hS[:, u, :], bank[1 + u][:], ACT.Gelu).then_inc(s_h, 1)

            def ycopy(j, u, stored):
                act.wait_ge(p_y, j + 1)
                if stored is not None:
                    act.wait_ge(st_y[u], stored)
                s.activation(yS[:, u, :], bank[5 + u][:, 0:D], ACT.Copy).then_inc(s_y, 1)

            gelu(0, 0)
            gelu(1, 1)
            gelu(2, 0)
            ycopy(0, 0, None)
            gelu(3, 1)
            ycopy(1, 1, None)
            n = (NT - 4) // 2
            with act.Fori(0, n) as i:
                for u in range(2):
                    gelu(i * 2 + (4 + u), u)
                    ycopy(i * 2 + (2 + u), u, i * 16 + 16)
            for j in range(4 + 2 * n, NT):
                gelu(j, j % 2)
                ycopy(j - 2, j % 2, 16 * ((j - 2) // 2))
            for j in (NT - 2, NT - 1):
                ycopy(j, j % 2, 16 * (j // 2))

            own = Own(act, l_act)
            for i in range(B + LAST):
                if (t := seq(i - 7)) is not None:
                    p = t % 2
                    act.wait_ge(d_we, 2 * t + 1)
                    act.wait_ge(d_gn, t + 1)
                    ge(act, d_moe, t - 1)
                    for e in range(4):
                        ins = s.activation(wg[:, p, tcol(e)], bank[6][:, tcol(e)], ACT.Copy, scale=gn8[:, p, e:e + 1])
                    ins.then_inc(d_wg, 1)
                if (t := seq(i - 7)) is not None:
                    p = t % 2
                    act.wait_ge(d_we, 2 * t + 2)
                    act.wait_ge(d_gn, t + 1)
                    for e in range(4, NX):
                        ins = s.activation(wg[:, p, tcol(e)], bank[7][:, tcol(e - 4)], ACT.Copy, scale=gn8[:, p, e:e + 1])
                    ins.then_inc(d_wg, 1)
                if (t := seq(i - 5)) is not None:
                    p = t % 2
                    act.wait_ge(d_O, t + 1)
                    ge(act, d_w, t - 1)
                    s.activation(OT[:, p, :], bank[4][:, 256:384], ACT.Copy).then_inc(d_cO, 1)
                if (t := seq(i)) is not None:
                    p = t % 2
                    act.wait_ge(gathered[p], 32 * (t // 2 + 1))
                    ge(act, d_x2, t - 1)
                    for k in range(2):
                        ins = s.activation(ysc[k][:, p, :], yg[k][:, p, :], ACT.Copy, scale=routeD[:, 2 + k, t:t + 1])
                    ins.then_inc(d_ys, 1)
                if (t := seq(i - 6)) is not None:
                    p = t % 2
                    act.wait_ge(d_gmax, t + 1)
                    ge(act, d_gn, t - 1)
                    s.activation(ge8[:, p, :], bank[0][:, 384:384 + NX], ACT.Exp, bias=gmx[:, p, :], scale=-1.0,
                                 accum_out=gsm[:, p, :]).then_inc(d_gexp, 1)
                if (t := seq(i - 4)) is not None:
                    p = t % 2
                    act.wait_ge(d_sub, t + 1)
                    ge(act, d_pn, t - 1)
                    s.activation(pe_[:, p, :], ST2[:, p, :], ACT.Exp, scale=float(HD) ** -0.5).then_inc(d_exp2, 1)
                if (t := seq(i - 5)) is not None:
                    p = t % 2
                    act.wait_ge(d_xf2, t + 1)
                    ssq_ok = own(s.activation(junk[:, p, :], xn[:, t, :], ACT.Square, accum_out=ssq[:, p, :]))
                if (t := seq(i - 5)) is not None:
                    p = t % 2
                    own.need(ssq_ok)
                    ge(act, d_r6, t - 1)
                    s.activation(ve6[:, p, :], ssq[:, p, :], ACT.Identity, bias=rmse[:], scale=1.0 / D).then_inc(d_ssq, 1)
                if (t := seq(i)) is not None:
                    p = t % 2
                    act.wait_ge(d_xn3T, t + 1)
                    ge(act, d_o, t - 1)
                    s.activation(xn3T[:, p, :], bank[0][:, 0:P], ACT.Copy).then_inc(d_cxn3, 1)
                if (t := seq(i - 2)) is not None:
                    p = t % 2
                    act.wait_ge(d_hT, t + 1)
                    ge(act, d_qkv, t - 1)
                    s.activation(hTd[:, p, :], bank[2][:, 0:P], ACT.Copy).then_inc(d_chT, 1)
                if (t := seq(i)) is not None:
                    p = t % 2
                    act.wait_ge(d_min, t + 1)
                    ge(act, d_pT, t - 1)
                    ge(act, d_rc, t - 1)
                    s.activation(pr[:, p, :], bank[1][:, 0:P], ACT.Exp, bias=mx1[:, p, :], scale=-1.0,
                                 accum_out=sm1[:, p, :]).then_inc(d_exp, 1)
                if (t := seq(i - 1)) is not None:
                    p = t % 2
                    act.wait_ge(d_rc, t + 1)
                    s.activation(pr[:, p, :], pr[:, p, :], ACT.Copy, scale=rc1[:, p, :]).then_inc(d_p, 1)
                if (t := seq(i - 5)) is not None:
                    p = t % 2
                    act.wait_ge(d_r6, t + 1)
                    ge(act, d_h2T, t - 1)
                    s.activation(h2[:, p, :], xn[:, t, :], ACT.Copy, scale=r6[:, p, :]).then_inc(d_h2, 1)
                if (t := seq(i - 1)) is not None:
                    p = t % 2
                    act.wait_ge(d_pT, t + 1)
                    ge(act, d_o, t - 1)
                    s.activation(pT[:, p, :], bank[0][:, P:2 * P], ACT.Copy).then_inc(d_cpT, 1)
                if (t := seq(i - 5)) is not None:
                    p = t % 2
                    act.wait_ge(d_h2T, t + 1)
                    ge(act, d_we, 2 * (t - 1))
                    ge(act, d_lg, t - 1)
                    s.activation(h2T[:, p, :], bank[2][:, P:2 * P], ACT.Copy).then_inc(d_ch2T, 1)
                if (t := seq(i - 1)) is not None:
                    p = t % 2
                    act.wait_ge(d_o, t + 1)
                    ge(act, d_var4, t - 1)
                    s.activation(t3[:, p, :], bank[1][:, P:2 * P], ACT.Tanh).then_inc(d_tanh, 1)
                if (t := seq(i - 3)) is not None:
                    p = t % 2
                    act.wait_ge(d_S, t + 1)
                    ge(act, d_S2, t - 1)
                    s.activation(ST[:, p, :], bank[4][:, 0:256], ACT.Copy).then_inc(d_cS, 1)
                if (t := seq(i - 2)) is not None:
                    act.wait_ge(d_qkv, t + 1)
                    ge(act, d_pv, 2 * (t - 3))
                    s.activation(qkv[:, t % 4, :], bank[3][:, 0:3 * D], ACT.Copy).then_inc(d_cqkv, 1)

        @block.tensor
        def _(pe):

            def mm(o, l, r, start=True, stop=True):
                return nc.tensor.matmul(o, l, r, start=start, stop=stop, skip_group_check=True)

            pe.wait_ge(k_id, 1)
            for n in range(FIRST, STOP):
                j, k = divmod(n, STEPS)
                if 0 <= n < T:
                    pe.wait_ge(gs_ok, n + 1)
                    mm(bank[j % 2][:, k * B:(k + 1) * B], W("AT"), gs[:, n % 2, :], start=False, stop=False).then_inc(u_ok, 1)
                if k == 0 and (m := tile(j + 1)) is not None:
                    pe.wait_ge(s_ginp, m + 1)
                    ge(pe, state_ok, (m - 1) * STEPS)
                    mm(bank[m % 2][:, 0:P], W("AT"), ginp[:, m % 2, :], stop=False)
                if k == 1 and (m := tile(j + 2)) is not None:
                    pe.wait_ge(retd, m + 1)
                    ge(pe, s_gate, m)
                    pe.wait_ge(ld_w, 48)
                    mm(bank[3][:, 0:P], W("WiT"), ret[:, m % 2, :]).then_inc(p_inp, 1)
                if k == 1 and (i := tile(j - 4)) is not None:
                    pe.wait_ge(picks_ok, i + 1)
                    pe.wait_ge(k_low, 1)
                    ge(pe, rank_ok, i)
                    ge(pe, sc_ok, min(i + 2, TILES))
                    mm(bank[6][:, P:P + NE], onesb[:], picks[:, i % 2, :])
                    mm(bank[6][:, P + NE:P + 2 * NE], lower[:], picks[:, i % 2, :]).then_inc(p_cnt, 1)
                if k == 2 and (m := tile(j + 1)) is not None:
                    mm(bank[m % 2][:, 0:P], W("BmT"), inp[:, m % 2, :], start=False, stop=False).then_inc(p_u, 1)
                if k == 3 and (m := tile(j + 2)) is not None:
                    pe.wait_ge(s_inp, m + 1)
                    mm(bank[3][:, P:2 * P], W("WgT"), inp[:, m % 2, :]).then_inc(p_gate, 1)
                if k == 4 and (i := tile(j - 1)) is not None:
                    pe.wait_ge(state_ok, (i + 1) * STEPS)
                    pe.wait_ge(ld_rows, 16)
                    ge(pe, x1_ok, i)
                    mm(bank[4][:, 0:P], ones3[:], rows[:, R_BO0:R_BO0 + D], stop=False)
                    mm(bank[4][:, 0:P], sT[:, tcol(i)], W("Wo0T"), start=False).then_inc(p_o, 1)
                if k == 5 and (m := tile(j + 3)) is not None:
                    pe.wait_ge(ln1_x, m + 1)
                    ge(pe, retd, m)
                    nc.tensor.transpose(bank[2][:, 0:P], xa[:, m % 2, :], ident[:]).then_inc(ln1_t, 1)
                if k == 5 and (i := tile(j - 2)) is not None:
                    pe.wait_ge(ln2_x, i + 1)
                    ge(pe, s_xT, i)
                    nc.tensor.transpose(bank[5][:, 0:P], xn[:, i, :], ident[:]).then_inc(p_xT, 1)
                if k == 6 and (b := tile(j)) is not None:
                    ge(pe, s_v, b)
                    mm(bank[7][:, 0:P], ctxT[:, tcol(b)], W("Wo2T")).then_inc(p_v, 1)
                if k == 7 and (i := tile(j - 2)) is not None:
                    pe.wait_ge(s_xT, i + 1)
                    ge(pe, sc_ok, i)
                    ge(pe, rank_ok, i - 1)
                    mm(bank[6][:, 0:NE], ones3[:], rows[:, R_GB:R_GB + NE], stop=False)
                    mm(bank[6][:, 0:NE], xnT[:, i % 2, :], gatew[:], start=False).then_inc(p_sc, 1)
                if n == T + 5:
                    pe.wait_ge(state_ok, T)
                    pe.wait_ge(ld_d, 64)
                    mm(bank[3][0:1, 0:2 * D], bd, wkv[:, D:3 * D]).then_inc(p_wkv, 1)
                    mm(bank[2][:, 0:2 * D], wkv[:, 0:D], wkv[:, D:3 * D]).then_inc(p_wkv, 1)
                    for c in range(2):
                        mm(bank[c][:], W("Win"), ctxT[:, g512(c)]).then_inc(p_kw, 1)
            pe.wait_ge(tabc_ok, 1)
            nc.tensor.transpose(bank[4][0:2, 0:P], tabc[:], ident[:]).then_inc(p_tab, 1)
            for c in range(2, 4):
                pe.wait_ge(s_kw, c - 1)
                mm(bank[c % 2][:], W("Win"), ctxT[:, g512(c)]).then_inc(p_kw, 1)
            pe.wait_ge(s_wkv, 1)
            pe.wait_ge(s_kw, NG)
            pe.wait_ge(bq3, 1)
            pe.wait_ge(tab_ok, 1)
            pe.wait_ge(ld_moe, 32)

            def t_in(j, u4, u):
                pe.wait_ge(ld_in[u4], (j + (4 - u4)) * 4)
                nc.tensor.transpose(bank[0][:, 0:P], xin[:, u4, :], ident[:]).then_inc(p_in, 1)

            held = [pe.alloc_register(f"expert{u}") for u in range(4)]

            def fetch(j, u):
                pe.reg_load(held[u % 4], tab[0:1, bass.ds(j, 1)])

            def expert(u):
                return nc.snap(held[u % 4], engines=[pe.engine], min_val=0, max_val=NE - 1)

            w1e = w1[:].rearrange("p (e f) -> p e f", e=NE)
            w2e = w2[:].rearrange("p (e c d) -> p e c d", e=NE, c=4)
            b1e = rows[:, R_B1:R_B1 + NE * F].rearrange("k (e f) -> k e f", e=NE)
            b2e = rows[:, R_B2:R_B2 + NE * D].rearrange("k (e d) -> k e d", e=NE)

            def of(table, e):
                return table[:, bass.ds(e, 1), :].rearrange("p a d -> p (a d)")

            def hidden(j, u, e):
                pe.wait_ge(s_in, j + 1)
                mm(bank[1 + u][:], ones3[:], of(b1e, e), stop=False)
                mm(bank[1 + u][:], xsT[:, u, :], of(w1e, e), start=False).then_inc(p_h, 1)

            def t_hidden(j, u):
                pe.wait_ge(s_h, j + 1)
                for c in range(4):
                    ins = nc.tensor.transpose(bank[3 + u][:, c * P:(c + 1) * P], hS[:, u, c * P:(c + 1) * P], ident[:])
                ins.then_inc(p_hT, 1)

            def yout(j, u, e):
                pe.wait_ge(s_hT, j + 1)
                if not isinstance(j, int) or j >= 2:
                    pe.wait_ge(s_y, j - 1)
                o = bank[5 + u][:, 0:D]
                mm(o, ones3[:], of(b2e, e), stop=False)
                for c in range(4):
                    ins = mm(o, hT[:, u, c * P:(c + 1) * P], of(w2e[:, :, c, :], e),
                             start=False, stop=c == 3)
                ins.then_inc(p_y, 1)

            def step(k, u4, e):
                fixed = isinstance(k, int)
                if not fixed or 0 <= k + 2 < NT:
                    hidden(k + 2, u4 % 2, e[(u4 + 2) % 4])
                if not fixed or k + 3 < NT:
                    t_in(k + 3, (u4 + 3) % 4, (u4 + 3) % 2)
                if not fixed or 0 <= k + 1 < NT:
                    t_hidden(k + 1, (u4 + 1) % 2)
                if not fixed or k + 3 < NT:
                    fetch(k + 3, u4 + 3)
                    e[(u4 + 3) % 4] = expert(u4 + 3)
                if not fixed or k >= 0:
                    yout(k, u4 % 2, e[u4])

            n = (NT - 3) // 4
            e = [None] * 4
            for k in range(-3, 4):
                step(k, k % 4, e)
                if k == 1:
                    pe.wait_ge(route_ok, 1)
                    nc.tensor.transpose(bank[7][0:4 * TILES, 0:P], route[:].rearrange("p q i -> p (q i)"),
                                        ident[:]).then_inc(p_route, 1)
            with pe.Fori(1, n) as i:
                e = [expert(u) for u in range(3)] + [None]
                for u in range(4):
                    step(i * 4 + u, u, e)
            e = [expert(u) for u in range(3)] + [None]
            for k in range(4 * n, NT):
                step(k, k % 4, e)

            pe.wait_ge(ld_bq, 16)
            pe.wait_ge(s_wkv, 4)
            pe.wait_ge(padded_ok, 1)

            def flip(o, i, start=True):
                return nc.tensor.matmul(o, i, ident[:], start=start, stop=True, is_transpose=True, skip_group_check=True)

            def sums(t, half):
                for d in range(HD):
                    ins = flip(bank[4][:, half * P:(half + 1) * P],
                               prod[:, 0, t % 2, d * 256 + half * P:d * 256 + (half + 1) * P], start=d == 0)
                return ins

            for i in range(B + LAST):
                if (t := seq(i - 6)) is not None:
                    p = t % 2
                    pe.wait_ge(d_ch2T, t + 1)
                    ge(pe, d_cpT, upto(i - 2))
                    ge(pe, d_gexp, t)
                    mm(bank[0][:, 384:384 + NX], minus3[:], rows[:, R_BG:R_BG + NX], stop=False)
                    mm(bank[0][:, 384:384 + NX], h2T[:, p, :], we[:, NX * D:NX * D + NX], start=False).then_inc(d_lg, 1)
                if (t := seq(i - 5)) is not None:
                    p = t % 2
                    pe.wait_ge(d_pv, 2 * t + 2)
                    for k in range(H // 2, H):
                        ins = flip(bank[4][:, 256:384], prod[:, 1, p, k * P:(k + 1) * P], start=False)
                    ins.then_inc(d_O, 1)
                if (t := seq(i - 6)) is not None:
                    p = t % 2
                    pe.wait_ge(d_ch2T, t + 1)
                    ge(pe, d_wg, 2 * t - 1)
                    mm(bank[6][:], h2T[:, p, :], we[:, g512(0)]).then_inc(d_we, 1)
                if (t := seq(i - 6)) is not None:
                    p = t % 2
                    ge(pe, d_wg, 2 * t)
                    mm(bank[7][:], h2T[:, p, :], we[:, g512(1)]).then_inc(d_we, 1)
                if (t := seq(i - 5)) is not None:
                    p = t % 2
                    pe.wait_ge(d_cO, t + 1)
                    ge(pe, d_sub, upto(i - 4))
                    ge(pe, d_xf2, t)
                    mm(bank[5][:, 256:384], ones3[:], rows[:, R_BO:R_BO + D], stop=False)
                    mm(bank[5][:, 256:384], OT[:, p, :], W("Wo"), start=False).then_inc(d_w, 1)
                if (t := seq(i - 8)) is not None:
                    p = t % 2
                    pe.wait_ge(d_half, t + 1)
                    ge(pe, d_cqkv, upto(i - 3))
                    ge(pe, d_out, t)
                    for k in range(4):
                        ins = mm(bank[3][:, 384:512], ident[:], wg[:, p, tcol(k)], start=k == 0, stop=k == 3)
                    ins.then_inc(d_moe, 1)
                if (t := seq(i - 3)) is not None:
                    pe.wait_ge(d_qk, t + 1)
                    ge(pe, d_cO, upto(i - 5))
                    ge(pe, d_cS, t)
                    sums(t, 0)
                if (t := seq(i)) is not None:
                    p = t % 2
                    pe.wait_ge(d_xn3, t + 1)
                    ge(pe, d_gexp, upto(i - 6))
                    ge(pe, d_cxn3, t)
                    flip(bank[0][:, 0:P], xn3[:, p, :]).then_inc(d_xn3T, 1)
                if (t := seq(i)) is not None:
                    p = t % 2
                    pe.wait_ge(d_cxn3, t + 1)
                    ge(pe, d_tanh, upto(i - 2))
                    ge(pe, d_exp, t)
                    mm(bank[1][:, 0:P], onesb[64:65, :], padded[:, tcol(t)], stop=False)
                    mm(bank[1][:, 0:P], xn3T[:, p, :], ctxT[:, tcol(t)], start=False).then_inc(d_score, 1)
                if (t := seq(i - 2)) is not None:
                    p = t % 2
                    pe.wait_ge(d_h, t + 1)
                    ge(pe, d_ch2T, upto(i - 6))
                    ge(pe, d_chT, t)
                    flip(bank[2][:, 0:P], hrow[:, p, :]).then_inc(d_hT, 1)
                if (t := seq(i - 3)) is not None:
                    sums(t, 1).then_inc(d_S, 1)
                if (t := seq(i - 1)) is not None:
                    p = t % 2
                    pe.wait_ge(d_p, t + 1)
                    ge(pe, d_cxn3, upto(i - 0))
                    ge(pe, d_cpT, t)
                    flip(bank[0][:, P:2 * P], pr[:, p, :]).then_inc(d_pT, 1)
                if (t := seq(i - 5)) is not None:
                    p = t % 2
                    pe.wait_ge(d_h2, t + 1)
                    ge(pe, d_chT, upto(i - 2))
                    ge(pe, d_ch2T, t)
                    flip(bank[2][:, P:2 * P], h2[:, p, :]).then_inc(d_h2T, 1)
                if (t := seq(i - 1)) is not None:
                    p = t % 2
                    pe.wait_ge(d_cpT, t + 1)
                    ge(pe, d_exp, upto(i - 0))
                    ge(pe, d_tanh, t)
                    mm(bank[1][:, P:2 * P], ones3[:], rows[:, R_BOUT:R_BOUT + D], stop=False)
                    mm(bank[1][:, P:2 * P], xn3T[:, p, :], W("Wo1T"), start=False, stop=False)
                    mm(bank[1][:, P:2 * P], pT[:, p, :], cw2[:, t, :], start=False).then_inc(d_o, 1)
                if (t := seq(i - 2)) is not None:
                    p = t % 2
                    pe.wait_ge(d_chT, t + 1)
                    ge(pe, d_out, upto(i - 8))
                    ge(pe, d_cqkv, t)
                    mm(bank[3][:, 0:3 * D], ones3[:], rowsq[:], stop=False)
                    mm(bank[3][:, 0:3 * D], hTd[:, p, :], wqkv[:], start=False).then_inc(d_qkv, 1)
                if (t := seq(i - 3)) is not None:
                    p = t % 2
                    pe.wait_ge(d_cS, t + 1)
                    ge(pe, d_xf2, upto(i - 5))
                    ge(pe, d_sub, t)
                    for k in range(2):
                        ins = flip(bank[5][:, k * P:(k + 1) * P], ST[:, p, k * P:(k + 1) * P])
                    ins.then_inc(d_S2, 1)
                if (t := seq(i - 4)) is not None:
                    p = t % 2
                    pe.wait_ge(d_pv, 2 * t + 1)
                    ge(pe, d_cS, upto(i - 3))
                    ge(pe, d_cO, t)
                    for k in range(H // 2):
                        flip(bank[4][:, 256:384], prod[:, 1, p, k * P:(k + 1) * P], start=k == 0)

        @block.vector
        def _(dve):
            v = nc.vector
            chained = [0]

            def chain(ins):
                dve.wait_ge(dchain, mark(ins))

            def mark(ins):
                chained[0] += 1
                ins.then_inc(dchain, 1)
                return chained[0]

            v.memset(ones3[:], 1.0).then_inc(k_dve, 1)
            v.memset(minus3[:], -1.0)
            v.memset(onesb[:], 1.0)
            v.memset(zeros[:], 0.0)
            v.memset(ones24[:], 1.0)
            v.memset(total[:], 0.0)
            v.memset(rmse[:], RMS_EPS)
            v.memset(gs[:, 0, :], 0.0).then_inc(gs_ok, 1)
            chain(v.memset(dec, 1.0))
            chain(v.memset(dec.rearrange("p (b t) -> p b t", t=T)[:, :, 0:1], 0.0))
            dve.wait_ge(ld_w, 48)
            chain(v.tensor_scalar(dec, dec, col("decay"), None, ALU.mult))
            v.tensor_scalar(hbg[:], col("bg"), 0.5, None, ALU.mult).then_inc(k_dve, 1)
            for k in range(NG):
                dve.wait_ge(ctx2, k + 1)
                rg = rT[:, k * G4:(k + 1) * G4, :].rearrange("p b t -> p (b t)")
                v.tensor_tensor_scan(rg, dec, rg, 0.0, ALU.mult, ALU.add).then_inc(rscan, 1)

            def stats(src, st, mv, ve, i, ready):
                chain(v.bn_stats(st[:, i, :], src))
                chain(v.bn_aggr(mv[:, i, :], st[:, i, :]))
                v.tensor_scalar(ve[:, i:i + 1], mv[:, i, 1:2], EPS, None, ALU.add).then_inc(ready, 1)

            for t in range(FIRST, STOP):
                if 0 <= t < T - 1:
                    dve.wait_ge(state_ok, t + 1)
                    m, n = divmod(t + 1, STEPS)
                    v.tensor_tensor(gs[:, (t + 1) % 2, :], gate[:, m % 3, n * B:(n + 1) * B],
                                    sT[:, t * B:(t + 1) * B], ALU.mult).then_inc(gs_ok, 1)
                j, k = divmod(t, STEPS)
                if k == 0 and (m := tile(j + 2)) is not None:
                    dve.wait_ge(ln1_t, m + 1)
                    dve.wait_ge(rscan, NG)
                    ge(dve, p_inp, m - 1)
                    v.tensor_tensor(ret[:, m % 2, :].rearrange("p (t b) -> p t b", b=B),
                                    bank[2][:, 0:P].rearrange("p (t b) -> p t b", b=B),
                                    rT[:, :, m * STEPS:(m + 1) * STEPS].rearrange("p b t -> p t b"), ALU.mult).then_inc(retd, 1)
                if k == 0 and (i := tile(j - 2)) is not None:
                    dve.wait_ge(x1_ok, i + 1)
                    chain(v.bn_aggr(mv2[:, i, :], st2[:, i, :]))
                    v.tensor_scalar(ve2[:, i:i + 1], mv2[:, i, 1:2], EPS, None, ALU.add).then_inc(ln2_var, 1)
                if k == 1 and (m := tile(j + 3)) is not None:
                    dve.wait_ge(ld_x[m // 4], 16)
                    stats(x[:, m, :], st1, mv1, ve1, m, ln1_var)
                if k == 0 and (i := tile(j - 3)) is not None:
                    dve.wait_ge(p_sc, i + 1)
                    v.tensor_copy(sc[:, i % 2, :], bank[6][:, 0:NE]).then_inc(sc_ok, 1)
                    dve.wait_ge(sc_ok, i + 1)
                    v.max(m8[:, i, :], sc[:, i % 2, :])
                if k == 2 and (i := tile(j - 3)) is not None:
                    chain(v.memset(settled[:], 0.0))
                    chain(v.max_index(i8[:, i, :], m8[:, i, :], sc[:, i % 2, :]))
                    v.tensor_copy(i8f[:, i, :], i8[:, i, 0:2])
                if k == 3 and (i := tile(j - 4)) is not None:
                    dve.wait_ge(p_cnt, i + 1)
                    v.tensor_tensor(rank[:], bank[6][:, P + NE:P + 2 * NE], total[:], ALU.add)
                    chain(v.tensor_tensor(total[:], bank[6][:, P:P + NE], total[:], ALU.add))
                    v.tensor_tensor(rank[:], rank[:], ecap[:], ALU.add).then_inc(rank_ok, 1)
                if k == 3 and (i := tile(j - 2)) is not None:
                    dve.wait_ge(ln2_rstd, i + 1)
                    v.tensor_scalar(xn[:, i, :], x[:, i, :], mv2[:, i, 0:1], rs2[:, i:i + 1], ALU.subtract,
                                    ALU.mult).then_inc(ln2_x, 1)
                if k == 4 and (m := tile(j + 3)) is not None:
                    dve.wait_ge(ln1_rstd, m + 1)
                    ge(dve, ln1_t, m - 1)
                    v.tensor_scalar(xa[:, m % 2, :], x[:, m, :], mv1[:, m, 0:1], rs1[:, m:m + 1], ALU.subtract,
                                    ALU.mult).then_inc(ln1_x, 1)
                if k == 4 and (i := tile(j - 3)) is not None:
                    dve.wait_ge(k_iota, 4)
                    for q in range(2):
                        ins = v.tensor_scalar(pick[q][:, i, :], iota_e[:], i8f[:, i, q:q + 1], None, ALU.is_equal)
                    picked = mark(ins)
                if k == 5 and (i := tile(j - 3)) is not None:
                    dve.wait_ge(dchain, picked)
                    ge(dve, p_cnt, i - 1)
                    v.tensor_tensor(picks[:, i % 2, :], pick[0][:, i, :], pick[1][:, i, :], ALU.add).then_inc(picks_ok, 1)
                if k == 5 and (m := tile(j + 2)) is not None:
                    dve.wait_ge(s_gate, m + 1)
                    gm, im, om = gate[:, m % 3, :], inp[:, m % 2, :], ginp[:, m % 2, :]
                    chain(v.tensor_scalar(gm, gm, 0.5, 0.5, ALU.mult, ALU.add))
                    ge(dve, p_u, m - 1)
                    gated = mark(v.tensor_tensor(om, gm, im, ALU.mult))
                if k == 6 and (m := tile(j + 2)) is not None:
                    dve.wait_ge(dchain, gated)
                    im, om = inp[:, m % 2, :], ginp[:, m % 2, :]
                    v.tensor_tensor(om, im, om, ALU.subtract).then_inc(s_ginp, 1)
                if k == 6 and (i := tile(j - 4)) is not None:
                    dve.wait_ge(rank_ok, i + 1)
                    for q in range(2):
                        ins = v.tensor_tensor_reduce(out=junkr[:, q, :], in0=pick[q][:, i, :], in1=rank[:], scale=1.0, scalar=0.0,
                                                     op0=ALU.mult, op1=ALU.add, accum_out=slotf[:, q, i:i + 1])
                    chain(ins)
                    v.tensor_copy(sloti[:, :, i:i + 1], slotf[:, :, i:i + 1]).then_inc(slot_ok, 1)
                if k == 6 and (i := tile(j - 1)) is not None:
                    dve.wait_ge(p_o, i + 1)
                    added = mark(v.tensor_tensor(x[:, i, :], bank[4][:, 0:P], x[:, i, :], ALU.add))
                if k == 7 and (i := tile(j - 1)) is not None:
                    dve.wait_ge(dchain, added)
                    v.bn_stats(st2[:, i, :], x[:, i, :]).then_inc(x1_ok, 1)
                if t == -1:
                    dve.wait_ge(ld_rowf, 16)
                    chain(v.tensor_copy(rowb[:, 0, :], rowf[:, 0, :]))
                    chain(v.tensor_tensor(rowf[:, 1, :], rowf[:, 0, :], rowb[:, 0, :], ALU.subtract))
                    chain(v.tensor_copy(rowb[:, 1, :], rowf[:, 1, :]))
                    chain(v.tensor_tensor(rowf[:, 2, :], rowf[:, 1, :], rowb[:, 1, :], ALU.subtract))
                    v.tensor_copy(rowb[:, 2, :], rowf[:, 2, :]).then_inc(rows3, 1)
            v.tensor_tensor(endrow[:], total[:], ecap[:], ALU.add)
            chain(v.tensor_scalar(npad[:], total[:], 1.0, float(P - 1), ALU.max, ALU.add))
            v.tensor_copy(endrow_i[:], endrow[0:1, :]).then_inc(endrow_ok, 1)
            chain(v.tensor_copy(npad_i[:], npad[:]))
            chain(v.tensor_scalar(npad_i[:], npad_i[:], 7, 7, ALU.arith_shift_right, ALU.arith_shift_left))
            chain(v.tensor_copy(npad[:], npad_i[:]))
            chain(v.tensor_tensor_scan(end_e[:], ones24[:], npad[:], 0.0, ALU.mult, ALU.add))
            chain(v.tensor_scalar(over[:], end_e[:], iota_p[:], None, ALU.is_le))
            chain(v.tensor_reduce(tabc[:, 0:1], over[:], AX, ALU.add))
            v.tensor_scalar(junkr[:, 0, :], npad[:], -1.0, float(CAP), ALU.mult, ALU.add)
            chain(v.tensor_scalar(tabc[:, 0:1], tabc[:, 0:1], float(NE - 1), None, ALU.min))
            chain(v.tensor_tensor(junkr[:, 0, :], junkr[:, 0, :], over[:], ALU.mult))
            chain(v.tensor_reduce(tabc[:, 1:2], junkr[:, 0, :], AX, ALU.add))
            chain(v.tensor_tensor(tabc[:, 1:2], tabc[:, 1:2], iota_p[:], ALU.add))
            v.tensor_tensor(tabc[:, 1:2], tabc[:, 1:2], endrow[:, NE - 1:NE], ALU.min).then_inc(tabc_ok, 1)
            dve.wait_ge(p_tab, 1)
            v.tensor_copy(tab[:], bank[4][0:2, 0:P]).then_inc(tab_ok, 1)
            v.tensor_tensor(mixs[:], m8[:, :, 1:2].rearrange("p b a -> p (b a)"),
                            m8[:, :, 0:1].rearrange("p b a -> p (b a)"), ALU.subtract).then_inc(mix_d, 1)
            dve.wait_ge(ld_d, 64)
            v.tensor_copy(lens[:], lens_i[:])
            dve.wait_ge(ld_bqf, 16)
            bsum = bqkv[:, 3 * D:6 * D]
            v.tensor_copy(bsum[:, 0:D], bqkv[:, 0:D])
            dve.wait_ge(p_wkv, 2)
            chain(v.tensor_tensor(bsum[:, D:3 * D], bank[3][0:1, 0:2 * D], bqkv[:, D:3 * D], ALU.add))
            chain(v.tensor_copy(bqkv3[:, 0, :], bsum))
            chain(v.tensor_tensor(bsum, bsum, bqkv3[:, 0, :], ALU.subtract))
            chain(v.tensor_copy(bqkv3[:, 1, :], bsum))
            chain(v.tensor_tensor(bsum, bsum, bqkv3[:, 1, :], ALU.subtract))
            v.tensor_copy(bqkv3[:, 2, :], bsum).then_inc(bq3, 1)
            chain(v.tensor_tensor(base_e[:], end_e[:], npad[:], ALU.subtract))
            chain(v.tensor_tensor(base_e[:], base_e[:], ecap[:], ALU.subtract))
            for q in range(2):
                chain(v.tensor_tensor(tmp_re, pick[q][:], base_e[:].unsqueeze(1).to_broadcast([P, TILES, NE]), ALU.mult))
                chain(v.tensor_reduce(route[:, q, :], tmp_re, AX, ALU.add))
                v.tensor_tensor(route[:, q, :], route[:, q, :], slotf[:, q, :], ALU.add)
            dve.wait_ge(mix_e, 1)
            chain(v.tensor_scalar(mixs[:], mixe[:], 1.0, None, ALU.add))
            chain(v.reciprocal(route[:, 2, :], mixs[:]))
            v.tensor_tensor(route[:, 3, :], mixe[:], route[:, 2, :], ALU.mult).then_inc(route_ok, 1)

            def copy_in(j, u):
                dve.wait_ge(p_in, j + 1)
                if not isinstance(j, int) or j >= 2:
                    dve.wait_ge(p_h, j - 1)
                v.tensor_copy(xsT[:, u, :], bank[0][:, 0:P]).then_inc(s_in, 1)

            def copy_hT(j, u):
                dve.wait_ge(p_hT, j + 1)
                if not isinstance(j, int) or j >= 2:
                    dve.wait_ge(p_y, j - 1)
                v.tensor_copy(hT[:, u, :], bank[3 + u][:]).then_inc(s_hT, 1)

            copy_in(0, 0)
            copy_in(1, 1)
            copy_in(2, 0)
            copy_hT(0, 0)
            copy_in(3, 1)
            copy_hT(1, 1)
            dve.wait_ge(p_route, 1)
            v.tensor_copy(routeT[:], bank[7][0:4 * TILES, 0:P]).then_inc(routeT_ok, 1)
            n = (NT - 4) // 2
            with dve.Fori(0, n) as i:
                for u in range(2):
                    copy_in(i * 2 + (4 + u), u)
                    copy_hT(i * 2 + (2 + u), u)
            for j in range(4 + 2 * n, NT + 2):
                if j < NT:
                    copy_in(j, j % 2)
                copy_hT(j - 2, j % 2)
            pad = padded.rearrange("o (b t) -> o b t", b=B)
            chain(v.tensor_tensor(pad, iota_s[64:65, :].unsqueeze(1).to_broadcast([1, B, T]),
                                  lens[64:65, :].unsqueeze(2).to_broadcast([1, B, T]), ALU.is_ge))
            v.tensor_scalar(padded, padded, -BIG, None, ALU.mult).then_inc(padded_ok, 1)

            def pv(t, part):
                k = slice(part * 8, part * 8 + 8)
                o = prod[:, 1, t % 2, :].rearrange("p (g h d) -> p g h d", g=H, h=H)[:, k, :, :]
                w = hd(pn[:, t % 2, :], H, H).rearrange("p h g -> p g h")[:, k, :].unsqueeze(3).to_broadcast([P, 8, H, HD])
                vv = hd(qkv[:, t % 4, 2 * D:3 * D], H, HD)[:, k, :].unsqueeze(2).to_broadcast([P, 8, H, HD])
                return v.tensor_tensor(o, w, vv, ALU.mult)

            def qk(t, part):
                k = slice(part * 4, part * 4 + 4)
                o = prod[:, 0, t % 2, :].rearrange("p (d h g) -> p d h g", d=HD, h=H)[:, k, :, :]
                q = hd(qkv[:, t % 4, 0:D], HD, H)[:, k, :].unsqueeze(3).to_broadcast([P, 4, H, H])
                kk = hd(qkv[:, t % 4, D:2 * D], HD, H)[:, k, :].unsqueeze(2).to_broadcast([P, 4, H, H])
                return v.tensor_tensor(o, q, kk, ALU.mult)

            dve.wait_ge(ld_route, 16)
            dve.wait_ge(ld_res, 16)
            own = Own(dve, l_dve)
            for i in range(B + LAST):
                if (t := seq(i - 3)) is not None:
                    dve.wait_ge(d_cqkv, t + 1)
                    ge(dve, d_S, t - 1)
                    qk(t, 0)
                if (t := seq(i - 3)) is not None:
                    qk(t, 1).then_inc(d_qk, 1)
                if (t := seq(i - 4)) is not None:
                    p = t % 2
                    dve.wait_ge(d_S2, t + 1)
                    mx16_ok = own(v.tensor_reduce(mx16[:, p, :], hd(bank[5][:, 0:256], H, H), AX, ALU.max))
                if (t := seq(i - 6)) is not None:
                    p = t % 2
                    dve.wait_ge(d_lg, t + 1)
                    ge(dve, d_gexp, t - 1)
                    v.tensor_reduce(gmx[:, p, :], bank[0][:, 384:384 + NX], AX, ALU.min).then_inc(d_gmax, 1)
                if (t := seq(i - 4)) is not None:
                    p = t % 2
                    own.need(mx16_ok)
                    ge(dve, d_exp2, t - 1)
                    v.tensor_tensor(hd(ST2[:, p, :], H, H), hd(bank[5][:, 0:256], H, H),
                                    mx16[:, p, :].unsqueeze(2).to_broadcast([P, H, H]), ALU.subtract).then_inc(d_sub, 1)
                if (t := seq(i - 2)) is not None:
                    p = t % 2
                    own.need(x3_ok)
                    st4_ok = own(v.bn_stats(st4[:, p, :], x[:, t, :]))
                if (t := seq(i - 1)) is not None:
                    p = t % 2
                    dve.wait_ge(d_exp, t + 1)
                    ge(dve, d_p, t - 1)
                    v.reciprocal(rc1[:, p, :], sm1[:, p, :]).then_inc(d_rc, 1)
                if (t := seq(i)) is not None:
                    p = t % 2
                    dve.wait_ge(d_x2, t + 1)
                    st3_ok = own(v.bn_stats(st3[:, p, :], x[:, t, :]))
                if (t := seq(i - 2)) is not None:
                    p = t % 2
                    own.need(st4_ok)
                    mv4_ok = own(v.bn_aggr(mv4[:, p, :], st4[:, p, :]))
                if (t := seq(i)) is not None:
                    p = t % 2
                    own.need(st3_ok)
                    mv3_ok = own(v.bn_aggr(mv3[:, p, :], st3[:, p, :]))
                if (t := seq(i)) is not None:
                    p = t % 2
                    own.need(mv3_ok)
                    ge(dve, d_r3, t - 1)
                    v.tensor_scalar(ve3[:, p, :], mv3[:, p, 1:2], EPS, None, ALU.add).then_inc(d_var3, 1)
                if (t := seq(i - 2)) is not None:
                    p = t % 2
                    own.need(mv4_ok)
                    ge(dve, d_r45, t - 1)
                    v.tensor_scalar(ve4[:, p, 0:1], mv4[:, p, 1:2], EPS, None, ALU.add)
                    v.tensor_scalar(ve4[:, p, 1:2], mv4[:, p, 1:2], 1.0 + RMS_EPS, RMS_EPS * EPS, ALU.mult, ALU.add).then_inc(d_var4, 1)
                if (t := seq(i - 4)) is not None:
                    p = t % 2
                    dve.wait_ge(d_exp2, t + 1)
                    sum16_ok = own(v.tensor_reduce(sum16[:, p, :], hd(pe_[:, p, :], H, H), AX, ALU.add))
                if (t := seq(i - 5)) is not None:
                    dve.wait_ge(d_w, t + 1)
                    v.tensor_tensor(xn[:, t, :], bank[5][:, 256:384], xn[:, t, :], ALU.add).then_inc(d_xf2, 1)
                if (t := seq(i)) is not None:
                    p = t % 2
                    dve.wait_ge(d_r3, t + 1)
                    ge(dve, d_xn3T, t - 1)
                    v.tensor_scalar(xn3[:, p, :], x[:, t, :], mv3[:, p, 0:1], r3[:, p, :], ALU.subtract, ALU.mult).then_inc(d_xn3, 1)
                if (t := seq(i - 4)) is not None:
                    p = t % 2
                    own.need(sum16_ok)
                    ge(dve, d_pn, t - 1)
                    v.reciprocal(rec16[:, p, :], sum16[:, p, :]).then_inc(d_rec16, 1)
                if (t := seq(i - 2)) is not None:
                    p = t % 2
                    dve.wait_ge(d_r45, t + 1)
                    ge(dve, d_hT, t - 1)
                    v.tensor_scalar(xn[:, t, :], x[:, t, :], mv4[:, p, 0:1], r45[:, p, 0:1], ALU.subtract, ALU.mult)
                    v.tensor_scalar(hrow[:, p, :], x[:, t, :], mv4[:, p, 0:1], r45[:, p, 1:2], ALU.subtract, ALU.mult).then_inc(d_h, 1)
                if (t := seq(i - 6)) is not None:
                    p = t % 2
                    dve.wait_ge(d_gexp, t + 1)
                    ge(dve, d_wg, 2 * (t - 1))
                    own.need(own(v.reciprocal(grc[:, p, :], gsm[:, p, :])))
                    v.tensor_scalar(gn8[:, p, :], ge8[:, p, :], grc[:, p, :], None, ALU.mult).then_inc(d_gn, 1)
                if (t := seq(i - 8)) is not None:
                    dve.wait_ge(d_moe, t + 1)
                    dve.wait_ge(d_acc, t + 1)
                    v.tensor_tensor(x[:, t, :], bank[3][:, 384:512], x[:, t, :], ALU.add).then_inc(d_out, 1)
                if (t := seq(i)) is not None:
                    p = t % 2
                    dve.wait_ge(d_score, t + 1)
                    ge(dve, d_exp, t - 1)
                    v.tensor_reduce(mx1[:, p, :], bank[1][:, 0:P], AX, ALU.min).then_inc(d_min, 1)
                if (t := seq(i - 4)) is not None:
                    dve.wait_ge(d_pn, t + 1)
                    ge(dve, d_O, t - 1)
                    pv(t, 0).then_inc(d_pv, 1)
                if (t := seq(i - 4)) is not None:
                    pv(t, 1).then_inc(d_pv, 1)
                if (t := seq(i - 1)) is not None:
                    p = t % 2
                    dve.wait_ge(d_tanh, t + 1)
                    x3_ok = own(v.tensor_tensor(x[:, t, :], x[:, t, :], t3[:, p, :], ALU.add))


def kernel(**inputs):
    import numpy as np
    import concourse.bacc as bacc
    from concourse.bass_utils import run_bass_kernel_spmd as run

    i = {k: np.asarray(v) for k, v in inputs.items()}
    c = np.ascontiguousarray
    Wout = i["L1_xattn_W_out"]
    dh = lambda w: c(w.reshape(w.shape[:-1] + (H, HD)).swapaxes(-1, -2)).reshape(w.shape)

    def kv(w):
        w = w.reshape(w.shape[:-1] + (H, 2, HD))
        k, v_ = w[..., 0, :], w[..., 1, :]
        flat = w.shape[:-3] + (D,)
        return np.concatenate([c(k.swapaxes(-1, -2)).reshape(flat), c(v_).reshape(flat)], axis=-1)

    wp = {
        "WiT": i["L0_xattn_Wi"].T, "WgT": i["L0_xattn_Wg"].T, "AT": i["L0_xattn_A"].T, "BmT": i["L0_xattn_Bm"].T,
        "Wo0T": i["L0_xattn_Wo"].T, "Win": i["L1_xattn_W_in"], "Wo1T": Wout[:, :D].T, "Wo2T": Wout[:, D:].T,
        "Wq": dh(i["L1_ffn_Wq"]), "Wo": i["L1_ffn_Wo"],
    }
    arrays = {
        "x": c(i["x"].transpose(1, 0, 2)).reshape(TOK, D),
        "ctxT": c(i["ctx_1024"].transpose(2, 0, 1)).reshape(D, TOK),
        "wpk": c(np.concatenate([wp[n] for n in W_NAMES], axis=1)),
        "cols": c(np.stack([np.repeat(i["L0_xattn_decay"].reshape(H), HD), i["L0_xattn_bi"], i["L0_xattn_bg"],
                            i["L1_ffn_gamma1"], i["L1_ffn_gamma2"]], axis=1)),
        "gate_w": c(i["L0_ffn_gate_w"]),
        "rowb": c(np.concatenate([i["L0_ffn_b1"].reshape(-1), i["L0_ffn_b2"].reshape(-1), i["L1_xattn_b_out"],
                                  i["L1_ffn_bo"], i["L0_xattn_bo"], i["L0_ffn_gate_b"], i["L1_ffn_bg"]])).reshape(RP, RC),
        "wkv": c(np.concatenate([i["L1_ffn_Wdown"].T, kv(i["L1_ffn_Wup"])], axis=1)),
        "bd": c(i["L1_ffn_bdown"]).reshape(-1, 1),
        "bqkv": c(np.concatenate([dh(i["L1_ffn_bq"]), kv(i["L1_ffn_bup"])])).reshape(1, 3 * D),
        "we": c(np.concatenate([i["L1_ffn_We"].transpose(1, 0, 2).reshape(D, NX * D), i["L1_ffn_Wg"]], axis=1)),
        "lens": c(i["_lenS2"]).reshape(1, B),
        "w1": c(i["L0_ffn_w1"]), "w2": c(i["L0_ffn_w2"]),
    }
    nc = bacc.Bacc("TRN2", target_bir_lowering=False, num_devices=1)
    a = {n: nc.dram_tensor(f"in_{n}", v.shape, mybir.dt.from_np(v.dtype), kind="ExternalInput").ap() for n, v in arrays.items()}
    out = nc.dram_tensor("out_0", (B, T, D), F32, kind="ExternalOutput").ap()
    build(nc, a, out)
    r = run(nc, [{f"in_{n}": v for n, v in arrays.items()}], core_ids=[0])
    return r.results[0]["out_0"]
```

```python
from contextlib import ExitStack

import concourse.bass as bass
from concourse import mybir

ALU = mybir.AluOpType
ACT = mybir.ActivationFunctionType
F32 = mybir.dt.float32
BF16 = mybir.dt.bfloat16
U32 = mybir.dt.uint32
I32 = mybir.dt.int32
AX = mybir.AxisListType.X

P = 128
B, T, D = 16, 128, 128
TOK = B * T
TILES = TOK // P
STEPS = P // B
NE, F = 24, 512
CAP = TOK + P
NT = (2 * TOK + NE * (P - 1)) // P
H, HD = 16, 8
NX = 8
EPS, RMS_EPS = 1e-5, 1e-6
G4 = 4
NG = B // G4
BIG = -1e30
ZERO_AT = (0, 4, 8, 12, 18, 24)
ZG = len(ZERO_AT) - 1
AHEAD, BEHIND = 3, 4

W_NAMES = ("WiT", "WgT", "AT", "BmT", "Wo0T", "Win", "Wo1T", "Wo2T", "Wq", "Wo")
COLS = ("decay", "bi", "bg", "gamma1", "gamma2")
R_B1, R_B2 = 0, NE * F
R_BOUT = R_B2 + NE * D
R_BO = R_BOUT + D
R_BO0 = R_BO + D
R_GB = R_BO0 + D
R_BG = R_GB + NE
NROW = R_BG + NX
RP = 116
RC = NROW // RP
assert RP * RC == NROW


def build(nc, a, out):
    with ExitStack() as ctx:
        def sb(name, shape, dt=F32):
            return ctx.enter_context(nc.sbuf_tensor(name, shape, dt))

        def sem(name):
            return ctx.enter_context(nc.semaphore(name))

        bank = [ctx.enter_context(nc.psum_tensor(f"bank{i}", [P, 512], F32)) for i in range(8)]

        lists = nc.dram_tensor("lists", (NE * CAP, D), F32, kind="Internal").ap()
        said = nc.dram_tensor("said", (NT * P, D), F32, kind="Internal").ap()
        res_dram = nc.dram_tensor("res_dram", (TOK, D), F32, kind="Internal").ap()
        route_dram = nc.dram_tensor("route_dram", (4, TOK), F32, kind="Internal").ap()
        rows_dram = nc.dram_tensor("rows_dram", (3, NROW), BF16, kind="Internal").ap()
        bq_dram = nc.dram_tensor("bq_dram", (3, 3 * D), BF16, kind="Internal").ap()

        w1 = sb("w1", [P, NE * F])
        w2 = sb("w2", [P, NE * 4 * D])
        rows_all = sb("rows_all", [P, NROW // 2])
        rows = rows_all[0:3, :].bitcast(BF16)
        wkv = rows_all[64:128, 0:3 * D]
        bd = rows_all[64:128, 3 * D:3 * D + 1]
        ctxT = sb("ctxT", [P, TOK])
        x = sb("x", [P, B, D])
        xn = sb("xn", [P, B, D])
        cw2 = sb("cw2", [P, B, D])
        rT = sb("rT", [P, B, T])
        sT = sb("sT", [P, TOK])
        wpk = sb("wpk", [P, len(W_NAMES) * P])
        cols = sb("cols", [P, len(COLS)])
        gatew = sb("gatew", [P, NE])
        ident = sb("ident", [P, P])
        rowf = sT[0:RP, 1024:1024 + 3 * RC].rearrange("p (k c) -> p k c", k=3)
        rowb = sT[0:RP, 1536:1536 + 3 * RC].bitcast(BF16)[:, 0:3 * RC].rearrange("p (k c) -> p k c", k=3)
        tiles_a = sb("tiles_a", [P, 8, P])
        xa, ret, inp, ginp = (tiles_a[:, 2 * k:2 * k + 2, :] for k in range(4))
        gate = sb("gate", [P, 3, P])
        hbg = sb("hbg", [P, 1])
        gs = sb("gs", [P, 2, B])
        mhalf = sb("mhalf", [P, 2])
        rmse = sb("rmse", [P, 1])
        settled = sb("settled", [P, 1])
        st1, st2 = (sb(f"st{k}", [P, TILES, 6]) for k in (1, 2))
        mv1, mv2 = (sb(f"mv{k}", [P, TILES, 2]) for k in (1, 2))
        ve1, ve2, rs1, rs2 = (sb(n, [P, TILES]) for n in ("ve1", "ve2", "rs1", "rs2"))
        ones3, minus3 = (sb(n, [3, P], BF16) for n in ("ones3", "minus3"))
        onesb = sb("onesb", [P, P], BF16)
        lower = sb("lower", [P, P], BF16)
        zeros = sb("zeros", [P, P])
        xnT = sb("xnT", [P, 2, P])
        sc = sb("sc", [P, 2, NE])
        m8 = sb("m8", [P, TILES, 8])
        i8 = sb("i8", [P, TILES, 8], U32)
        i8f = sb("i8f", [P, TILES, 2])
        iota_e = sb("iota_e", [P, NE])
        iota_s = sb("iota_s", [P, P])
        iota_p = sb("iota_p", [P, 1])
        ecap = sb("ecap", [P, NE])
        pick = [sb(f"pick{k}", [P, TILES, NE]) for k in range(2)]
        picks = sb("picks", [P, 2, NE], BF16)
        total = sb("total", [P, NE])
        rank = sb("rank", [P, NE])
        junkr = sb("junkr", [P, 2, NE])
        slotf = sb("slotf", [P, 2, TILES])
        sloti = sb("sloti", [P, 2, TILES], I32)
        endrow = sb("endrow", [P, NE])
        endrow_i = sb("endrow_i", [1, NE], I32)
        npad_i = sb("npad_i", [P, NE], I32)
        npad = sb("npad", [P, NE])
        end_e = sb("end_e", [P, NE])
        base_e = sb("base_e", [P, NE])
        ones24 = sb("ones24", [P, NE])
        over = sb("over", [P, NE])
        tabc = sb("tabc", [P, 2])
        tab = sb("tab", [2, P], I32)
        route = sb("route", [P, 4, TILES])
        routeT = sb("routeT", [4 * TILES, P])
        mixe = sb("mixe", [P, TILES])
        mixs = sb("mixs", [P, TILES])
        hS = rT[:, 0:8, :].rearrange("p (u a) b -> p u (a b)", u=2)
        hT = rT[:, 8:16, :].rearrange("p (u a) b -> p u (a b)", u=2)
        xin, xsT, yS = tiles_a[:, 0:4, :], tiles_a[:, 4:6, :], tiles_a[:, 6:8, :]
        dec = cw2[:, 0:G4, :].rearrange("p b t -> p (b t)")
        tmp_re = sT[:, 0:TILES * NE].rearrange("p (i e) -> p i e", e=NE)
        bqkv = sT[0:1, 512:512 + 6 * D]
        bqkv3 = sb("bqkv3", [1, 3, 3 * D], BF16)
        rowsq = sb("rowsq", [3, 3 * D], BF16)
        wqkv = sb("wqkv", [P, 3 * D])
        we = sb("we", [P, NX * D + NX])
        lens_i = sb("lens_i", [P, B], I32)
        lens = sb("lens", [P, B])
        routeD = sb("routeD", [P, 4, B])
        rowD = sb("rowD", [P, 2, B], I32)
        prod = w1[:, 0:4 * 2048].rearrange("p (k u n) -> p k u n", k=2, u=2)
        spare = [0]

        def room(n, u=2):
            at = spare[0]
            spare[0] += n * u
            return w2[:, at:at + n * u].rearrange("p (u n) -> p u n", u=u)

        yg, ysc = ([room(D) for _ in range(2)] for _ in range(2))
        xn3, xn3T, pr, pT, t3, hrow, hTd, OT, h2, h2T, junk = (room(D) for _ in range(11))
        qkv = room(3 * D, 4)
        ST, ST2, pe_, pn = (room(2 * D) for _ in range(4))
        wg = room(NX * D)
        mx16, sum16, rec16 = room(H), room(H), room(H)
        ge8, gn8 = room(NX), room(NX)
        st3, st4 = room(6), room(6)
        mv3, mv4, ve4, r45, nm4 = (room(2) for _ in range(5))
        ve3, r3, nm3, mx1, sm1, rc1, ssq, ve6, r6, gmx, gsm, grc = (room(1) for _ in range(12))
        assert spare[0] <= NE * 4 * D
        padded = sT[64:65, 1024:2048].bitcast(BF16)

        def W(name):
            k = W_NAMES.index(name)
            return wpk[:, k * P:(k + 1) * P]

        def col(name):
            k = COLS.index(name)
            return cols[:, k:k + 1]

        ld_x = [sem(f"ld_x{g}") for g in range(4)]
        ld_ctx = [sem(f"ld_ctx{g}") for g in range(NG)]
        ld_w, ld_moe, ld_rowf, ld_rows, ld_bqf, ld_d = map(sem, ("ld_w", "ld_moe", "ld_rowf", "ld_rows", "ld_bqf", "ld_d"))
        st_rows, st_res, ld_res, st_route, ld_route = map(sem, ("st_rows", "st_res", "ld_res", "st_route", "ld_route"))
        st_zero = [sem(f"st_zero{g}") for g in range(ZG)]
        bq3, st_bq, ld_bq = map(sem, ("bq3", "st_bq", "ld_bq"))
        k_filled, k_shaped, k_iota, k_dve, rows3 = map(
            sem, ("k_filled", "k_shaped", "k_iota", "k_dve", "rows3"))
        ln1_var, ln1_rstd, ln1_x, ln1_t, ctx2, rscan, retd = map(
            sem, ("ln1_var", "ln1_rstd", "ln1_x", "ln1_t", "ctx2", "rscan", "retd"))
        p_inp, s_inp, p_gate, s_gate, s_ginp, p_u = map(sem, ("p_inp", "s_inp", "p_gate", "s_gate", "s_ginp", "p_u"))
        gs_ok, u_ok, state_ok, dchain = map(sem, ("gs_ok", "u_ok", "state_ok", "dchain"))
        p_o, x1_ok, ln2_var, ln2_rstd, ln2_x, p_xT, s_xT, p_sc, sc_ok = map(
            sem, ("p_o", "x1_ok", "ln2_var", "ln2_rstd", "ln2_x", "p_xT", "s_xT", "p_sc", "sc_ok"))
        picks_ok, p_cnt, rank_ok, slot_ok, res_ok, scattered = map(
            sem, ("picks_ok", "p_cnt", "rank_ok", "slot_ok", "res_ok", "scattered"))
        p_v, s_v, p_kw, s_kw, p_wkv, s_wkv = map(sem, ("p_v", "s_v", "p_kw", "s_kw", "p_wkv", "s_wkv"))
        endrow_ok, tabc_ok, p_tab, tab_ok, mix_d, mix_e, route_ok, p_route, routeT_ok = map(
            sem, ("endrow_ok", "tabc_ok", "p_tab", "tab_ok", "mix_d", "mix_e", "route_ok", "p_route", "routeT_ok"))
        ld_in = [sem(f"ld_in{u}") for u in range(4)]
        p_in, s_in, p_h, s_h, p_hT, s_hT, p_y, s_y = map(
            sem, ("p_in", "s_in", "p_h", "s_h", "p_hT", "s_hT", "p_y", "s_y"))
        st_y = [sem(f"st_y{u}") for u in range(2)]
        (d_ys, d_x2, d_var3, d_r3, d_nm3, d_xn3, d_xn3T, d_cxn3, d_score, d_min, d_exp, d_rc, d_p, d_pT, d_cpT,
         d_o, d_tanh, d_x3, d_var4, d_r45, d_nm4, d_h, d_hT, d_chT, d_qkv, d_cqkv, d_qk, d_S, d_cS, d_S2, d_sub,
         d_exp2, d_rec16, d_pn, d_pv, d_O, d_cO, d_w, d_xf2, d_acc, d_ssq, d_r6, d_h2, d_h2T, d_ch2T, d_lg,
         d_we, d_gmax, d_gexp, d_gn, d_wg, d_half, d_moe, d_out, d_row) = (
            sem("d_" + n) for n in (
                "ys x2 var3 r3 nm3 xn3 xn3T cxn3 score min exp rc p pT cpT o tanh x3 var4 r45 nm4 h hT chT qkv "
                "cqkv qk S cS S2 sub exp2 rec16 pn pv O cO w xf2 acc ssq r6 h2 h2T ch2T lg we gmax gexp gn wg "
                "half moe out row").split())
        gathered = [sem(f"gathered{u}") for u in range(2)]
        st_d, padded_ok = sem("st_d"), sem("padded_ok")
        l_dve, l_pool, l_act = map(sem, ("l_dve", "l_pool", "l_act"))

        block = ctx.enter_context(nc.Block())

        def ge(eng, semaphore, count):
            if not isinstance(count, int) or count > 0:
                eng.wait_ge(semaphore, count)

        LAST = 13

        class Own:

            def __init__(self, eng, semaphore):
                self.eng, self.semaphore, self.n = eng, semaphore, 0

            def __call__(self, ins):
                ins.then_inc(self.semaphore, 1)
                self.n += 1
                return self.n

            def need(self, count):
                self.eng.wait_ge(self.semaphore, count)

        def hd(ap, a, b):
            return ap.rearrange("p (a b) -> p a b", a=a, b=b)

        def seq(i):
            return i if 0 <= i < B else None

        def upto(i):
            return min(max(i + 1, 0), B)

        def tile(j):
            return j if 0 <= j < TILES else None

        def tcol(i):
            return slice(i * P, (i + 1) * P)

        def g512(g):
            return slice(g * 512, (g + 1) * 512)

        def zero_fill(eng, g):
            for e in range(ZERO_AT[g], ZERO_AT[g + 1]):
                end = eng.value_load(endrow_i[0:1, e:e + 1], min_val=0, max_val=NE * CAP - P)
                eng.dma_start(lists[bass.ds(end, P), :], zeros[:]).then_inc(st_zero[g], 16)

        FIRST, STOP = -AHEAD * STEPS, (TILES + BEHIND) * STEPS

        @block.sync
        def _(sp):
            xv = a["x"].rearrange("(i p) d -> p i d", p=P)
            sp.dma_start(rowf[:, 0, :], a["rowb"]).then_inc(ld_rowf, 16)
            for g in range(4):
                sp.dma_start(x[:, 4 * g:4 * g + 4, :], xv[:, 4 * g:4 * g + 4, :]).then_inc(ld_x[g], 16)
            for t_, n in ((wkv, "wkv"), (bd, "bd"), (we[:], "we")):
                sp.dma_start(t_, a[n]).then_inc(ld_d, 16)
            sp.dma_start(lens_i[:], a["lens"].to_broadcast([P, B])).then_inc(ld_d, 16)
            sp.wait_ge(rows3, 1)
            sp.dma_start(rows_dram.rearrange("k (p c) -> p k c", p=RP), rowb).then_inc(st_rows, 16)
            sp.wait_ge(st_rows, 16)
            sp.dma_start(rows, rows_dram).then_inc(ld_rows, 16)
            sp.dma_start(w1[:].rearrange("p (e f) -> p e f", e=NE), a["w1"].rearrange("e p f -> p e f")).then_inc(ld_moe, 16)
            sp.dma_start(w2[:].rearrange("p (e c d) -> p e c d", e=NE, c=4),
                         a["w2"].rearrange("e (c p) d -> p e c d", c=4)).then_inc(ld_moe, 16)
            for i in range(TILES):
                sp.wait_ge(res_ok, i + 1)
                sp.dma_start(res_dram[i * P:(i + 1) * P, :], x[:, i, :]).then_inc(st_res, 16)
            sp.wait_ge(endrow_ok, 1)
            zero_fill(sp, 0)
            sp.wait_ge(tab_ok, 1)
            sp.wait_ge(scattered, 16 * 2 * TILES)
            so = said.rearrange("(n p) d -> n p d", p=P)

            def load(j, u):
                if isinstance(j, int):
                    for g in range(ZG):
                        if j == ZERO_AT[g] or (j == 0 and g == 0):
                            sp.wait_ge(st_zero[g], 16 * (ZERO_AT[g + 1] - ZERO_AT[g]))
                row = sp.value_load(tab[1:2, bass.ds(j, 1)], min_val=0, max_val=NE * CAP - P)
                sp.dma_start(xin[:, u, :], lists[bass.ds(row, P), :]).then_inc(ld_in[u], 16)

            def store(j, u):
                sp.wait_ge(s_y, j + 1)
                sp.dma_start(so[bass.ds(j, 1), :, :].rearrange("a p d -> p (a d)"), yS[:, u, :]).then_inc(st_y[u], 16)

            for j in range(4):
                load(j, j)

            def step(j, u):
                if not isinstance(j, int) or j + 4 < NT:
                    sp.wait_ge(p_in, j + 1)
                    load(j + 4, u)
                if not isinstance(j, int) or j >= 3:
                    store(j - 3, (u + 1) % 2)

            full = (NT - 4) // 4
            peeled = NE // 4
            for j in range(4 * peeled):
                step(j, j % 4)
            with sp.Fori(peeled, full) as i:
                for u in range(4):
                    step(i * 4 + u, u)
            for j in range(4 * full, NT + 3):
                step(j, j % 4)

            for t in range(B):
                sp.wait_ge(d_out, t + 1)
                sp.dma_start(out[t, :, :], x[:, t, :]).then_inc(st_d, 16)
            sp.wait_ge(st_d, 16 * B)

        @block.gpsimd
        def _(pool):
            g = nc.gpsimd
            g.memset(mhalf[:], -0.5).then_inc(k_filled, 1)
            g.memset(ident[:], 0.0).then_inc(k_filled, 1)
            g.memset(lower[:], 1.0).then_inc(k_filled, 1)
            pool.wait_ge(k_filled, 3)
            g.affine_select(out=ident[:], in_=ident[:], compare_op=ALU.not_equal, fill=1.0, base=0,
                            pattern=[[-1, P]], channel_multiplier=1).then_inc(k_shaped, 1)
            g.affine_select(out=lower[:], in_=lower[:], compare_op=ALU.is_gt, fill=0.0, base=0,
                            pattern=[[1, P]], channel_multiplier=-1).then_inc(k_shaped, 1)
            for tile_, pattern, by in ((iota_e, [[1, NE]], 0), (iota_s, [[1, P]], 0), (iota_p, [[0, 1]], P),
                                       (ecap, [[CAP, NE]], 0)):
                g.iota(tile_[:], pattern=pattern, base=0, channel_multiplier=by,
                       allow_small_or_imprecise_dtypes=True).then_inc(k_iota, 1)
            for j in range(-AHEAD, TILES + BEHIND):
                if (i := tile(j - 2)) is not None:
                    pool.wait_ge(ln2_var, i + 1)
                    g.tensor_tensor(rs2[:, i:i + 1], ve2[:, i:i + 1], mhalf[:, 0:1], ALU.pow).then_inc(ln2_rstd, 1)
                if (m := tile(j + 3)) is not None:
                    pool.wait_ge(ln1_var, m + 1)
                    g.tensor_tensor(rs1[:, m:m + 1], ve1[:, m:m + 1], mhalf[:, 0:1], ALU.pow).then_inc(ln1_rstd, 1)
                if (i := tile(j - 2)) is not None:
                    pool.wait_ge(ln2_x, i + 1)
                    g.tensor_tensor(x[:, i, :], x[:, i, :], xn[:, i, :], ALU.add).then_inc(res_ok, 1)
                if (i := tile(j - 4)) is not None:
                    pool.wait_ge(slot_ok, i + 1)
                    for k in range(2):
                        pool.indirect_dma_start(lists[:, :], bass.IndirectOffsetOnAxis(ap=sloti[:, k, i:i + 1], axis=0),
                                                xn[:, i, :], None).then_inc(scattered, 16)
            pool.wait_ge(p_o, TILES)
            pool.dma_start(bqkv[:, 0:3 * D], a["bqkv"]).then_inc(ld_bqf, 16)
            pool.wait_ge(endrow_ok, 1)
            for zg in range(1, ZG):
                zero_fill(pool, zg)
            pool.wait_ge(bq3, 1)
            pool.dma_start(bq_dram.rearrange("k c -> (k c)").unsqueeze(0), bqkv3[:].rearrange("p k c -> p (k c)")).then_inc(st_bq, 16)
            pool.wait_ge(st_bq, 16)
            pool.dma_start(rowsq[:], bq_dram).then_inc(ld_bq, 16)
            pool.wait_ge(st_res, 16 * TILES)
            pool.dma_start(x[:], res_dram.rearrange("(t b) d -> t b d", b=B)).then_inc(ld_res, 16)
            pool.wait_ge(routeT_ok, 1)
            pool.dma_start(route_dram.rearrange("q (i p) -> (q i) p", p=P), routeT[:]).then_inc(st_route, 16)
            pool.wait_ge(st_route, 16)
            pool.dma_start(routeD[:], route_dram.rearrange("q (t b) -> t q b", b=B)).then_inc(ld_route, 16)
            pool.wait_ge(ld_route, 16)
            g.tensor_copy(rowD[:], routeD[:, 0:2, :]).then_inc(d_row, 1)
            pool.wait_ge(d_row, 1)
            pool.wait_ge(st_y[0], 16 * ((NT + 1) // 2))
            pool.wait_ge(st_y[1], 16 * (NT // 2))
            pool.wait_ge(ld_res, 16)
            own = Own(pool, l_pool)
            for i in range(-1, B + LAST):
                if (t := seq(i)) is not None:
                    p = t % 2
                    ge(pool, d_ys, t - 1)
                    pool.indirect_dma_start(yg[0][:, p, :], None, said[:, :],
                                            bass.IndirectOffsetOnAxis(ap=rowD[:, 0, t:t + 1], axis=0)).then_inc(gathered[p], 16)
                if (t := seq(i - 4)) is not None:
                    p = t % 2
                    pool.wait_ge(d_var4, t + 1)
                    ge(pool, d_h, t - 1)
                    g.tensor_tensor(r45[:, p, :], ve4[:, p, :], mhalf[:], ALU.pow).then_inc(d_r45, 1)
                if (t := seq(i - 11)) is not None:
                    pool.wait_ge(d_xf2, t + 1)
                    g.tensor_tensor(x[:, t, :], x[:, t, :], xn[:, t, :], ALU.add).then_inc(d_acc, 1)
                if (t := seq(i - 2)) is not None:
                    p = t % 2
                    pool.wait_ge(d_var3, t + 1)
                    ge(pool, d_xn3, t - 1)
                    g.tensor_tensor(r3[:, p, :], ve3[:, p, :], mhalf[:, 0:1], ALU.pow).then_inc(d_r3, 1)
                if (t := seq(i)) is not None:
                    p = t % 2
                    pool.indirect_dma_start(yg[1][:, p, :], None, said[:, :],
                                            bass.IndirectOffsetOnAxis(ap=rowD[:, 1, t:t + 1], axis=0)).then_inc(gathered[p], 16)
                if (t := seq(i - 1)) is not None:
                    p = t % 2
                    pool.wait_ge(d_ys, t + 1)
                    x2a = own(g.tensor_tensor(x[:, t, :], x[:, t, :], ysc[0][:, p, :], ALU.add))
                if (t := seq(i - 11)) is not None:
                    p = t % 2
                    pool.wait_ge(d_wg, 2 * t + 2)
                    g.tensor_tensor(wg[:, p, g512(0)], wg[:, p, g512(0)], wg[:, p, g512(1)], ALU.add).then_inc(d_half, 1)
                if (t := seq(i - 9)) is not None:
                    p = t % 2
                    pool.wait_ge(d_ssq, t + 1)
                    ge(pool, d_h2, t - 1)
                    g.tensor_tensor(r6[:, p, :], ve6[:, p, :], mhalf[:, 0:1], ALU.pow).then_inc(d_r6, 1)
                if (t := seq(i - 7)) is not None:
                    p = t % 2
                    pool.wait_ge(d_rec16, t + 1)
                    ge(pool, d_pv, 2 * (t - 1))
                    g.tensor_tensor(hd(pn[:, p, :], H, H), hd(pe_[:, p, :], H, H),
                                    rec16[:, p, :].unsqueeze(2).to_broadcast([P, H, H]), ALU.mult).then_inc(d_pn, 1)
                if (t := seq(i - 3)) is not None:
                    p = t % 2
                    pool.wait_ge(d_tanh, t + 1)
                    g.tensor_tensor(x[:, t, :], x[:, t, :], t3[:, p, :], ALU.add).then_inc(d_x3, 1)
                if (t := seq(i - 1)) is not None:
                    p = t % 2
                    own.need(x2a)
                    g.tensor_tensor(x[:, t, :], x[:, t, :], ysc[1][:, p, :], ALU.add).then_inc(d_x2, 1)

        @block.scalar
        def _(act):
            s = nc.scalar
            act.dma_start(cols[:], a["cols"]).then_inc(ld_ctx[0], 16)
            for k in range(NG):
                act.dma_start(ctxT[:, g512(k)], a["ctxT"][:, g512(k)]).then_inc(ld_ctx[k], 16)
            for t, n in ((wpk, "wpk"), (gatew, "gate_w")):
                act.dma_start(t[:], a[n]).then_inc(ld_w, 16)
            for k in range(NG):
                act.wait_ge(ld_ctx[k], 32 if k == 0 else 16)
                s.activation(rT[:, k * G4:(k + 1) * G4, :].rearrange("p b t -> p (b t)"), ctxT[:, g512(k)],
                             ACT.Square).then_inc(ctx2, 1)
            act.wait_ge(ld_w, 32)
            for t in range(FIRST, STOP):
                if 0 <= t < T:
                    if t == 1024 // B:
                        act.wait_ge(st_rows, 16)
                    act.wait_ge(u_ok, t + 1)
                    s.activation(sT[:, t * B:(t + 1) * B], bank[t // STEPS % 2][:, t % STEPS * B:(t % STEPS + 1) * B],
                                 ACT.Tanh).then_inc(state_ok, 1)
                j, k = divmod(t, STEPS)

                if k == 2 and (m := tile(j + 2)) is not None:
                    act.wait_ge(p_inp, m + 1)
                    ge(act, p_u, m - 1)
                    s.activation(inp[:, m % 2, :], bank[3][:, 0:P], ACT.Identity, bias=col("bi")).then_inc(s_inp, 1)
                if k == 4 and (m := tile(j + 2)) is not None:
                    act.wait_ge(p_gate, m + 1)
                    s.activation(gate[:, m % 3, :], bank[3][:, P:2 * P], ACT.Tanh, bias=hbg[:], scale=0.5).then_inc(s_gate, 1)
                if k == 6 and (i := tile(j - 2)) is not None:
                    act.wait_ge(p_xT, i + 1)
                    ge(act, p_sc, i - 1)
                    s.activation(xnT[:, i % 2, :], bank[5][:, 0:P], ACT.Copy).then_inc(s_xT, 1)
                if k == 7 and (b := tile(j)) is not None:
                    act.wait_ge(p_v, b + 1)
                    s.activation(cw2[:, b, :], bank[7][:, 0:P], ACT.Copy).then_inc(s_v, 1)
            for k, at_ in enumerate((0, 1, 3, 5)):
                act.wait_ge(p_kw, k + 1)
                s.activation(ctxT[:, g512(k)], bank[at_][:], ACT.Copy, scale=-1.0).then_inc(s_kw, 1)

            act.wait_ge(ld_d, 64)
            act.wait_ge(p_wkv, 2)
            s.activation(wqkv[:, D:3 * D], bank[2][:, 0:2 * D], ACT.Copy, scale=col("gamma1")).then_inc(s_wkv, 1)
            s.activation(wqkv[:, 0:D], W("Wq"), ACT.Copy, scale=col("gamma1")).then_inc(s_wkv, 1)
            s.activation(we[:], we[:], ACT.Copy, scale=col("gamma2")).then_inc(s_wkv, 1)
            act.wait_ge(s_wkv, 3)
            s.activation(we[:, NX * D:], we[:, NX * D:], ACT.Copy, scale=-1.0).then_inc(s_wkv, 1)
            act.wait_ge(mix_d, 1)
            s.activation(mixe[:], mixs[:], ACT.Exp).then_inc(mix_e, 1)
            def gelu(j, u):
                act.wait_ge(p_h, j + 1)
                s.activation(hS[:, u, :], bank[1 + u][:], ACT.Gelu).then_inc(s_h, 1)

            def ycopy(j, u, stored):
                act.wait_ge(p_y, j + 1)
                if stored is not None:
                    act.wait_ge(st_y[u], stored)
                s.activation(yS[:, u, :], bank[5 + u][:, 0:D], ACT.Copy).then_inc(s_y, 1)

            gelu(0, 0)
            gelu(1, 1)
            gelu(2, 0)
            ycopy(0, 0, None)
            gelu(3, 1)
            ycopy(1, 1, None)
            n = (NT - 4) // 2
            with act.Fori(0, n) as i:
                for u in range(2):
                    gelu(i * 2 + (4 + u), u)
                    ycopy(i * 2 + (2 + u), u, i * 16 + 16)
            for j in range(4 + 2 * n, NT):
                gelu(j, j % 2)
                ycopy(j - 2, j % 2, 16 * ((j - 2) // 2))
            for j in (NT - 2, NT - 1):
                ycopy(j, j % 2, 16 * (j // 2))

            own = Own(act, l_act)
            for i in range(0, B + LAST):
                if (t := seq(i - 3)) is not None:
                    p = t % 2
                    act.wait_ge(d_rc, t + 1)
                    s.activation(pr[:, p, :], pr[:, p, :], ACT.Copy, scale=rc1[:, p, :]).then_inc(d_p, 1)
                if (t := seq(i - 1)) is not None:
                    p = t % 2
                    act.wait_ge(gathered[p], 32 * (t // 2 + 1))
                    ge(act, d_x2, t - 1)
                    for k in range(2):
                        ins = s.activation(ysc[k][:, p, :], yg[k][:, p, :], ACT.Copy, scale=routeD[:, 2 + k, t:t + 1])
                    ins.then_inc(d_ys, 1)
                if (t := seq(i - 6)) is not None:
                    p = t % 2
                    act.wait_ge(d_S, t + 1)
                    ge(act, d_S2, t - 1)
                    s.activation(ST[:, p, :], bank[4][:, 0:256], ACT.Copy).then_inc(d_cS, 1)
                if (t := seq(i - 10)) is not None:
                    p = t % 2
                    act.wait_ge(d_gmax, t + 1)
                    ge(act, d_gn, t - 1)
                    s.activation(ge8[:, p, :], bank[0][:, 384:384 + NX], ACT.Exp, bias=gmx[:, p, :], scale=-1.0,
                                 accum_out=gsm[:, p, :]).then_inc(d_gexp, 1)
                if (t := seq(i - 3)) is not None:
                    p = t % 2
                    act.wait_ge(d_pT, t + 1)
                    ge(act, d_o, t - 1)
                    s.activation(pT[:, p, :], bank[0][:, P:2 * P], ACT.Copy).then_inc(d_cpT, 1)
                if (t := seq(i - 4)) is not None:
                    p = t % 2
                    act.wait_ge(d_nm4, t + 1)
                    ge(act, d_hT, t - 1)
                    s.activation(xn[:, t, :], x[:, t, :], ACT.Identity, bias=nm4[:, p, 0:1], scale=r45[:, p, 0:1])
                    s.activation(hrow[:, p, :], x[:, t, :], ACT.Identity, bias=nm4[:, p, 1:2], scale=r45[:, p, 1:2]).then_inc(d_h, 1)
                if (t := seq(i - 9)) is not None:
                    p = t % 2
                    act.wait_ge(d_xf2, t + 1)
                    ssq_ok = own(s.activation(junk[:, p, :], xn[:, t, :], ACT.Square, accum_out=ssq[:, p, :]))
                if (t := seq(i - 9)) is not None:
                    p = t % 2
                    own.need(ssq_ok)
                    ge(act, d_r6, t - 1)
                    s.activation(ve6[:, p, :], ssq[:, p, :], ACT.Identity, bias=rmse[:], scale=1.0 / D).then_inc(d_ssq, 1)
                if (t := seq(i - 2)) is not None:
                    p = t % 2
                    act.wait_ge(d_nm3, t + 1)
                    ge(act, d_xn3T, t - 1)
                    s.activation(xn3[:, p, :], x[:, t, :], ACT.Identity, bias=nm3[:, p, :], scale=r3[:, p, :]).then_inc(d_xn3, 1)
                if (t := seq(i - 3)) is not None:
                    p = t % 2
                    act.wait_ge(d_o, t + 1)
                    ge(act, d_x3, t - 1)
                    s.activation(t3[:, p, :], bank[1][:, P:2 * P], ACT.Tanh).then_inc(d_tanh, 1)
                if (t := seq(i - 9)) is not None:
                    p = t % 2
                    act.wait_ge(d_r6, t + 1)
                    ge(act, d_h2T, t - 1)
                    s.activation(h2[:, p, :], xn[:, t, :], ACT.Copy, scale=r6[:, p, :]).then_inc(d_h2, 1)
                if (t := seq(i - 4)) is not None:
                    p = t % 2
                    act.wait_ge(d_hT, t + 1)
                    ge(act, d_qkv, t - 1)
                    s.activation(hTd[:, p, :], bank[2][:, 0:P], ACT.Copy).then_inc(d_chT, 1)
                if (t := seq(i - 2)) is not None:
                    p = t % 2
                    act.wait_ge(d_xn3T, t + 1)
                    ge(act, d_o, t - 1)
                    s.activation(xn3T[:, p, :], bank[0][:, 0:P], ACT.Copy).then_inc(d_cxn3, 1)
                if (t := seq(i - 8)) is not None:
                    p = t % 2
                    act.wait_ge(d_O, t + 1)
                    ge(act, d_w, t - 1)
                    s.activation(OT[:, p, :], bank[4][:, 256:384], ACT.Copy).then_inc(d_cO, 1)
                if (t := seq(i - 10)) is not None:
                    p = t % 2
                    act.wait_ge(d_we, 2 * t + 1)
                    act.wait_ge(d_gn, t + 1)
                    ge(act, d_moe, t - 1)
                    for e in range(4):
                        ins = s.activation(wg[:, p, tcol(e)], bank[6][:, tcol(e)], ACT.Copy, scale=gn8[:, p, e:e + 1])
                    ins.then_inc(d_wg, 1)
                if (t := seq(i - 9)) is not None:
                    p = t % 2
                    act.wait_ge(d_h2T, t + 1)
                    ge(act, d_we, 2 * (t - 1))
                    ge(act, d_lg, t - 1)
                    s.activation(h2T[:, p, :], bank[2][:, P:2 * P], ACT.Copy).then_inc(d_ch2T, 1)
                if (t := seq(i - 6)) is not None:
                    p = t % 2
                    act.wait_ge(d_sub, t + 1)
                    ge(act, d_pn, t - 1)
                    s.activation(pe_[:, p, :], ST2[:, p, :], ACT.Exp, scale=float(HD) ** -0.5).then_inc(d_exp2, 1)
                if (t := seq(i - 2)) is not None:
                    p = t % 2
                    act.wait_ge(d_min, t + 1)
                    ge(act, d_pT, t - 1)
                    ge(act, d_rc, t - 1)
                    s.activation(pr[:, p, :], bank[1][:, 0:P], ACT.Exp, bias=mx1[:, p, :], scale=-1.0,
                                 accum_out=sm1[:, p, :]).then_inc(d_exp, 1)
                if (t := seq(i - 4)) is not None:
                    act.wait_ge(d_qkv, t + 1)
                    ge(act, d_pv, 2 * (t - 3))
                    s.activation(qkv[:, t % 4, :], bank[3][:, 0:3 * D], ACT.Copy).then_inc(d_cqkv, 1)
                if (t := seq(i - 10)) is not None:
                    p = t % 2
                    act.wait_ge(d_we, 2 * t + 2)
                    act.wait_ge(d_gn, t + 1)
                    for e in range(4, NX):
                        ins = s.activation(wg[:, p, tcol(e)], bank[7][:, tcol(e - 4)], ACT.Copy, scale=gn8[:, p, e:e + 1])
                    ins.then_inc(d_wg, 1)

        @block.tensor
        def _(pe):

            def mm(o, l, r, start=True, stop=True):
                return nc.tensor.matmul(o, l, r, start=start, stop=stop, skip_group_check=True)

            pe.wait_ge(k_shaped, 1)
            for n in range(FIRST, STOP):
                j, k = divmod(n, STEPS)
                if 0 <= n < T:
                    pe.wait_ge(gs_ok, n + 1)
                    mm(bank[j % 2][:, k * B:(k + 1) * B], W("AT"), gs[:, n % 2, :], start=False, stop=False).then_inc(u_ok, 1)
                if k == 0 and (m := tile(j + 1)) is not None:
                    pe.wait_ge(s_ginp, m + 1)
                    ge(pe, state_ok, (m - 1) * STEPS)
                    mm(bank[m % 2][:, 0:P], W("AT"), ginp[:, m % 2, :], stop=False)
                if k == 1 and (m := tile(j + 2)) is not None:
                    pe.wait_ge(retd, m + 1)
                    ge(pe, s_gate, m)
                    pe.wait_ge(ld_w, 32)
                    mm(bank[3][:, 0:P], W("WiT"), ret[:, m % 2, :]).then_inc(p_inp, 1)
                if k == 1 and (i := tile(j - 4)) is not None:
                    pe.wait_ge(picks_ok, i + 1)
                    pe.wait_ge(k_shaped, 2)
                    ge(pe, rank_ok, i)
                    ge(pe, sc_ok, min(i + 2, TILES))
                    mm(bank[6][:, P:P + NE], onesb[:], picks[:, i % 2, :])
                    mm(bank[6][:, P + NE:P + 2 * NE], lower[:], picks[:, i % 2, :]).then_inc(p_cnt, 1)
                if k == 2 and (m := tile(j + 1)) is not None:
                    mm(bank[m % 2][:, 0:P], W("BmT"), inp[:, m % 2, :], start=False, stop=False).then_inc(p_u, 1)
                if k == 3 and (m := tile(j + 2)) is not None:
                    pe.wait_ge(s_inp, m + 1)
                    mm(bank[3][:, P:2 * P], W("WgT"), inp[:, m % 2, :]).then_inc(p_gate, 1)
                if k == 4 and (i := tile(j - 1)) is not None:
                    pe.wait_ge(state_ok, (i + 1) * STEPS)
                    pe.wait_ge(ld_rows, 16)
                    ge(pe, x1_ok, i)
                    mm(bank[4][:, 0:P], ones3[:], rows[:, R_BO0:R_BO0 + D], stop=False)
                    mm(bank[4][:, 0:P], sT[:, tcol(i)], W("Wo0T"), start=False).then_inc(p_o, 1)
                if k == 5 and (m := tile(j + 3)) is not None:
                    pe.wait_ge(ln1_x, m + 1)
                    ge(pe, retd, m)
                    nc.tensor.transpose(bank[2][:, 0:P], xa[:, m % 2, :], ident[:]).then_inc(ln1_t, 1)
                if k == 5 and (i := tile(j - 2)) is not None:
                    pe.wait_ge(ln2_x, i + 1)
                    ge(pe, s_xT, i)

                    nc.tensor.transpose(bank[5][:, 0:P], xn[:, i, :], ident[:]).then_inc(p_xT, 1)
                if k == 6 and (b := tile(j)) is not None:
                    ge(pe, s_v, b)
                    mm(bank[7][:, 0:P], ctxT[:, tcol(b)], W("Wo2T")).then_inc(p_v, 1)
                if k == 7 and (i := tile(j - 2)) is not None:
                    pe.wait_ge(s_xT, i + 1)
                    ge(pe, sc_ok, i)
                    ge(pe, rank_ok, i - 1)
                    mm(bank[6][:, 0:NE], ones3[:], rows[:, R_GB:R_GB + NE], stop=False)
                    mm(bank[6][:, 0:NE], xnT[:, i % 2, :], gatew[:], start=False).then_inc(p_sc, 1)

            pe.wait_ge(ld_d, 64)
            pe.wait_ge(s_v, TILES)
            pe.wait_ge(ln1_t, TILES)
            mm(bank[7][0:1, 0:2 * D], bd, wkv[:, D:3 * D]).then_inc(p_wkv, 1)
            mm(bank[2][:, 0:2 * D], wkv[:, 0:D], wkv[:, D:3 * D]).then_inc(p_wkv, 1)
            pe.wait_ge(tabc_ok, 1)
            nc.tensor.transpose(bank[4][0:2, 0:P], tabc[:], ident[:]).then_inc(p_tab, 1)
            for c in range(4):
                mm(bank[(0, 1, 3, 5)[c]][:], W("Win"), ctxT[:, g512(c)]).then_inc(p_kw, 1)
            pe.wait_ge(s_wkv, 1)
            pe.wait_ge(s_kw, NG)
            pe.wait_ge(tab_ok, 1)
            pe.wait_ge(ld_moe, 32)

            def t_in(j, u4, u):
                pe.wait_ge(ld_in[u4], (j + (4 - u4)) * 4)
                nc.tensor.transpose(bank[0][:, 0:P], xin[:, u4, :], ident[:]).then_inc(p_in, 1)

            held = [pe.alloc_register(f"expert{u}") for u in range(4)]

            def fetch(j, u):
                pe.reg_load(held[u % 4], tab[0:1, bass.ds(j, 1)])

            def expert(u):
                return nc.snap(held[u % 4], engines=[pe.engine], min_val=0, max_val=NE - 1)

            w1e = w1[:].rearrange("p (e f) -> p e f", e=NE)
            w2e = w2[:].rearrange("p (e c d) -> p e c d", e=NE, c=4)
            b1e = rows[:, R_B1:R_B1 + NE * F].rearrange("k (e f) -> k e f", e=NE)
            b2e = rows[:, R_B2:R_B2 + NE * D].rearrange("k (e d) -> k e d", e=NE)

            def of(table, e):
                return table[:, bass.ds(e, 1), :].rearrange("p a d -> p (a d)")

            def hidden(j, u, e):
                pe.wait_ge(s_in, j + 1)
                mm(bank[1 + u][:], ones3[:], of(b1e, e), stop=False)
                mm(bank[1 + u][:], xsT[:, u, :], of(w1e, e), start=False).then_inc(p_h, 1)

            def t_hidden(j, u):
                pe.wait_ge(s_h, j + 1)
                for c in range(4):
                    ins = nc.tensor.transpose(bank[3 + u][:, c * P:(c + 1) * P], hS[:, u, c * P:(c + 1) * P], ident[:])
                ins.then_inc(p_hT, 1)

            def yout(j, u, e):
                pe.wait_ge(s_hT, j + 1)
                if not isinstance(j, int) or j >= 2:
                    pe.wait_ge(s_y, j - 1)
                o = bank[5 + u][:, 0:D]
                mm(o, ones3[:], of(b2e, e), stop=False)
                for c in range(4):
                    ins = mm(o, hT[:, u, c * P:(c + 1) * P], of(w2e[:, :, c, :], e),
                             start=False, stop=c == 3)
                ins.then_inc(p_y, 1)

            def step(k, u4, e):
                fixed = isinstance(k, int)
                if not fixed or 0 <= k + 2 < NT:
                    hidden(k + 2, u4 % 2, e[(u4 + 2) % 4])
                if not fixed or k + 3 < NT:
                    t_in(k + 3, (u4 + 3) % 4, (u4 + 3) % 2)
                if not fixed or 0 <= k + 1 < NT:
                    t_hidden(k + 1, (u4 + 1) % 2)
                if not fixed or k + 3 < NT:
                    fetch(k + 3, u4 + 3)
                    e[(u4 + 3) % 4] = expert(u4 + 3)
                if not fixed or k >= 0:
                    yout(k, u4 % 2, e[u4])

            n = (NT - 3) // 4
            e = [None] * 4
            for k in range(-3, 8):
                step(k, k % 4, e)
                if k == 5:
                    pe.wait_ge(route_ok, 2)
                    pe.wait_ge(bq3, 1)
                    nc.tensor.transpose(bank[7][0:4 * TILES, 0:P], route[:].rearrange("p q i -> p (q i)"),
                                        ident[:]).then_inc(p_route, 1)
            with pe.Fori(2, n) as i:
                e = [expert(u) for u in range(3)] + [None]
                for u in range(4):
                    step(i * 4 + u, u, e)
            e = [expert(u) for u in range(3)] + [None]
            for k in range(4 * n, NT):
                step(k, k % 4, e)

            pe.wait_ge(ld_bq, 16)
            pe.wait_ge(s_wkv, 4)
            pe.wait_ge(padded_ok, 1)

            def flip(o, i, start=True):
                return nc.tensor.matmul(o, i, ident[:], start=start, stop=True, is_transpose=True, skip_group_check=True)

            def sums(t, half):
                for d in range(HD):
                    ins = flip(bank[4][:, half * P:(half + 1) * P],
                               prod[:, 0, t % 2, d * 256 + half * P:d * 256 + (half + 1) * P], start=d == 0)
                return ins

            for i in range(0, B + LAST):
                if (t := seq(i - 8)) is not None:
                    p = t % 2
                    pe.wait_ge(d_pv, 2 * t + 2)
                    for k in range(H // 2, H):
                        ins = flip(bank[4][:, 256:384], prod[:, 1, p, k * P:(k + 1) * P], start=False)
                    ins.then_inc(d_O, 1)
                if (t := seq(i - 2)) is not None:
                    p = t % 2
                    pe.wait_ge(d_xn3, t + 1)
                    ge(pe, d_cpT, upto(i - 3))
                    ge(pe, d_cxn3, t)
                    flip(bank[0][:, 0:P], xn3[:, p, :]).then_inc(d_xn3T, 1)
                if (t := seq(i - 10)) is not None:
                    p = t % 2
                    ge(pe, d_wg, 2 * t)
                    mm(bank[7][:], h2T[:, p, :], we[:, g512(1)]).then_inc(d_we, 1)
                if (t := seq(i - 2)) is not None:
                    p = t % 2
                    pe.wait_ge(d_cxn3, t + 1)
                    ge(pe, d_tanh, upto(i - 3))
                    ge(pe, d_exp, t)
                    mm(bank[1][:, 0:P], onesb[64:65, :], padded[:, tcol(t)], stop=False)
                    mm(bank[1][:, 0:P], xn3T[:, p, :], ctxT[:, tcol(t)], start=False).then_inc(d_score, 1)
                if (t := seq(i - 9)) is not None:
                    p = t % 2
                    pe.wait_ge(d_h2, t + 1)
                    ge(pe, d_chT, upto(i - 4))
                    ge(pe, d_ch2T, t)
                    flip(bank[2][:, P:2 * P], h2[:, p, :]).then_inc(d_h2T, 1)
                if (t := seq(i - 4)) is not None:
                    p = t % 2
                    pe.wait_ge(d_chT, t + 1)
                    ge(pe, d_out, upto(i - 12))
                    ge(pe, d_cqkv, t)
                    mm(bank[3][:, 0:3 * D], ones3[:], rowsq[:], stop=False)
                    mm(bank[3][:, 0:3 * D], hTd[:, p, :], wqkv[:], start=False).then_inc(d_qkv, 1)
                if (t := seq(i - 5)) is not None:
                    pe.wait_ge(d_qk, t + 1)
                    ge(pe, d_cO, upto(i - 8))
                    ge(pe, d_cS, t)
                    sums(t, 0)
                if (t := seq(i - 8)) is not None:
                    p = t % 2
                    pe.wait_ge(d_cO, t + 1)
                    ge(pe, d_sub, upto(i - 6))
                    ge(pe, d_xf2, t)
                    mm(bank[5][:, 256:384], ones3[:], rows[:, R_BO:R_BO + D], stop=False)
                    mm(bank[5][:, 256:384], OT[:, p, :], W("Wo"), start=False).then_inc(d_w, 1)
                if (t := seq(i - 5)) is not None:
                    sums(t, 1).then_inc(d_S, 1)
                if (t := seq(i - 11)) is not None:
                    p = t % 2
                    pe.wait_ge(d_half, t + 1)
                    ge(pe, d_cqkv, upto(i - 4))
                    ge(pe, d_out, t)
                    for k in range(4):
                        ins = mm(bank[3][:, 384:512], ident[:], wg[:, p, tcol(k)], start=k == 0, stop=k == 3)
                    ins.then_inc(d_moe, 1)
                if (t := seq(i - 9)) is not None:
                    p = t % 2
                    pe.wait_ge(d_ch2T, t + 1)
                    ge(pe, d_cxn3, upto(i - 2))
                    ge(pe, d_gexp, t)
                    mm(bank[0][:, 384:384 + NX], minus3[:], rows[:, R_BG:R_BG + NX], stop=False)
                    mm(bank[0][:, 384:384 + NX], h2T[:, p, :], we[:, NX * D:NX * D + NX], start=False).then_inc(d_lg, 1)
                if (t := seq(i - 9)) is not None:
                    p = t % 2
                    pe.wait_ge(d_ch2T, t + 1)
                    ge(pe, d_wg, 2 * t - 1)
                    mm(bank[6][:], h2T[:, p, :], we[:, g512(0)]).then_inc(d_we, 1)
                if (t := seq(i - 2)) is not None:
                    p = t % 2
                    pe.wait_ge(d_p, t + 1)
                    ge(pe, d_gexp, upto(i - 9))
                    ge(pe, d_cpT, t)
                    flip(bank[0][:, P:2 * P], pr[:, p, :]).then_inc(d_pT, 1)
                if (t := seq(i - 7)) is not None:
                    p = t % 2
                    pe.wait_ge(d_pv, 2 * t + 1)
                    ge(pe, d_cS, upto(i - 5))
                    ge(pe, d_cO, t)
                    for k in range(H // 2):
                        flip(bank[4][:, 256:384], prod[:, 1, p, k * P:(k + 1) * P], start=k == 0)
                if (t := seq(i - 2)) is not None:
                    p = t % 2
                    pe.wait_ge(d_cpT, t + 1)
                    ge(pe, d_exp, upto(i - 2))
                    ge(pe, d_tanh, t)
                    mm(bank[1][:, P:2 * P], ones3[:], rows[:, R_BOUT:R_BOUT + D], stop=False)
                    mm(bank[1][:, P:2 * P], xn3T[:, p, :], W("Wo1T"), start=False, stop=False)
                    mm(bank[1][:, P:2 * P], pT[:, p, :], cw2[:, t, :], start=False).then_inc(d_o, 1)
                if (t := seq(i - 5)) is not None:
                    p = t % 2
                    pe.wait_ge(d_cS, t + 1)
                    ge(pe, d_xf2, upto(i - 8))
                    ge(pe, d_sub, t)
                    for k in range(2):
                        ins = flip(bank[5][:, k * P:(k + 1) * P], ST[:, p, k * P:(k + 1) * P])
                    ins.then_inc(d_S2, 1)
                if (t := seq(i - 3)) is not None:
                    p = t % 2
                    pe.wait_ge(d_h, t + 1)
                    ge(pe, d_ch2T, upto(i - 9))
                    ge(pe, d_chT, t)
                    flip(bank[2][:, 0:P], hrow[:, p, :]).then_inc(d_hT, 1)

        @block.vector
        def _(dve):
            v = nc.vector
            chained = [0]

            def chain(ins):
                dve.wait_ge(dchain, mark(ins))

            def mark(ins):
                chained[0] += 1
                ins.then_inc(dchain, 1)
                return chained[0]

            def stats(src, st, mv, ve, i, ready):
                chain(v.bn_stats(st[:, i, :], src))
                chain(v.bn_aggr(mv[:, i, :], st[:, i, :]))
                v.tensor_scalar(ve[:, i:i + 1], mv[:, i, 1:2], EPS, None, ALU.add).then_inc(ready, 1)

            v.memset(ones3[:], 1.0).then_inc(k_dve, 1)
            v.memset(minus3[:], -1.0)
            v.memset(onesb[:], 1.0)
            v.memset(zeros[:], 0.0)
            v.memset(ones24[:], 1.0)
            v.memset(total[:], 0.0)
            v.memset(rmse[:], RMS_EPS)
            v.memset(gs[:, 0, :], 0.0).then_inc(gs_ok, 1)
            chain(v.memset(dec, 1.0))
            chain(v.memset(dec.rearrange("p (b t) -> p b t", t=T)[:, :, 0:1], 0.0))
            dve.wait_ge(ld_ctx[0], 32)
            chain(v.tensor_scalar(dec, dec, col("decay"), None, ALU.mult))
            v.tensor_scalar(hbg[:], col("bg"), 0.5, None, ALU.mult).then_inc(k_dve, 1)
            dve.wait_ge(ld_x[0], 16)
            stats(x[:, 0, :], st1, mv1, ve1, 0, ln1_var)
            dve.wait_ge(ld_rowf, 16)
            chain(v.tensor_copy(rowb[:, 0, :], rowf[:, 0, :]))
            chain(v.tensor_tensor(rowf[:, 1, :], rowf[:, 0, :], rowb[:, 0, :], ALU.subtract))
            chain(v.tensor_copy(rowb[:, 1, :], rowf[:, 1, :]))
            chain(v.tensor_tensor(rowf[:, 2, :], rowf[:, 1, :], rowb[:, 1, :], ALU.subtract))
            v.tensor_copy(rowb[:, 2, :], rowf[:, 2, :]).then_inc(rows3, 1)
            for k in range(NG):
                dve.wait_ge(ctx2, k + 1)
                rg = rT[:, k * G4:(k + 1) * G4, :].rearrange("p b t -> p (b t)")
                v.tensor_tensor_scan(rg, dec, rg, 0.0, ALU.mult, ALU.add).then_inc(rscan, 1)

            for t in range(FIRST, STOP):
                if 0 <= t < T - 1:
                    dve.wait_ge(state_ok, t + 1)
                    m, n = divmod(t + 1, STEPS)
                    v.tensor_tensor(gs[:, (t + 1) % 2, :], gate[:, m % 3, n * B:(n + 1) * B],
                                    sT[:, t * B:(t + 1) * B], ALU.mult).then_inc(gs_ok, 1)
                j, k = divmod(t, STEPS)
                if k == 0 and (m := tile(j + 2)) is not None:
                    dve.wait_ge(ln1_t, m + 1)
                    dve.wait_ge(rscan, NG)
                    ge(dve, p_inp, m - 1)
                    v.tensor_tensor(ret[:, m % 2, :].rearrange("p (t b) -> p t b", b=B),
                                    bank[2][:, 0:P].rearrange("p (t b) -> p t b", b=B),
                                    rT[:, :, m * STEPS:(m + 1) * STEPS].rearrange("p b t -> p t b"), ALU.mult).then_inc(retd, 1)
                if k == 0 and (i := tile(j - 2)) is not None:
                    dve.wait_ge(x1_ok, i + 1)
                    chain(v.bn_aggr(mv2[:, i, :], st2[:, i, :]))
                    v.tensor_scalar(ve2[:, i:i + 1], mv2[:, i, 1:2], EPS, None, ALU.add).then_inc(ln2_var, 1)
                if k == 1 and (m := tile(j + 3)) is not None and m > 0:
                    dve.wait_ge(ld_x[m // 4], 16)
                    stats(x[:, m, :], st1, mv1, ve1, m, ln1_var)
                if k == 0 and (i := tile(j - 3)) is not None:
                    dve.wait_ge(p_sc, i + 1)
                    v.tensor_copy(sc[:, i % 2, :], bank[6][:, 0:NE]).then_inc(sc_ok, 1)
                    dve.wait_ge(sc_ok, i + 1)
                    v.max(m8[:, i, :], sc[:, i % 2, :])
                if k == 2 and (i := tile(j - 3)) is not None:
                    chain(v.memset(settled[:], 0.0))
                    chain(v.max_index(i8[:, i, :], m8[:, i, :], sc[:, i % 2, :]))
                    v.tensor_copy(i8f[:, i, :], i8[:, i, 0:2])
                if k == 3 and (i := tile(j - 4)) is not None:
                    dve.wait_ge(p_cnt, i + 1)
                    v.tensor_tensor(rank[:], bank[6][:, P + NE:P + 2 * NE], total[:], ALU.add)
                    chain(v.tensor_tensor(total[:], bank[6][:, P:P + NE], total[:], ALU.add))
                    v.tensor_tensor(rank[:], rank[:], ecap[:], ALU.add).then_inc(rank_ok, 1)
                    if i == TILES - 1:
                        chain(v.tensor_tensor(endrow[:], total[:], ecap[:], ALU.add))
                        v.tensor_copy(endrow_i[:], endrow[0:1, :]).then_inc(endrow_ok, 1)
                if k == 3 and (i := tile(j - 2)) is not None:
                    dve.wait_ge(ln2_rstd, i + 1)
                    v.tensor_scalar(xn[:, i, :], x[:, i, :], mv2[:, i, 0:1], rs2[:, i:i + 1], ALU.subtract,
                                    ALU.mult).then_inc(ln2_x, 1)
                if k == 4 and (m := tile(j + 3)) is not None:
                    dve.wait_ge(ln1_rstd, m + 1)
                    ge(dve, ln1_t, m - 1)
                    v.tensor_scalar(xa[:, m % 2, :], x[:, m, :], mv1[:, m, 0:1], rs1[:, m:m + 1], ALU.subtract,
                                    ALU.mult).then_inc(ln1_x, 1)
                if k == 4 and (i := tile(j - 3)) is not None:
                    dve.wait_ge(k_iota, 4)
                    for q in range(2):
                        ins = v.tensor_scalar(pick[q][:, i, :], iota_e[:], i8f[:, i, q:q + 1], None, ALU.is_equal)
                    picked = mark(ins)
                if k == 5 and (i := tile(j - 3)) is not None:
                    dve.wait_ge(dchain, picked)
                    ge(dve, p_cnt, i - 1)
                    v.tensor_tensor(picks[:, i % 2, :], pick[0][:, i, :], pick[1][:, i, :], ALU.add).then_inc(picks_ok, 1)
                if k == 5 and (m := tile(j + 2)) is not None:
                    dve.wait_ge(s_gate, m + 1)
                    gm, im, om = gate[:, m % 3, :], inp[:, m % 2, :], ginp[:, m % 2, :]
                    chain(v.tensor_scalar(gm, gm, 0.5, 0.5, ALU.mult, ALU.add))
                    ge(dve, p_u, m - 1)
                    gated = mark(v.tensor_tensor(om, gm, im, ALU.mult))
                if k == 6 and (m := tile(j + 2)) is not None:
                    dve.wait_ge(dchain, gated)
                    im, om = inp[:, m % 2, :], ginp[:, m % 2, :]
                    v.tensor_tensor(om, im, om, ALU.subtract).then_inc(s_ginp, 1)
                if k == 6 and (i := tile(j - 4)) is not None:
                    dve.wait_ge(rank_ok, i + 1)
                    for q in range(2):
                        ins = v.tensor_tensor_reduce(out=junkr[:, q, :], in0=pick[q][:, i, :], in1=rank[:], scale=1.0, scalar=0.0,
                                                     op0=ALU.mult, op1=ALU.add, accum_out=slotf[:, q, i:i + 1])
                    chain(ins)
                    v.tensor_copy(sloti[:, :, i:i + 1], slotf[:, :, i:i + 1]).then_inc(slot_ok, 1)
                if k == 6 and (i := tile(j - 1)) is not None:
                    dve.wait_ge(p_o, i + 1)
                    added = mark(v.tensor_tensor(x[:, i, :], bank[4][:, 0:P], x[:, i, :], ALU.add))
                if k == 7 and (i := tile(j - 1)) is not None:
                    dve.wait_ge(dchain, added)
                    v.bn_stats(st2[:, i, :], x[:, i, :]).then_inc(x1_ok, 1)

            chain(v.tensor_scalar(npad[:], total[:], 1.0, float(P - 1), ALU.max, ALU.add))

            chain(v.tensor_copy(npad_i[:], npad[:]))
            chain(v.tensor_scalar(npad_i[:], npad_i[:], 7, 7, ALU.arith_shift_right, ALU.arith_shift_left))
            chain(v.tensor_copy(npad[:], npad_i[:]))
            chain(v.tensor_tensor_scan(end_e[:], ones24[:], npad[:], 0.0, ALU.mult, ALU.add))
            chain(v.tensor_scalar(over[:], end_e[:], iota_p[:], None, ALU.is_le))
            chain(v.tensor_reduce(tabc[:, 0:1], over[:], AX, ALU.add))
            v.tensor_scalar(junkr[:, 0, :], npad[:], -1.0, float(CAP), ALU.mult, ALU.add)
            chain(v.tensor_scalar(tabc[:, 0:1], tabc[:, 0:1], float(NE - 1), None, ALU.min))
            chain(v.tensor_tensor(junkr[:, 0, :], junkr[:, 0, :], over[:], ALU.mult))
            chain(v.tensor_reduce(tabc[:, 1:2], junkr[:, 0, :], AX, ALU.add))
            chain(v.tensor_tensor(tabc[:, 1:2], tabc[:, 1:2], iota_p[:], ALU.add))
            v.tensor_tensor(tabc[:, 1:2], tabc[:, 1:2], endrow[:, NE - 1:NE], ALU.min).then_inc(tabc_ok, 1)
            dve.wait_ge(p_tab, 1)
            v.tensor_copy(tab[:], bank[4][0:2, 0:P]).then_inc(tab_ok, 1)
            v.tensor_tensor(mixs[:], m8[:, :, 1:2].rearrange("p b a -> p (b a)"),
                            m8[:, :, 0:1].rearrange("p b a -> p (b a)"), ALU.subtract).then_inc(mix_d, 1)

            def copy_in(j, u):
                dve.wait_ge(p_in, j + 1)
                if not isinstance(j, int) or j >= 2:
                    dve.wait_ge(p_h, j - 1)
                v.tensor_copy(xsT[:, u, :], bank[0][:, 0:P]).then_inc(s_in, 1)

            def copy_hT(j, u):
                dve.wait_ge(p_hT, j + 1)
                if not isinstance(j, int) or j >= 2:
                    dve.wait_ge(p_y, j - 1)
                v.tensor_copy(hT[:, u, :], bank[3 + u][:]).then_inc(s_hT, 1)

            bsum = bqkv[:, 3 * D:6 * D]
            peeled = 10
            for j in range(peeled):
                copy_in(j, j % 2)
                if j >= 2:
                    copy_hT(j - 2, j % 2)
                if j == 2:
                    dve.wait_ge(ld_d, 64)
                    v.tensor_copy(lens[:], lens_i[:])
                    dve.wait_ge(ld_bqf, 16)
                    v.tensor_copy(bsum[:, 0:D], bqkv[:, 0:D])
                    dve.wait_ge(p_wkv, 2)
                    summed = mark(v.tensor_tensor(bsum[:, D:3 * D], bank[7][0:1, 0:2 * D], bqkv[:, D:3 * D], ALU.add))
                if j == 3:
                    dve.wait_ge(dchain, summed)
                    chain(v.tensor_copy(bqkv3[:, 0, :], bsum))
                    summed = mark(v.tensor_tensor(bsum, bsum, bqkv3[:, 0, :], ALU.subtract))
                if j == 4:
                    dve.wait_ge(dchain, summed)
                    chain(v.tensor_copy(bqkv3[:, 1, :], bsum))
                    chain(v.tensor_tensor(bsum, bsum, bqkv3[:, 1, :], ALU.subtract))
                    v.tensor_copy(bqkv3[:, 2, :], bsum).then_inc(bq3, 1)
                if j == 5:
                    chain(v.tensor_tensor(base_e[:], end_e[:], npad[:], ALU.subtract))
                    v.tensor_tensor(base_e[:], base_e[:], ecap[:], ALU.subtract)
                    dve.wait_ge(mix_e, 1)
                    chain(v.tensor_scalar(mixs[:], mixe[:], 1.0, None, ALU.add))
                    chain(v.reciprocal(route[:, 2, :], mixs[:]))
                    v.tensor_tensor(route[:, 3, :], mixe[:], route[:, 2, :], ALU.mult)
                if j in (6, 7):
                    q = j - 6
                    chain(v.tensor_tensor(tmp_re, pick[q][:], base_e[:].unsqueeze(1).to_broadcast([P, TILES, NE]), ALU.mult))
                    chain(v.tensor_reduce(route[:, q, :], tmp_re, AX, ALU.add))
                    v.tensor_tensor(route[:, q, :], route[:, q, :], slotf[:, q, :], ALU.add).then_inc(route_ok, 1)
            dve.wait_ge(p_route, 1)
            v.tensor_copy(routeT[:], bank[7][0:4 * TILES, 0:P]).then_inc(routeT_ok, 1)
            n = (NT - 4) // 2
            with dve.Fori((peeled - 4) // 2, n) as i:
                for u in range(2):
                    copy_in(i * 2 + (4 + u), u)
                    copy_hT(i * 2 + (2 + u), u)
            for j in range(4 + 2 * n, NT + 2):
                if j < NT:
                    copy_in(j, j % 2)
                copy_hT(j - 2, j % 2)
            pad = padded.rearrange("o (b t) -> o b t", b=B)
            chain(v.tensor_tensor(pad, iota_s[64:65, :].unsqueeze(1).to_broadcast([1, B, T]),
                                  lens[64:65, :].unsqueeze(2).to_broadcast([1, B, T]), ALU.is_ge))
            v.tensor_scalar(padded, padded, -BIG, None, ALU.mult).then_inc(padded_ok, 1)

            def pv(t, part):
                k = slice(part * 8, part * 8 + 8)
                o = prod[:, 1, t % 2, :].rearrange("p (g h d) -> p g h d", g=H, h=H)[:, k, :, :]
                w = hd(pn[:, t % 2, :], H, H).rearrange("p h g -> p g h")[:, k, :].unsqueeze(3).to_broadcast([P, 8, H, HD])
                vv = hd(qkv[:, t % 4, 2 * D:3 * D], H, HD)[:, k, :].unsqueeze(2).to_broadcast([P, 8, H, HD])
                return v.tensor_tensor(o, w, vv, ALU.mult)

            def qk(t, part):
                k = slice(part * 4, part * 4 + 4)
                o = prod[:, 0, t % 2, :].rearrange("p (d h g) -> p d h g", d=HD, h=H)[:, k, :, :]
                q = hd(qkv[:, t % 4, 0:D], HD, H)[:, k, :].unsqueeze(3).to_broadcast([P, 4, H, H])
                kk = hd(qkv[:, t % 4, D:2 * D], HD, H)[:, k, :].unsqueeze(2).to_broadcast([P, 4, H, H])
                return v.tensor_tensor(o, q, kk, ALU.mult)

            dve.wait_ge(ld_route, 16)
            dve.wait_ge(ld_res, 16)
            own = Own(dve, l_dve)
            for i in range(0, B + LAST):
                if (t := seq(i - 8)) is not None:
                    p = t % 2
                    own.need(mx16_ok)
                    ge(dve, d_exp2, t - 1)
                    v.tensor_tensor(hd(ST2[:, p, :], H, H), hd(bank[5][:, 0:256], H, H),
                                    mx16[:, p, :].unsqueeze(2).to_broadcast([P, H, H]), ALU.subtract).then_inc(d_sub, 1)
                if (t := seq(i - 4)) is not None:
                    p = t % 2
                    dve.wait_ge(d_score, t + 1)
                    ge(dve, d_exp, t - 1)
                    v.tensor_reduce(mx1[:, p, :], bank[1][:, 0:P], AX, ALU.min).then_inc(d_min, 1)
                if (t := seq(i - 5)) is not None:
                    p = t % 2
                    own.need(st4_ok)
                    mv4_ok = own(v.bn_aggr(mv4[:, p, :], st4[:, p, :]))
                if (t := seq(i - 3)) is not None:
                    p = t % 2
                    dve.wait_ge(d_x2, t + 1)
                    st3_ok = own(v.bn_stats(st3[:, p, :], x[:, t, :]))
                if (t := seq(i - 5)) is not None:
                    p = t % 2
                    own.need(mv4_ok)
                    ge(dve, d_r45, t - 1)
                    v.tensor_scalar(ve4[:, p, 0:1], mv4[:, p, 1:2], EPS, None, ALU.add)
                    v.tensor_scalar(ve4[:, p, 1:2], mv4[:, p, 1:2], 1.0 + RMS_EPS, RMS_EPS * EPS, ALU.mult, ALU.add).then_inc(d_var4, 1)
                if (t := seq(i - 3)) is not None:
                    p = t % 2
                    own.need(st3_ok)
                    mv3_ok = own(v.bn_aggr(mv3[:, p, :], st3[:, p, :]))
                if (t := seq(i - 9)) is not None:
                    dve.wait_ge(d_pn, t + 1)
                    ge(dve, d_O, t - 1)
                    pv(t, 0).then_inc(d_pv, 1)
                if (t := seq(i - 4)) is not None:
                    p = t % 2
                    dve.wait_ge(d_exp, t + 1)
                    ge(dve, d_p, t - 1)
                    v.reciprocal(rc1[:, p, :], sm1[:, p, :]).then_inc(d_rc, 1)
                if (t := seq(i - 3)) is not None:
                    p = t % 2
                    own.need(mv3_ok)
                    ge(dve, d_r3, t - 1)
                    v.tensor_scalar(ve3[:, p, :], mv3[:, p, 1:2], EPS, None, ALU.add).then_inc(d_var3, 1)
                if (t := seq(i - 9)) is not None:
                    pv(t, 1).then_inc(d_pv, 1)
                if (t := seq(i - 11)) is not None:
                    p = t % 2
                    dve.wait_ge(d_lg, t + 1)
                    ge(dve, d_gexp, t - 1)
                    v.tensor_reduce(gmx[:, p, :], bank[0][:, 384:384 + NX], AX, ALU.min).then_inc(d_gmax, 1)
                if (t := seq(i - 10)) is not None:
                    dve.wait_ge(d_w, t + 1)
                    v.tensor_tensor(xn[:, t, :], bank[5][:, 256:384], xn[:, t, :], ALU.add).then_inc(d_xf2, 1)
                if (t := seq(i - 5)) is not None:
                    p = t % 2
                    dve.wait_ge(d_r45, t + 1)
                    ge(dve, d_h, t - 1)
                    v.tensor_scalar(nm4[:, p, :], r45[:, p, :], mv4[:, p, 0:1], -1.0, ALU.mult, ALU.mult).then_inc(d_nm4, 1)
                if (t := seq(i - 8)) is not None:
                    p = t % 2
                    dve.wait_ge(d_exp2, t + 1)
                    sum16_ok = own(v.tensor_reduce(sum16[:, p, :], hd(pe_[:, p, :], H, H), AX, ALU.add))
                if (t := seq(i - 3)) is not None:
                    p = t % 2
                    dve.wait_ge(d_r3, t + 1)
                    ge(dve, d_xn3, t - 1)
                    v.tensor_scalar(nm3[:, p, :], r3[:, p, :], mv3[:, p, 0:1], -1.0, ALU.mult, ALU.mult).then_inc(d_nm3, 1)
                if (t := seq(i - 6)) is not None:
                    dve.wait_ge(d_cqkv, t + 1)
                    ge(dve, d_S, t - 1)
                    qk(t, 0)
                if (t := seq(i - 8)) is not None:
                    p = t % 2
                    own.need(sum16_ok)
                    ge(dve, d_pn, t - 1)
                    v.reciprocal(rec16[:, p, :], sum16[:, p, :]).then_inc(d_rec16, 1)
                if (t := seq(i - 13)) is not None:
                    dve.wait_ge(d_moe, t + 1)
                    dve.wait_ge(d_acc, t + 1)
                    v.tensor_tensor(x[:, t, :], bank[3][:, 384:512], x[:, t, :], ALU.add).then_inc(d_out, 1)
                if (t := seq(i - 6)) is not None:
                    qk(t, 1).then_inc(d_qk, 1)
                if (t := seq(i - 7)) is not None:
                    p = t % 2
                    dve.wait_ge(d_S2, t + 1)
                    mx16_ok = own(v.tensor_reduce(mx16[:, p, :], hd(bank[5][:, 0:256], H, H), AX, ALU.max))
                if (t := seq(i - 11)) is not None:
                    p = t % 2
                    dve.wait_ge(d_gexp, t + 1)
                    ge(dve, d_wg, 2 * (t - 1))
                    own.need(own(v.reciprocal(grc[:, p, :], gsm[:, p, :])))
                    v.tensor_scalar(gn8[:, p, :], ge8[:, p, :], grc[:, p, :], None, ALU.mult).then_inc(d_gn, 1)
                if (t := seq(i - 4)) is not None:
                    p = t % 2
                    dve.wait_ge(d_x3, t + 1)
                    st4_ok = own(v.bn_stats(st4[:, p, :], x[:, t, :]))


def kernel(**inputs):
    import numpy as np
    import concourse.bacc as bacc
    from concourse.bass_utils import run_bass_kernel_spmd as run

    i = {k: np.asarray(v) for k, v in inputs.items()}
    c = np.ascontiguousarray
    Wout = i["L1_xattn_W_out"]
    dh = lambda w: c(w.reshape(w.shape[:-1] + (H, HD)).swapaxes(-1, -2)).reshape(w.shape)

    def kv(w):
        w = w.reshape(w.shape[:-1] + (H, 2, HD))
        k, v_ = w[..., 0, :], w[..., 1, :]
        flat = w.shape[:-3] + (D,)
        return np.concatenate([c(k.swapaxes(-1, -2)).reshape(flat), c(v_).reshape(flat)], axis=-1)

    wp = {
        "WiT": i["L0_xattn_Wi"].T, "WgT": i["L0_xattn_Wg"].T, "AT": i["L0_xattn_A"].T, "BmT": i["L0_xattn_Bm"].T,
        "Wo0T": i["L0_xattn_Wo"].T, "Win": i["L1_xattn_W_in"], "Wo1T": Wout[:, :D].T, "Wo2T": Wout[:, D:].T,
        "Wq": dh(i["L1_ffn_Wq"]), "Wo": i["L1_ffn_Wo"],
    }
    arrays = {
        "x": c(i["x"].transpose(1, 0, 2)).reshape(TOK, D),
        "ctxT": c(i["ctx_1024"].transpose(2, 0, 1)).reshape(D, TOK),
        "wpk": c(np.concatenate([wp[n] for n in W_NAMES], axis=1)),
        "cols": c(np.stack([np.repeat(i["L0_xattn_decay"].reshape(H), HD), i["L0_xattn_bi"], i["L0_xattn_bg"],
                            i["L1_ffn_gamma1"], i["L1_ffn_gamma2"]], axis=1)),
        "gate_w": c(i["L0_ffn_gate_w"]),
        "rowb": c(np.concatenate([i["L0_ffn_b1"].reshape(-1), i["L0_ffn_b2"].reshape(-1), i["L1_xattn_b_out"],
                                  i["L1_ffn_bo"], i["L0_xattn_bo"], i["L0_ffn_gate_b"], i["L1_ffn_bg"]])).reshape(RP, RC),
        "wkv": c(np.concatenate([i["L1_ffn_Wdown"].T, kv(i["L1_ffn_Wup"])], axis=1)),
        "bd": c(i["L1_ffn_bdown"]).reshape(-1, 1),
        "bqkv": c(np.concatenate([dh(i["L1_ffn_bq"]), kv(i["L1_ffn_bup"])])).reshape(1, 3 * D),
        "we": c(np.concatenate([i["L1_ffn_We"].transpose(1, 0, 2).reshape(D, NX * D), i["L1_ffn_Wg"]], axis=1)),
        "lens": c(i["_lenS2"]).reshape(1, B),
        "w1": c(i["L0_ffn_w1"]), "w2": c(i["L0_ffn_w2"]),
    }
    nc = bacc.Bacc("TRN2", target_bir_lowering=False, num_devices=1)
    a = {n: nc.dram_tensor(f"in_{n}", v.shape, mybir.dt.from_np(v.dtype), kind="ExternalInput").ap() for n, v in arrays.items()}
    out = nc.dram_tensor("out_0", (B, T, D), F32, kind="ExternalOutput").ap()
    build(nc, a, out)
    r = run(nc, [{f"in_{n}": v for n, v in arrays.items()}], core_ids=[0])
    return r.results[0]["out_0"]
```
